# Optimizing a Trainium2 kernel written in Bass

```python
import numpy as np
import jax
import jax.numpy as jnp

def _softmax(x, axis=-1):
    return jax.nn.softmax(x, axis=axis)

def _gelu(x):
    return jax.nn.gelu(x, approximate=True)

def _silu(x):
    return jax.nn.silu(x)

def _sigmoid(x):
    return jax.nn.sigmoid(x)

def _layernorm(x, axis=-1, eps=1e-05):
    m = jnp.mean(x, axis=axis, keepdims=True)
    v = jnp.var(x, axis=axis, keepdims=True)
    return (x - m) / jnp.sqrt(v + eps)

def _scatter_add(tgt, idx, src, axis=0):
    return tgt.at[idx].add(src)

def _segment_sum(src, seg, n):
    return jax.ops.segment_sum(src, seg, n)
kernel_name = 'mk_gnn_preln_d2_gnn_r64_707eb5'

def setup_inputs(seed: int=0):
    np.random.seed(seed)
    _w = jnp.asarray

    def _rec_inputs():
        import jax
        import jax.numpy as jnp
        _gk = jax.random.key(seed)
        x = -0.0005121 + 1.001 * jax.random.normal(jax.random.fold_in(_gk, 1), (100000, 32), jnp.float32)
        src = jax.random.randint(jax.random.fold_in(_gk, 2), (50000,), 0, 100000, jnp.int32)
        dst = jnp.minimum((100000 * jax.random.uniform(jax.random.fold_in(_gk, 3), (50000,)) ** 2.0).astype(jnp.int32), 99999)
        _o = jnp.argsort(dst, stable=True)
        src = src[_o]
        dst = dst[_o]
        edge_attr_2 = jax.random.uniform(jax.random.fold_in(_gk, 11), (50000, 2), jnp.float32, 0.0, 1)
        return (x, src, dst, edge_attr_2)
    x, src, dst, edge_attr_2 = _rec_inputs()

    def _L0_gnn_setup():
        import jax, jax.numpy as jnp
        import numpy as np
        N_NODES = 100000
        N_EDGES = 50000
        IN_CH = 32
        OUT_CH = 32
        DIM = 2
        KSIZE = 3

        def _basis(pseudo):
            p = jnp.clip(pseudo, 0.0, 1.0)
            grid = jnp.linspace(0.0, 1.0, KSIZE, dtype=p.dtype)
            dist = jnp.abs(p[:, :, None] - grid[None, None, :])
            b = jnp.maximum(1.0 - dist * (KSIZE - 1), 0.0)
            basis = jnp.einsum('ea,eb->eab', b[:, 0], b[:, 1])
            return basis.reshape(p.shape[0], -1)
        key = jax.random.key(seed)
        k1, k2, k3, k4, k5, k6 = jax.random.split(key, 6)
        x = jax.random.normal(k1, (N_NODES, IN_CH), dtype=jnp.float32)
        pseudo = jax.random.uniform(k2, (N_EDGES, DIM), dtype=jnp.float32)
        weight = jax.random.normal(k3, (KSIZE * KSIZE, IN_CH, OUT_CH), dtype=jnp.float32) / np.sqrt(IN_CH)
        root_w = jax.random.normal(k4, (OUT_CH, IN_CH), dtype=jnp.float32) / np.sqrt(IN_CH)
        root_b = jax.random.normal(k5, (OUT_CH,), dtype=jnp.float32) * 0.01
        edge_index = jax.random.randint(k6, (2, N_EDGES), 0, N_NODES, dtype=jnp.int64)
        return {'x': x, 'pseudo': pseudo, 'weight': weight, 'root_w': root_w, 'root_b': root_b, 'edge_index': edge_index}
    _L0_gnn_all = _L0_gnn_setup()
    _L0_gnn_in = {k: v for k, v in _L0_gnn_all.items() if k in ('weight', 'root_w', 'root_b')}
    del _L0_gnn_all

    def _L1_gnn_setup():
        import jax, jax.numpy as jnp
        import numpy as np
        H, C = (8, 32)
        N, E = (100000, 25000)
        NEG_SLOPE = 0.2
        LN_EPS = 1e-05

        def layer_norm(x, g, b):
            mu = jnp.mean(x, axis=-1, keepdims=True)
            var = jnp.mean((x - mu) ** 2, axis=-1, keepdims=True)
            return (x - mu) * jax.lax.rsqrt(var + LN_EPS) * g + b

        def gat_conv(x, edge_index, W_gat, att_src, att_dst, bias_gat):
            n = x.shape[0]
            loops = jnp.arange(n, dtype=edge_index.dtype)
            ei = jnp.concatenate([edge_index, jnp.stack([loops, loops])], axis=1)
            src, dst = (ei[0], ei[1])
            xp = (x @ W_gat).reshape(n, H, C)
            a_src = jnp.einsum('nhc,hc->nh', xp, att_src)
            a_dst = jnp.einsum('nhc,hc->nh', xp, att_dst)
            alpha = jax.nn.leaky_relu(a_src[src] + a_dst[dst], NEG_SLOPE)
            m = jax.ops.segment_max(alpha, dst, num_segments=n)
            ea = jnp.exp(alpha - m[dst])
            denom = jax.ops.segment_sum(ea, dst, num_segments=n)
            attn = ea / (denom[dst] + 1e-16)
            msg = xp[src] * attn[..., None]
            out = jax.ops.segment_sum(msg, dst, num_segments=n)
            return out.mean(axis=1) + bias_gat
        key = jax.random.key(seed)
        ks = jax.random.split(key, 8)
        x = jax.random.normal(ks[0], (N, C), dtype=jnp.float32)
        edge_index = jax.random.randint(ks[1], (2, E), 0, N, dtype=jnp.int64)
        s = 1.0 / np.sqrt(C)
        W_gat = jax.random.normal(ks[2], (C, H * C), dtype=jnp.float32) * s
        att_src = jax.random.normal(ks[3], (H, C), dtype=jnp.float32) * s
        att_dst = jax.random.normal(ks[4], (H, C), dtype=jnp.float32) * s
        bias_gat = jnp.zeros((C,), jnp.float32)
        w1 = jax.random.normal(ks[5], (C, 128), dtype=jnp.float32) * s
        b1 = jnp.zeros((128,), jnp.float32)
        w2 = jax.random.normal(ks[6], (128, C), dtype=jnp.float32) / np.sqrt(128)
        b2 = jnp.zeros((C,), jnp.float32)
        g1 = jnp.ones((C,), jnp.float32)
        be1 = jnp.zeros((C,), jnp.float32)
        g2 = jnp.ones((C,), jnp.float32)
        be2 = jnp.zeros((C,), jnp.float32)
        return dict(x=x, edge_index=edge_index, W_gat=W_gat, att_src=att_src, att_dst=att_dst, bias_gat=bias_gat, w1=w1, b1=b1, w2=w2, b2=b2, g1=g1, be1=be1, g2=g2, be2=be2)
    _L1_gnn_all = _L1_gnn_setup()
    _L1_gnn_in = {k: v for k, v in _L1_gnn_all.items() if k in ('W_gat', 'att_src', 'att_dst', 'bias_gat', 'w1', 'b1', 'w2', 'b2', 'g1', 'be1', 'g2', 'be2')}
    del _L1_gnn_all
    return {'x': x, 'src': src, 'dst': dst, 'edge_attr_2': edge_attr_2, 'L0_gnn_weight': _L0_gnn_in['weight'], 'L0_gnn_root_w': _L0_gnn_in['root_w'], 'L0_gnn_root_b': _L0_gnn_in['root_b'], 'L1_gnn_W_gat': _L1_gnn_in['W_gat'], 'L1_gnn_att_src': _L1_gnn_in['att_src'], 'L1_gnn_att_dst': _L1_gnn_in['att_dst'], 'L1_gnn_bias_gat': _L1_gnn_in['bias_gat'], 'L1_gnn_w1': _L1_gnn_in['w1'], 'L1_gnn_b1': _L1_gnn_in['b1'], 'L1_gnn_w2': _L1_gnn_in['w2'], 'L1_gnn_b2': _L1_gnn_in['b2'], 'L1_gnn_g1': _L1_gnn_in['g1'], 'L1_gnn_be1': _L1_gnn_in['be1'], 'L1_gnn_g2': _L1_gnn_in['g2'], 'L1_gnn_be2': _L1_gnn_in['be2']}

def reference(x, src, dst, edge_attr_2, L0_gnn_weight, L0_gnn_root_w, L0_gnn_root_b, L1_gnn_W_gat, L1_gnn_att_src, L1_gnn_att_dst, L1_gnn_bias_gat, L1_gnn_w1, L1_gnn_b1, L1_gnn_w2, L1_gnn_b2, L1_gnn_g1, L1_gnn_be1, L1_gnn_g2, L1_gnn_be2):
    import jax
    import jax.numpy as jnp

    def _L0_gnn_ref(x, pseudo, weight, root_w, root_b, edge_index):
        import jax, jax.numpy as jnp
        import numpy as np
        N_NODES = 100000
        N_EDGES = 50000
        IN_CH = 32
        OUT_CH = 32
        DIM = 2
        KSIZE = 3

        def _basis(pseudo):
            p = jnp.clip(pseudo, 0.0, 1.0)
            grid = jnp.linspace(0.0, 1.0, KSIZE, dtype=p.dtype)
            dist = jnp.abs(p[:, :, None] - grid[None, None, :])
            b = jnp.maximum(1.0 - dist * (KSIZE - 1), 0.0)
            basis = jnp.einsum('ea,eb->eab', b[:, 0], b[:, 1])
            return basis.reshape(p.shape[0], -1)
        row, col = (edge_index[0], edge_index[1])
        basis = _basis(pseudo)
        messages = jnp.einsum('ek,ei,kio->eo', basis, x[row], weight)
        out = jnp.zeros((x.shape[0], weight.shape[2]), dtype=x.dtype).at[col].add(messages)
        degree = jnp.zeros((x.shape[0],), dtype=x.dtype).at[col].add(jnp.ones_like(col, dtype=x.dtype))
        out = out / jnp.maximum(degree, 1.0)[:, None]
        out = out + x @ root_w.T + root_b
        return out

    def _L1_gnn_ref(x, edge_index, W_gat, att_src, att_dst, bias_gat, w1, b1, w2, b2, g1, be1, g2, be2):
        import jax, jax.numpy as jnp
        import numpy as np
        H, C = (8, 32)
        N, E = (100000, 25000)
        NEG_SLOPE = 0.2
        LN_EPS = 1e-05

        def layer_norm(x, g, b):
            mu = jnp.mean(x, axis=-1, keepdims=True)
            var = jnp.mean((x - mu) ** 2, axis=-1, keepdims=True)
            return (x - mu) * jax.lax.rsqrt(var + LN_EPS) * g + b

        def gat_conv(x, edge_index, W_gat, att_src, att_dst, bias_gat):
            n = x.shape[0]
            loops = jnp.arange(n, dtype=edge_index.dtype)
            ei = jnp.concatenate([edge_index, jnp.stack([loops, loops])], axis=1)
            src, dst = (ei[0], ei[1])
            xp = (x @ W_gat).reshape(n, H, C)
            a_src = jnp.einsum('nhc,hc->nh', xp, att_src)
            a_dst = jnp.einsum('nhc,hc->nh', xp, att_dst)
            alpha = jax.nn.leaky_relu(a_src[src] + a_dst[dst], NEG_SLOPE)
            m = jax.ops.segment_max(alpha, dst, num_segments=n)
            ea = jnp.exp(alpha - m[dst])
            denom = jax.ops.segment_sum(ea, dst, num_segments=n)
            attn = ea / (denom[dst] + 1e-16)
            msg = xp[src] * attn[..., None]
            out = jax.ops.segment_sum(msg, dst, num_segments=n)
            return out.mean(axis=1) + bias_gat
        h = gat_conv(x, edge_index, W_gat, att_src, att_dst, bias_gat)
        h = layer_norm(h + x, g1, be1)
        ff = jax.nn.relu(h @ w1 + b1) @ w2 + b2
        return layer_norm(ff + h, g2, be2)
    edge_index = jnp.stack([src, dst])
    h = jnp.maximum(_layernorm(x, axis=-1), 0.0)
    x = x + _L0_gnn_ref(h, edge_attr_2, L0_gnn_weight, L0_gnn_root_w, L0_gnn_root_b, edge_index)
    h = jnp.maximum(_layernorm(x, axis=-1), 0.0)
    x = x + _L1_gnn_ref(h, edge_index, L1_gnn_W_gat, L1_gnn_att_src, L1_gnn_att_dst, L1_gnn_bias_gat, L1_gnn_w1, L1_gnn_b1, L1_gnn_w2, L1_gnn_b2, L1_gnn_g1, L1_gnn_be1, L1_gnn_g2, L1_gnn_be2)
    return x

_drawn_inputs = setup_inputs


def setup_inputs(seed=0):
    import zlib

    import numpy as np

    out = dict(_drawn_inputs(seed))
    spreads = {'L1_gnn_bias_gat': (0.0, 0.1),
     'L1_gnn_b1': (0.0, 0.375),
     'L1_gnn_b2': (0.0, 0.1),
     'L1_gnn_g1': (1.0, 0.2),
     'L1_gnn_be1': (0.0, 0.1),
     'L1_gnn_g2': (1.0, 0.2),
     'L1_gnn_be2': (0.0, 0.1)}
    factors = {'L0_gnn_root_b': 6.909, 'L1_gnn_att_src': 3.348, 'L1_gnn_att_dst': 8.0}
    for name, (base, spread) in spreads.items():
        noise = np.random.default_rng([zlib.crc32(name.encode()), seed]).standard_normal(out[name].shape)
        drawn = base * np.exp(spread * noise) if base else spread * noise
        out[name] = jnp.asarray(drawn.astype(out[name].dtype))
    for name, factor in factors.items():
        out[name] = (out[name] * factor).astype(out[name].dtype)
    return out
```

```python
import concourse.bass as bass
from concourse import mybir
from concourse.alu_op_type import AluOpType as ALU
from contextlib import ExitStack

F32 = mybir.dt.float32
I32 = mybir.dt.int32
ACT = mybir.ActivationFunctionType
AX = mybir.AxisListType

N, E, F, H, HID, KS = 100000, 50000, 32, 8, 128, 9
P = 125
TN = N // P
NB, NJ, CE = 5, 5, 16
SE = NJ * CE
TE = NB * SE
NC = NB * NJ
CN = TN // NC
W = CE * F
G = CE // 4
GF = 4 * F
WT = G * P
EPS = 1e-5
SLOPE = 0.2
DMAS = 16 * CE
N_BOOT = 2 + 6 * 4 + 2 + 2 + 2 + 3 + 2 + 2
BASE_DONE = 5 * NC + 3 * NC + 2 + 4
CREDIT = 4


class Uses:

    def __init__(self, depth=1):
        self.depth, self.base, self.n = depth, 0, 0

    def next(self):
        self.at = self.base + self.n
        self.room = self.at + CREDIT - min(self.n, self.depth - 1)
        bank = self.n % self.depth
        self.n += 1
        return self.at, bank

    def loop(self, b, per):
        self.first = self.base + self.n
        self.base, self.n = self.first + b * per, 0

    def end(self, times, per):
        assert self.n == per, (self.n, per)
        self.base, self.n = self.first + times * per, 0

    def restart(self):
        self.base, self.n = self.base + self.n, 0


def gnn_program(nc, x, src, dst, edge_attr, w0, root_w, root_b, w_gat, att_src, att_dst, bias_gat,
                w1, b1, w2, b2, g1, be1, g2, be2, out):
    x1_table = nc.dram_tensor("x1_table", [N + E, F], F32, kind="Internal").ap()
    x1_plain = nc.dram_tensor("x1_plain", [P, TN * F], F32, kind="Internal").ap()
    x1_dst = nc.dram_tensor("x1_dst", [NC, P, W], F32, kind="Internal").ap()
    base_dst = nc.dram_tensor("base_dst", [NC, P, W], F32, kind="Internal").ap()
    x_rows = x.rearrange("(p t) f -> p (t f)", p=P)
    x1_rows = x1_table[0:N, :].rearrange("(p t) f -> p (t f)", p=P)
    spare_rows = x1_table[N:N + E, :].rearrange("(c p s) f -> c p (s f)", c=NC, p=P)
    out_rows = out.rearrange("(p t) f -> p (t f)", p=P)
    edge_slots = lambda a: a.rearrange("(b p s) -> p b s", b=NB, p=P)

    with ExitStack() as ctx:
        sb = lambda name, shape, dt=F32: ctx.enter_context(nc.sbuf_tensor(name, shape, dt))
        ps = lambda name: ctx.enter_context(nc.psum_tensor(name, [128, 512], F32))
        sem = lambda name: ctx.enter_context(nc.semaphore(name))

        region1 = sb("region1", [128, TE * F])
        region2 = sb("region2", [128, TE * F])
        msgs = region1
        beta = region1[:, 0:H * TE]
        self_logit = region1[:, H * TE:2 * H * TE]
        denom = region1[:, 2 * H * TE:3 * H * TE]
        masked = region1[:, 3 * H * TE:4 * H * TE]
        weighted = region1[:, 3 * H * TE:3 * H * TE + 2048]
        basis = region2[:, 0:TE * KS]
        products = region2[:, TE * KS:TE * KS + 2 * KS * GF]
        w0_bd = region2[:, 5904:5904 + KS * GF]
        attr = region1[:, 0:800]
        hats = region1[:, 800:3200]
        row_f = region1[0:33, 3200:3200 + 2 * NB * P]
        row_s = region1[0:1, 4500:4500 + 2 * NB * P]
        whole = region1[0:33, 5800:5800 + NB * P]
        row_i = region1[0:1, 6500:6500 + 2 * NB * P].bitcast(I32)
        dst_i = region1[:, 7800:7800 + TE].bitcast(I32)
        dst_f = region1[:, 8200:8200 + TE]
        att = region1[:, 8600:8600 + 2 * H * F].rearrange("p (k c) -> p k c", k=2)
        gat = region1[:, 9200:9200 + H * F]
        diff = region2

        ring = sb("ring", [128, NJ, W])
        index = sb("index", [128, NJ, CE], I32)
        nodes = sb("nodes", [128, NJ, 2 * W])
        xT = sb("xT", [128, 3, WT]); hT = sb("hT", [128, 3, WT])
        sq = sb("sq", [128, 3, W]); hrow = sb("hrow", [128, 3, W])
        var = sb("var", [128, 3, CE]); std = sb("std", [128, 3, CE]); rstd = sb("rstd", [128, 3, CE])
        hid = sb("hid", [128, 4, WT])
        stage = sb("stage", [128, W])

        ident = sb("ident", [128, 128]); center = sb("center", [128, GF])
        root_bd = sb("root_bd", [128, GF])
        gat_bd = sb("gat_bd", [128, H * GF])
        base_bd = sb("base_bd", [128, GF])
        att_vec = sb("att_vec", [128, 2 * H])
        att_bd = sb("att_bd", [128, 4, 2 * H]); src_bd = sb("src_bd", [128, 4, H])
        w1_q = sb("w1_q", [128, 4, HID]); w2_c = sb("w2_c", [128, F])
        cols = sb("cols", [128, 8])
        ones = sb("ones", [128, 128])
        bias_row = sb("bias_row", [128, 3, W])
        g2_b = sb("g2_b", [128, F]); be2_b = sb("be2_b", [128, F])
        cont = sb("cont", [128, TE]); cont_next = sb("cont_next", [128, TE])
        head = sb("head", [128, TE]); tail = sb("tail", [128, TE])
        degree = sb("degree", [128, TE])
        scatter_to = sb("scatter_to", [128, TE], I32)
        row_cont = sb("row_cont", [33, NB * P]); row_pass = sb("row_pass", [33, NB * P])
        row_pass_back = sb("row_pass_back", [33, NB * P])
        tails = sb("tails", [128, 128]); tails_row = sb("tails_row", [33, 1 + P])
        carry_in = sb("carry_in", [33, P]); carry_row = sb("carry_row", [128, P]); carry_last = sb("carry_last", [33, 1])
        carry = sb("carry", [128, 40])
        next_i = sb("next_i", [128, NB], I32)
        flat = nodes[:, :, :].rearrange("p j w -> p (j w)")
        s_tails, s_in, s_carry = flat[0:H, 0:1 + NB * P], flat[0:H, 640:640 + NB * P], flat[0:H, 1280:1280 + NB * P]

        T = [ps(f"T{i}") for i in range(2)]
        C = [ps(f"C{i}") for i in range(2)]
        V = [ps(f"V{i}") for i in range(4)]

        boot_dma = sem("boot_dma"); boot_pool = sem("boot_pool"); boot_dve = sem("boot_dve")
        boot_pe = sem("boot_pe"); boot_act = sem("boot_act")
        ring_dma = [sem(f"ring_dma{j}") for j in range(NJ)]
        index_in = [sem(f"index_in{j}") for j in range(NJ)]
        ring_used = sem("ring_used")
        ring_saved = [sem(f"ring_saved{j}") for j in range(NJ)]
        ring_filled = sem("ring_filled")
        nodes_in = [sem(f"nodes_in{j}") for j in range(NJ)]
        nodes_ready = sem("nodes_ready")
        nodes_out = [sem(f"nodes_out{j}") for j in range(NJ)]
        spare_zero = sem("spare_zero")
        t_ready = sem("t_ready"); t_done = sem("t_done")
        c_ready = sem("c_ready"); c_done = sem("c_done")
        v_ready = sem("v_ready"); v_done = sem("v_done")
        f_ready = sem("f_ready"); f_done = sem("f_done")
        sq_ready = sem("sq_ready"); var_ready = sem("var_ready"); std_ready = sem("std_ready")
        dve_step = sem("dve_step")
        tails_ready = sem("tails_ready"); carry_ready = sem("carry_ready")
        exp_ready = sem("exp_ready")
        cleared = sem("cleared")
        exp_in = sem("exp_in")
        softmax_done = sem("softmax_done")
        sum_ready = sem("sum_ready")
        row_ready = sem("row_ready")
        stage_ready = sem("stage_ready"); msgs_done = sem("msgs_done")

        block = ctx.enter_context(nc.Block())
        unit = lambda t, k: t[0:P, k, :]

        BOOT = 0
        @block.sync
        def _(sp):
            n = [0]
            def load(to, frm, **kw):
                sp.dma_start(to, frm, **kw).then_inc(boot_dma, 16)
                n[0] += 1
            def index_load(of, c, b, j, done):
                if done is not None:
                    sp.wait_ge(ring_dma[j], done)
                sp.dma_start(index[0:P, j, :], of[0:E].rearrange("(b p j s) -> b p j s", b=NB, p=P, j=NJ)[bass.ds(b, 1), :, j, :] if not isinstance(b, int)
                             else of.rearrange("(b p j s) -> b p j s", b=NB, p=P, j=NJ)[b, :, j, :]).then_inc(index_in[j], 16)
            for j in range(NJ):
                index_load(src, j, 0, j, None)
            load(dst_i[0:P, :].rearrange("p (b s) -> p b s", b=NB), edge_slots(dst))
            load(attr[0:P, :].rearrange("p (b s) -> p b s", b=NB), edge_attr.rearrange("(b p s) a -> p b (s a)", b=NB, p=P))
            for j in range(NJ):
                sp.dma_start(nodes[0:P, j, :], x_rows[:, j * 2 * W:(j + 1) * 2 * W]).then_inc(nodes_in[j], 16)
            sp.wait_ge(boot_pool, 3)
            sp.wait_ge(boot_dve, 1)
            for t in range(4):
                q = slice(t * F, (t + 1) * F)
                load(w0_bd[q, :].rearrange("f (k t o) -> f k t o", k=KS, t=4)[:, :, t, :], w0.rearrange("k f o -> f k o"))
                load(root_bd[q, q], root_w)
                load(gat[q, :], w_gat)
                load(w1_q[q, t, :], w1)
                load(cols[q, 1:2], g1.rearrange("(f a) -> f a", a=1))
                load(cols[q, 2:3], be1.rearrange("(f a) -> f a", a=1))
            load(cols[:, 0:1], b1.rearrange("(f a) -> f a", a=1))
            load(w2_c[:, :], w2)
            for k, v in enumerate((att_src, att_dst)):
                load(att[:, k, :], v.rearrange("(a h) f -> a (h f)", a=1).to_broadcast([128, H * F]))
            for k, v in enumerate((g2, be2)):
                load((g2_b, be2_b)[k][0:P, :], v.rearrange("(a f) -> a f", a=1).to_broadcast([P, F]))
            for k, v in enumerate((root_b, bias_gat, b2)):
                load(bias_row[0:1, k, 0:F], v.rearrange("(a f) -> a f", a=1))
            ends = dst.rearrange("(c s) -> s c", s=SE)
            load(row_i[0:1, 0:NB * P], ends[0:1, :], allow_slow_non_contiguous=True)
            load(row_i[0:1, NB * P:2 * NB * P], ends[SE - 1:SE, :], allow_slow_non_contiguous=True)
            first = ends[0, :].rearrange("(b p) -> p b", b=NB)
            load(next_i[0:P - 1, :], first[1:P, :], allow_slow_non_contiguous=True)
            load(next_i[P - 1:P, 0:NB - 1], first[0:1, 1:NB], allow_slow_non_contiguous=True)
            assert n[0] == N_BOOT, n[0]

            def a_chunk(b, j, more):
                c = b * NJ + j
                if more:
                    index_load(src, c, b + 1, j, (b + 1) * DMAS)
                sp.dma_start(spare_rows[bass.ds(c, 1), :, :].rearrange("a p w -> (a p) w"), stage[0:P, :]).then_inc(spare_zero, 16)
                sp.wait_ge(nodes_ready, c + 1)
                for to in (x1_rows, x1_plain):
                    sp.dma_start(to[:, bass.ds(c * 2 * W, 2 * W)], nodes[0:P, j, :]).then_inc(nodes_out[j], 16)
                if more:
                    sp.wait_ge(nodes_out[j], (b + 1) * 32)
                    sp.dma_start(nodes[0:P, j, :], x_rows[:, bass.ds((c + NJ) * 2 * W, 2 * W)]).then_inc(nodes_in[j], 16)
            with sp.Fori(0, NB - 1) as b:
                for j in range(NJ):
                    a_chunk(b, j, True)
            for j in range(NJ):
                a_chunk(NB - 1, j, False)
            for j in range(NJ):
                sp.wait_ge(nodes_out[j], NB * 32)

            def node_load(u, j):
                sp.dma_start(nodes[0:P, j, 0:W], x1_plain[:, bass.ds(u * W, W)]).then_inc(nodes_in[j], 16)
            def node_store(u, j):
                sp.dma_start(out_rows[:, bass.ds(u * W, W)], nodes[0:P, j, 0:W]).then_inc(nodes_out[j], 16)
            for j in range(NJ):
                node_load(j, j)
            with sp.Fori(0, NB) as b:
                for j in range(NJ):
                    c = b * NJ + j
                    sp.wait_ge(nodes_ready, NC + c + 1)
                    node_store(c, j)
                    sp.wait_ge(nodes_out[j], NB * 32 + (b + 1) * 16)
                    node_load(c + NJ, j)

            for j in range(NJ):
                index_load(dst, j, 0, j, 2 * NB * DMAS)
            def b_chunk(b, j, more):
                c = b * NJ + j
                done = 2 * NB * DMAS + (b + 1) * DMAS
                if more:
                    index_load(dst, c, b + 1, j, done)
                else:
                    sp.wait_ge(ring_dma[j], done)
                sp.dma_start(x1_dst[bass.ds(c, 1), :, :].rearrange("a p w -> (a p) w"), ring[0:P, j, :]).then_inc(ring_saved[j], 16)
                sp.wait_ge(c_done, BASE_DONE + 6 * c)
                sp.dma_start(base_dst[bass.ds(c, 1), :, :].rearrange("a p w -> (a p) w"), nodes[0:P, j, W:2 * W]).then_inc(nodes_out[j], 16)
                sp.wait_ge(nodes_ready, 2 * NC + c + 1)
                node_store(NC + c, j)
                if more:
                    sp.wait_ge(nodes_out[j], NB * 48 + (b + 1) * 32)
                    node_load(NC + c + NJ, j)
            with sp.Fori(0, NB - 1) as b:
                for j in range(NJ):
                    b_chunk(b, j, True)
            for j in range(NJ):
                b_chunk(NB - 1, j, False)

            for j in range(NJ):
                index_load(src, j, 0, j, 3 * NB * DMAS)
            with sp.Fori(0, NB - 1) as b:
                for j in range(NJ):
                    index_load(src, None, b + 1, j, (3 * NB + 1 + b) * DMAS)

            def e_load(c, j):
                sp.dma_start(nodes[0:P, j, 0:W], x1_dst[bass.ds(c, 1), :, :].rearrange("a p w -> (a p) w")).then_inc(nodes_in[j], 16)
                sp.dma_start(nodes[0:P, j, W:2 * W], base_dst[bass.ds(c, 1), :, :].rearrange("a p w -> (a p) w")).then_inc(nodes_in[j], 16)
            for j in range(NJ):
                sp.wait_ge(nodes_out[j], NB * 80)
                sp.wait_ge(ring_saved[j], NB * 16)
            sp.wait_ge(softmax_done, 1)
            for j in range(NJ):
                e_load(j, j)
            with sp.Fori(0, NB - 1) as b:
                for j in range(NJ):
                    sp.wait_ge(nodes_ready, 3 * NC + b * NJ + j + 1)
                    e_load((b + 1) * NJ + j, j)
            for j in range(NJ):
                sp.wait_ge(ring_dma[j], 5 * NB * DMAS)

        @block.gpsimd
        def _(pool):
            pool.memset(ident[:, :], 0.0).then_inc(boot_pe, 1)
            pool.memset(w0_bd[:, :], 0.0).then_inc(boot_pool, 1)
            pool.memset(root_bd[:, :], 0.0).then_inc(boot_pool, 1)
            pool.memset(w1_q[:, :, :], 0.0).then_inc(boot_pool, 1)
            pool.wait_ge(boot_pe, 1)
            pool.affine_select(out=ident[:, :], in_=ident[:, :], compare_op=ALU.not_equal, fill=1.0, base=0,
                               pattern=[[-1, 128]], channel_multiplier=1).then_inc(boot_pool, 1)
            pool.iota(scatter_to[:, :], pattern=[[P * SE, NB], [1, SE]], base=N, channel_multiplier=SE).then_inc(boot_pool, 1)

            def gather(table, rows, j):
                pool.sem_inc(cleared, 1)
                for s in range(CE):
                    pool.indirect_dma_start(
                        out=ring[0:P, j, s * F:(s + 1) * F], out_offset=None, in_=table[:, :],
                        in_offset=bass.IndirectOffsetOnAxis(ap=index[0:P, j, s:s + 1], axis=0)).then_inc(ring_dma[j], 16)

            def gather_phase(table, rows, phase, used, saved=False):
                with pool.Fori(0, NB) as b:
                    for j in range(NJ):
                        pool.wait_ge(index_in[j], 16 * NB * phase + 16 * (b + 1))
                        pool.wait_ge(ring_used, NC * used + b * NJ + j + 1)
                        gather(table, rows, j)

            gather_phase(x, N, 0, 0)
            for j in range(NJ):
                pool.wait_ge(nodes_out[j], NB * 32)
            pool.wait_ge(spare_zero, NC * 16)
            with pool.Fori(0, NB) as b:
                for j in range(NJ):
                    pool.wait_ge(ring_filled, b * NJ + j + 1)
                    pool.sem_inc(cleared, 1)
                    for s in range(CE):
                        pool.indirect_dma_start(
                            out=x1_table[:, :], out_offset=bass.IndirectOffsetOnAxis(ap=index[0:P, j, s:s + 1], axis=0),
                            in_=ring[0:P, j, s * F:(s + 1) * F], in_offset=None, compute_op=ALU.add).then_inc(ring_dma[j], 16)
            for j in range(NJ):
                pool.wait_ge(ring_dma[j], 2 * NB * DMAS)
            def b_block(b):
                for j in range(NJ):
                    pool.wait_ge(index_in[j], 16 * NB + 16 * (b + 1))
                    pool.wait_ge(ring_used, NC + b * NJ + j + 1)
                    if not isinstance(b, int):
                        pool.wait_ge(ring_saved[j], 16 * b)
                    gather(x1_table, N + E, j)
            b_block(0)
            with pool.Fori(1, NB) as b:
                b_block(b)
            with pool.Fori(0, NB) as b:
                for j in range(NJ):
                    pool.wait_ge(index_in[j], 16 * NB * 2 + 16 * (b + 1))
                    pool.wait_ge(ring_used, 2 * NC + b * NJ + j + 1)
                    pool.wait_ge(ring_saved[j], 16 * NB)
                    gather(x1_table, N + E, j)
            for j in range(NJ):
                pool.wait_ge(nodes_out[j], NB * 80)
            last_row = pool.to_reg(N - 1)
            with pool.Fori(0, NB) as b:
                for j in range(NJ):
                    pool.wait_ge(ring_filled, NC + b * NJ + j + 1)
                    pool.sem_inc(cleared, 1)
                    for s in range(CE):
                        pool.indirect_dma_start(
                            out=out[:, :], out_offset=bass.IndirectOffsetOnAxis(ap=index[0:P, j, s:s + 1], axis=0),
                            in_=ring[0:P, j, s * F:(s + 1) * F], in_offset=None,
                            bounds_check=last_row, oob_is_err=False).then_inc(ring_dma[j], 16)

        @block.tensor
        def _(pe):
            tq, cq, vq, fq = Uses(2), Uses(2), Uses(4), Uses(4)
            mm = nc.tensor.matmul
            pe.sem_inc(ring_used, NJ)

            def transpose(rows, then=None):
                at, bank = tq.next()
                pe.wait_ge(t_done, tq.room)
                for g in range(G):
                    i = nc.tensor.transpose(T[bank][:, g * P:(g + 1) * P], rows[:, g * GF:(g + 1) * GF], ident[0:P, 0:P])
                    i.then_inc(t_ready, 1) if g == G - 1 else None
                return at

            def product(cols_T, right, n=GF, bias=None, t_at=None, frees=None):
                at, bank = cq.next()
                pe.wait_ge(c_done, cq.room)
                if t_at is not None:
                    pe.wait_ge(t_done, t_at + 1 + CREDIT)
                if bias is not None:
                    mm(C[bank][0:P, :], ones[:, 0:P], bias_row[:, bias, :], start=True, stop=True, skip_group_check=True)
                for g in range(G):
                    i = mm(C[bank][0:P, g * n:(g + 1) * n], cols_T[:, g * P:(g + 1) * P], right,
                           start=bias is None, stop=True, skip_group_check=True)
                    if g == 0 and frees is not None:
                        i.then_inc(frees, 1)
                i.then_inc(c_ready, 1)
                return at

            pe.wait_ge(boot_pool, 5)
            pe.wait_ge(boot_dma, 16 * N_BOOT)
            pe.wait_ge(boot_dve, 2)
            nc.tensor.transpose(T[0][:, 0:GF], root_bd[:, :], ident[:, :]).then_inc(boot_pe, 1)
            for m in range(2):
                for q, (lo, hi) in enumerate(((0, 4 * P), (4 * P, NB * P))):
                    mm(V[2 * m + q][0:33, 0:hi - lo], ones[0:1, 0:33], row_s[0:1, m * NB * P + lo:m * NB * P + hi],
                       start=True, stop=True).then_inc(boot_pe, 1)
            pe.wait_ge(boot_dve, 4)
            pe.wait_ge(t_done, CREDIT)

            def hidden_and_back(nT, k):
                for t in range(4):
                    at, bank = fq.next()
                    pe.wait_ge(f_done, fq.room)
                    mm(V[4 - fq.depth + bank][:, 0:WT], w1_q[:, t, :], nT, start=True, stop=True).then_inc(f_ready, 1)
                at, bank = cq.next()
                pe.wait_ge(c_done, cq.room)
                mm(C[bank][0:P, :], ones[:, 0:P], bias_row[:, 2, :], start=True, stop=True, skip_group_check=True)
                for g in range(G):
                    mm(C[bank][0:P, g * GF:(g + 1) * GF], nT[:, g * P:(g + 1) * P], center[:, :], start=False, stop=True, skip_group_check=True)
                for t in range(4):
                    pe.wait_ge(f_done, fq.at - 3 + t + 1 + CREDIT)
                    for g in range(G):
                        i = mm(C[bank][0:P, (4 * g + t) * F:(4 * g + t + 1) * F], hid[:, t, g * P:(g + 1) * P], w2_c[:, :],
                               start=False, stop=True, skip_group_check=True)
                i.then_inc(c_ready, 1)

            def carries(m):
                at, bank = tq.next()
                pe.wait_ge(t_done, tq.room)
                pe.wait_ge(tails_ready, m + 1)
                nc.tensor.transpose(T[bank][:, 0:P], tails[0:P, :], ident[0:P, 0:P]).then_inc(t_ready, 1)
                at, bank = tq.next()
                pe.wait_ge(t_done, tq.room)
                pe.wait_ge(carry_ready, m + 1)
                nc.tensor.transpose(T[bank][0:P, 0:128], carry_row[:, :], ident[:, :]).then_inc(t_ready, 1)

            tq.restart(); cq.restart()
            with pe.Fori(0, NB) as b:
                tq.loop(b, 6 * NJ + 2); cq.loop(b, 5 * NJ); vq.loop(b, 12 * NJ)
                for j in range(NJ):
                    pe.wait_ge(ring_dma[j], (b + 1) * DMAS)
                    t0 = transpose(unit(ring, j))
                    pe.wait_ge(nodes_in[j], (b + 1) * 16)
                    t1 = transpose(nodes[0:P, j, 0:W])
                    t2 = transpose(nodes[0:P, j, W:2 * W])
                    cs = [product(xT[:, k, :], center[:, :], t_at=t, frees=(ring_used, None, None)[k]) for k, t in enumerate((t0, t1, t2))]
                    ts = []
                    for k in range(3):
                        pe.wait_ge(c_done, cs[k] + 1 + CREDIT)
                        ts.append(transpose(unit(hrow, k)))
                    pe.wait_ge(t_done, ts[0] + 1 + CREDIT)
                    for g in range(G):
                        for q in range(3):
                            at, bank = vq.next()
                            pe.wait_ge(v_done, vq.room)
                            mm(V[bank][0:P, 0:3 * GF], hT[:, 0, g * P:(g + 1) * P], w0_bd[:, q * 3 * GF:(q + 1) * 3 * GF],
                               start=True, stop=True).then_inc(v_ready, 1)
                        if g < 2:
                            product(hT[:, 1 + g, :], root_bd[:, :], bias=0, t_at=ts[1 + g])
                carries(b)
                tq.end(NB, 6 * NJ + 2); cq.end(NB, 5 * NJ); vq.end(NB, 12 * NJ)

            def node_unit(j, loaded):
                pe.wait_ge(nodes_in[j], loaded)
                t = transpose(nodes[0:P, j, 0:W])
                c0 = product(xT[:, 1, :], center[:, :], t_at=t)
                pe.wait_ge(c_done, c0 + 1 + CREDIT)
                t = transpose(unit(hrow, 1))
                c0 = product(hT[:, 1, :], base_bd[:, :], bias=1, t_at=t)
                pe.wait_ge(c_done, c0 + 1 + CREDIT)
                t = transpose(unit(hrow, 1))
                pe.wait_ge(t_done, t + 1 + CREDIT)
                hidden_and_back(xT[:, 1, :], 1)

            pe.wait_ge(v_done, 12 * NC + CREDIT)
            cq.restart()
            with pe.Fori(0, NB) as b:
                tq.loop(b, 3 * NJ); cq.loop(b, 3 * NJ); fq.loop(b, 4 * NJ)
                for j in range(NJ):
                    node_unit(j, NB * 16 + (b + 1) * 16)
                tq.end(NB, 3 * NJ); cq.end(NB, 3 * NJ); fq.end(NB, 4 * NJ)

            def edge_front(j, phase, b):
                pe.wait_ge(ring_dma[j], (phase * NB + b + 1) * DMAS)
                t = transpose(unit(ring, j))
                c0 = product(xT[:, 0, :], center[:, :], t_at=t, frees=ring_used)
                pe.wait_ge(c_done, c0 + 1 + CREDIT)
                return transpose(unit(hrow, 0))

            with pe.Fori(0, NB) as b:
                tq.loop(b, 5 * NJ); cq.loop(b, 6 * NJ); fq.loop(b, 4 * NJ)
                for j in range(NJ):
                    t = edge_front(j, 2, b)
                    product(hT[:, 0, :], base_bd[:, :], bias=1, t_at=t)
                    product(hT[:, 0, :], att_bd[:, :, :].rearrange("f t h -> f (t h)"), n=8 * H)
                    node_unit(j, 2 * NB * 16 + (b + 1) * 16)
                tq.end(NB, 5 * NJ); cq.end(NB, 6 * NJ); fq.end(NB, 4 * NJ)
            with pe.Fori(0, NB) as b:
                tq.loop(b, 2 * NJ); cq.loop(b, 2 * NJ)
                for j in range(NJ):
                    t = edge_front(j, 3, b)
                    product(hT[:, 0, :], src_bd[:, :, :].rearrange("f t h -> f (t h)"), n=4 * H, t_at=t)
                tq.end(NB, 2 * NJ); cq.end(NB, 2 * NJ)

            tq.restart()
            for m in range(4):
                for half in (0, 1):
                    pe.wait_ge((tails_ready, carry_ready)[half], NB + m + 1)
                    for bb in range(NB):
                        at, bank = tq.next()
                        pe.wait_ge(t_done, tq.room)
                        if half == 0:
                            nc.tensor.transpose(T[bank][0:H, 0:P], tails[0:P, bb * H:(bb + 1) * H], ident[0:P, 0:P]).then_inc(t_ready, 1)
                        else:
                            nc.tensor.transpose(T[bank][0:P, 0:H], s_carry[:, bb * P:(bb + 1) * P], ident[0:H, 0:H]).then_inc(t_ready, 1)

            tq.restart(); cq.restart(); vq.restart()
            vq.depth = 2; fq.depth = 2; fq.restart()
            pe.wait_ge(f_done, 8 * NC + CREDIT)
            with pe.Fori(0, NB) as b:
                tq.loop(b, 2 * NJ + 2); cq.loop(b, NJ); vq.loop(b, 8 * NJ); fq.loop(b, 4 * NJ)
                for j in range(NJ):
                    pe.wait_ge(stage_ready, b * NJ + j + 1)
                    t = transpose(stage[0:P, :])
                    pe.wait_ge(t_done, t + 1 + CREDIT)
                    for g in range(G):
                        for q in range(2):
                            at, bank = vq.next()
                            pe.wait_ge(v_done, vq.room)
                            mm(V[bank][0:P, :], hT[:, 0, g * P:(g + 1) * P], gat_bd[:, q * 512:(q + 1) * 512],
                               start=True, stop=True).then_inc(v_ready, 1)
                carries(NB + 4 + b)
                for j in range(NJ):
                    pe.wait_ge(row_ready, b * NJ + j + 1)
                    t = transpose(unit(hrow, 1))
                    pe.wait_ge(t_done, t + 1 + CREDIT)
                    hidden_and_back(xT[:, 1, :], 1)
                tq.end(NB, 2 * NJ + 2); cq.end(NB, NJ); vq.end(NB, 8 * NJ); fq.end(NB, 4 * NJ)

        @block.scalar
        def _(act):
            tq, cq, fq, nq = Uses(2), Uses(2), Uses(4), Uses()
            act.sem_inc(t_done, CREDIT)
            act.sem_inc(f_done, CREDIT)
            act.wait_ge(boot_dve, 4)

            def evac(to, rows=128, width=WT, func=ACT.Copy, **kw):
                at, bank = tq.next()
                act.wait_ge(t_ready, at + 1)
                nc.scalar.activation(to, T[bank][0:rows, 0:width], func, **kw).then_inc(t_done, 1)

            def square(k, rows=None):
                if rows is None:
                    at, bank = cq.next()
                    act.wait_ge(c_ready, at + 1)
                    rows = C[bank][0:P, :]
                nc.scalar.activation(unit(sq, k), rows, ACT.Square).then_inc(sq_ready, 1)

            def root(k):
                at, _ = nq.next()
                act.wait_ge(var_ready, at + 1)
                nc.scalar.activation(unit(std, k), unit(var, k), ACT.Sqrt, scale=1.0 / F, bias=cols[0:P, 3:4]).then_inc(std_ready, 1)

            def hidden():
                for t in range(4):
                    at, bank = fq.next()
                    act.wait_ge(f_ready, at + 1)
                    nc.scalar.activation(hid[:, t, :], V[4 - fq.depth + bank][:, 0:WT], ACT.Relu, bias=cols[:, 0:1]).then_inc(f_done, 1)

            def affine():
                evac(xT[:, 1, :], func=ACT.Identity, scale=cols[:, 1:2], bias=cols[:, 2:3])

            def carries(n):
                evac(tails_row[0:n, 1:1 + P], rows=n, width=P)
                evac(carry[0:P, 0:n], rows=P, width=n)

            def node_unit():
                evac(xT[:, 1, :]); square(1); root(1)
                evac(hT[:, 1, :]); square(1); root(1)
                affine(); hidden(); square(1); root(1)

            with act.Fori(0, NB) as b:
                tq.loop(b, 6 * NJ + 2); cq.loop(b, 5 * NJ); nq.loop(b, 3 * NJ)
                for j in range(NJ):
                    for k in range(3):
                        evac(xT[:, k, :])
                    square(0); square(1); root(0); square(2); root(1); root(2)
                    for k in range(3):
                        evac(hT[:, k, :])
                    cq.next(); cq.next()
                carries(33)
                tq.end(NB, 6 * NJ + 2); cq.end(NB, 5 * NJ); nq.end(NB, 3 * NJ)
            with act.Fori(0, NB) as b:
                tq.loop(b, 3 * NJ); cq.loop(b, 3 * NJ); fq.loop(b, 4 * NJ); nq.loop(b, 3 * NJ)
                for j in range(NJ):
                    node_unit()
                tq.end(NB, 3 * NJ); cq.end(NB, 3 * NJ); fq.end(NB, 4 * NJ); nq.end(NB, 3 * NJ)
            with act.Fori(0, NB) as b:
                tq.loop(b, 5 * NJ); cq.loop(b, 6 * NJ); fq.loop(b, 4 * NJ); nq.loop(b, 4 * NJ)
                for j in range(NJ):
                    evac(xT[:, 0, :]); square(0); root(0)
                    evac(hT[:, 0, :]); cq.next(); cq.next()
                    node_unit()
                tq.end(NB, 5 * NJ); cq.end(NB, 6 * NJ); fq.end(NB, 4 * NJ); nq.end(NB, 4 * NJ)
            with act.Fori(0, NB) as b:
                tq.loop(b, 2 * NJ); cq.loop(b, 2 * NJ); nq.loop(b, NJ)
                for j in range(NJ):
                    evac(xT[:, 0, :]); square(0); root(0)
                    evac(hT[:, 0, :]); cq.next()
                tq.end(NB, 2 * NJ); cq.end(NB, 2 * NJ); nq.end(NB, NJ)
            tq.restart()
            for m in range(4):
                if m == 2:
                    act.wait_ge(exp_in, 1)
                    nc.scalar.activation(beta[0:P, :], beta[0:P, :], ACT.Exp).then_inc(exp_ready, 1)
                    nc.scalar.activation(self_logit[0:P, :], self_logit[0:P, :], ACT.Exp, scale=-1.0).then_inc(exp_ready, 1)
                for bb in range(NB):
                    evac(s_tails[:, 1 + bb * P:1 + (bb + 1) * P], rows=H, width=P)
                for bb in range(NB):
                    evac(carry[0:P, bb * H:(bb + 1) * H], rows=P, width=H)
            tq.restart(); cq.restart(); fq.depth = 2; fq.restart()
            with act.Fori(0, NB) as b:
                tq.loop(b, 2 * NJ + 2); cq.loop(b, NJ); fq.loop(b, 4 * NJ); nq.loop(b, 2 * NJ)
                for j in range(NJ):
                    c = b * NJ + j
                    nc.scalar.activation(stage[0:P, :], diff[0:P, bass.ds(c * W, W)], ACT.Copy).then_inc(stage_ready, 1)
                    evac(hT[:, 0, :])
                carries(F)
                for j in range(NJ):
                    act.wait_ge(sum_ready, b * NJ + j + 1)
                    square(1, unit(hrow, 1)); root(1)
                    affine(); hidden(); square(1); root(1)
                tq.end(NB, 2 * NJ + 2); cq.end(NB, NJ); fq.end(NB, 4 * NJ); nq.end(NB, 2 * NJ)

        @block.vector
        def _(dve):
            v = nc.vector
            steps = Uses()
            tq, cq, vq, nq, rq = Uses(2), Uses(2), Uses(4), Uses(), Uses(2)
            slots = lambda a: a.rearrange("p (s f) -> p s f", f=F)
            wide = lambda a: a.unsqueeze(2).to_broadcast([P, CE, F])

            def step(i):
                at, _ = steps.next()
                i.then_inc(dve_step, 1)
                dve.wait_ge(dve_step, at + 1)

            dve.sem_inc(c_done, CREDIT)
            dve.sem_inc(v_done, CREDIT)
            dve.sem_inc(msgs_done, CREDIT)
            for a, value in ((ones, 1.0), (gat_bd, 0.0), (center, 0.0), (att_bd, 0.0), (src_bd, 0.0), (bias_row, 0.0),
                             (stage, 0.0), (cont, 0.0), (cont_next, 0.0), (row_cont, 0.0), (row_pass, 0.0),
                             (row_pass_back, 0.0), (tails_row, 0.0), (carry_last, 0.0), (tails, 0.0), (carry_row, 0.0)):
                v.memset(a[:, :] if len(a.shape) == 2 else a[:, :, :], value)
            v.memset(next_i[:, :], -1).then_inc(boot_dve, 1)
            dve.wait_ge(boot_dve, 1)
            for t in range(4):
                q = slice(t * F, (t + 1) * F)
                i = v.memset(center[q, q], 1.0 / F)
            step(i)
            dve.wait_ge(boot_pool, 5)
            dve.wait_ge(boot_dma, 16 * N_BOOT)
            v.memset(cols[:, 3:4], EPS)
            step(v.tensor_tensor(center[:, :], ident[:, :], center[:, :], ALU.subtract))
            v.tensor_copy(row_s, row_i[0:1, :]).then_inc(boot_dve, 1)
            tmp = hrow[:, 0, 0:H * F]
            heads = lambda a: a.rearrange("p (h f) -> p h f", f=F)
            for k in range(2):
                step(v.tensor_tensor(tmp, gat[:, :], att[:, k, :], ALU.mult))
                step(v.tensor_reduce(att_vec[:, k * H:(k + 1) * H], heads(tmp), AX.X, ALU.add))
            for t in range(4):
                q = slice(t * F, (t + 1) * F)
                v.tensor_copy(att_bd[q, t, :], att_vec[q, :])
                v.tensor_copy(src_bd[q, t, :], att_vec[q, 0:H])
            mean = hrow[:, 1, 0:H]
            step(v.tensor_reduce(mean, heads(gat[:, :]), AX.X, ALU.add))
            step(v.tensor_scalar(mean, mean, 1.0 / F, None, ALU.mult))
            step(v.tensor_tensor(heads(tmp), heads(gat[:, :]), mean.unsqueeze(2).to_broadcast([128, H, F]), ALU.subtract))
            for t in range(4):
                q = slice(t * F, (t + 1) * F)
                i = v.tensor_scalar(gat_bd[q, :].rearrange("p (h t o) -> p h t o", h=H, t=4)[:, :, t, :], heads(hrow[q, 0, 0:H * F]),
                                    1.0 / H, None, ALU.mult)
            step(i)
            step(v.tensor_reduce(base_bd[:, :], gat_bd[:, :].rearrange("p (h c) -> p c h", h=H), AX.X, ALU.add))
            v.tensor_tensor(base_bd[:, :], base_bd[:, :], center[:, :], ALU.add)
            m1 = hrow[:, 2, 0:1]
            step(v.tensor_reduce(m1, w2_c[:, :], AX.X, ALU.add))
            step(v.tensor_scalar(m1, m1, 1.0 / F, None, ALU.mult))
            v.tensor_tensor(w2_c[:, :], w2_c[:, :], m1.to_broadcast([128, F]), ALU.subtract)
            for k in (1, 2):
                m2 = hrow[0:1, 2, k:k + 1]
                step(v.tensor_reduce(m2, bias_row[0:1, k, 0:F], AX.X, ALU.add))
                step(v.tensor_scalar(m2, m2, 1.0 / F, None, ALU.mult))
                step(v.tensor_tensor(bias_row[0:1, k, 0:F], bias_row[0:1, k, 0:F], m2.to_broadcast([1, F]), ALU.subtract))
            for k in range(3):
                i = v.tensor_copy(bias_row[0:1, k, F:W].rearrange("p (s f) -> p s f", f=F),
                                  bias_row[0:1, k, 0:F].unsqueeze(1).to_broadcast([1, CE - 1, F]))
            step(v.tensor_copy(dst_f[0:P, :], dst_i[0:P, :]))
            blocks = lambda a: a[0:P, :].rearrange("p (b s) -> p b s", b=NB)
            d = blocks(dst_f)
            same = (d[:, :, 1:SE], d[:, :, 0:SE - 1])
            v.tensor_tensor(blocks(cont)[:, :, 1:SE], *same, ALU.is_equal)
            v.tensor_tensor(blocks(cont_next)[:, :, 0:SE - 1], *same, ALU.is_equal)
            v.tensor_tensor(blocks(head), d, d[:, :, 0:1].to_broadcast([P, NB, SE]), ALU.is_equal)
            v.tensor_tensor(blocks(tail), d, d[:, :, SE - 1:SE].to_broadcast([P, NB, SE]), ALU.is_equal)
            nxt, on, spare = hrow[0:P, 0, 0:NB], hrow[0:P, 1, 0:TE], hrow[0:P, 2, 0:TE]
            v.tensor_copy(nxt, next_i[0:P, :])
            step(v.tensor_copy(spare, scatter_to[0:P, :]))
            step(v.tensor_copy(on, cont_next[0:P, :]))
            step(v.tensor_tensor(on.rearrange("p (b s) -> p b s", b=NB)[:, :, SE - 1], d[:, :, SE - 1], nxt, ALU.is_equal))
            step(v.tensor_tensor(spare, spare, dst_f[0:P, :], ALU.subtract))
            step(v.tensor_tensor(spare, spare, on, ALU.mult))
            step(v.tensor_tensor(spare, spare, dst_f[0:P, :], ALU.add))
            v.tensor_copy(scatter_to[0:P, :], spare)
            dve.wait_ge(boot_pe, 6)
            v.tensor_copy(root_bd[:, :], T[0][:, 0:GF])
            for m in range(2):
                v.tensor_copy(row_f[:, m * NB * P:m * NB * P + 4 * P], V[2 * m][0:33, 0:4 * P])
                i = v.tensor_copy(row_f[:, m * NB * P + 4 * P:(m + 1) * NB * P], V[2 * m + 1][0:33, 0:P])
            step(i)
            R = NB * P
            v.tensor_tensor(row_cont[:, 1:R], row_f[:, 1:R], row_f[:, R:2 * R - 1], ALU.is_equal)
            step(v.tensor_tensor(whole, row_f[:, 0:R], row_f[:, R:2 * R], ALU.is_equal))
            v.tensor_tensor(row_pass[:, 1:R], row_cont[:, 1:R], whole[:, 0:R - 1], ALU.mult)
            v.tensor_tensor(row_pass_back[:, 0:R - 1], row_cont[:, 1:R], whole[:, 1:R], ALU.mult)
            step(v.tensor_scalar(attr[0:P, :], attr[0:P, :], 1.0, 0.0, ALU.min, ALU.max))
            hat = hats[0:P, :].rearrange("p (a k t) -> p a k t", a=2, k=3)
            for a in range(2):
                for k in range(3):
                    u = attr[0:P, :].rearrange("p (t a) -> p a t", a=2)[:, a, :]
                    i = v.tensor_scalar(hat[:, a, k, :], u, 0.5 * k, None, ALU.subtract)
            step(i)
            step(v.scalar_tensor_tensor(out=hats[0:P, :], in0=hats[0:P, :], scalar=-1.0, in1=hats[0:P, :], op0=ALU.mult, op1=ALU.max))
            step(v.tensor_scalar(hats[0:P, :], hats[0:P, :], -2.0, 1.0, ALU.mult, ALU.add))
            step(v.tensor_scalar(hats[0:P, :], hats[0:P, :], 0.0, None, ALU.max))
            for k in range(KS):
                i = v.tensor_tensor(basis[0:P, :].rearrange("p (g k t) -> p g k t", k=KS, t=4)[:, :, k, :],
                                    hat[:, 0, k // 3, :].rearrange("p (g t) -> p g t", t=4),
                                    hat[:, 1, k % 3, :].rearrange("p (g t) -> p g t", t=4), ALU.mult)
            step(i)
            v.memset(var[:, :, :], 0.0).then_inc(boot_dve, 2)

            def spread(k):
                at, _ = nq.next()
                dve.wait_ge(sq_ready, at + 1)
                v.tensor_reduce(unit(var, k), slots(unit(sq, k)), AX.X, ALU.add).then_inc(var_ready, 1)
                return at

            def scale_of(k, at):
                dve.wait_ge(std_ready, at + 1)
                step(v.reciprocal(unit(rstd, k), unit(std, k)))

            def bank_ready():
                at, bank = cq.next()
                dve.wait_ge(c_ready, at + 1)
                return at, C[bank][0:P, :]

            def relu_rows(k, at):
                _, rows = bank_ready()
                scale_of(k, at)
                v.scalar_tensor_tensor(out=slots(unit(hrow, k)), in0=slots(rows), scalar=0.0, in1=wide(unit(rstd, k)),
                                       op0=ALU.max, op1=ALU.mult).then_inc(c_done, 1)

            def rows_over_std(k, at):
                at_c, rows = bank_ready()
                scale_of(k, at)
                v.tensor_tensor(slots(unit(hrow, k)), slots(rows), wide(unit(rstd, k)), ALU.mult).then_inc(c_done, 1)
                return at_c

            def scans_and_carry(rows, b, n):
                here = bass.ds(b * SE, SE)
                feature = rows[0:P, :].rearrange("p (t f) -> p t f", f=F)
                dve.wait_ge(msgs_done, rq.at + 1 + CREDIT)
                for f in range(F):
                    i = v.tensor_tensor_scan(feature[:, here, f], cont[0:P, here], feature[:, here, f], 0.0, ALU.mult, ALU.add)
                if n > F:
                    i = v.tensor_tensor_scan(degree[0:P, here], cont[0:P, here], ones[0:P, 0:SE], 0.0, ALU.mult, ALU.add)
                step(i)
                last = bass.ds(b * SE + SE - 1, 1)
                if n > F:
                    v.tensor_copy(tails[0:P, F:F + 1], degree[0:P, last])
                v.tensor_copy(tails[0:P, 0:F].rearrange("p (a f) -> p a f", a=1), feature[:, last, :]).then_inc(tails_ready, 1)
                at, _ = tq.next()
                dve.wait_ge(t_done, at + 1 + CREDIT)
                step(v.tensor_tensor(carry_in[0:n, :], tails_row[0:n, 0:P], row_cont[0:n, bass.ds(b * P, P)], ALU.mult))
                v.tensor_tensor_scan(carry_row[0:n, :], row_pass[0:n, bass.ds(b * P, P)], carry_in[0:n, :], carry_last[0:n, 0:1],
                                     ALU.mult, ALU.add).then_inc(carry_ready, 1)
                at, _ = tq.next()
                dve.wait_ge(t_done, at + 1 + CREDIT)
                v.tensor_copy(tails_row[0:n, 0:1], tails_row[0:n, P:P + 1])
                v.tensor_copy(carry_last[0:n, :], carry_row[0:n, P - 1:P])
                for f in range(F):
                    i = v.scalar_tensor_tensor(out=feature[:, here, f], in0=head[0:P, here], scalar=carry[0:P, f:f + 1],
                                               in1=feature[:, here, f], op0=ALU.mult, op1=ALU.add)
                if n > F:
                    i = v.scalar_tensor_tensor(out=degree[0:P, here], in0=head[0:P, here], scalar=carry[0:P, F:F + 1],
                                               in1=degree[0:P, here], op0=ALU.mult, op1=ALU.add)
                step(i)

            with dve.Fori(0, NB) as b:
                STEPS = 3 * NJ + 3
                tq.loop(b, 6 * NJ + 2); cq.loop(b, 5 * NJ); vq.loop(b, 12 * NJ); nq.loop(b, 3 * NJ); rq.loop(b, 4 * NJ); steps.loop(b, STEPS)
                for j in range(NJ):
                    c = b * NJ + j
                    for _ in range(6):
                        tq.next()
                    n0 = spread(0); n1 = spread(1)
                    relu_rows(0, n0)
                    n2 = spread(2)
                    relu_rows(1, n1); relu_rows(2, n2)
                    pending = []
                    def reduce_group():
                        g, at = pending.pop(0)
                        dve.wait_ge(v_done, at + 1 + CREDIT)
                        v.tensor_reduce(msgs[0:P, bass.ds(c * W + g * GF, GF)],
                                        products[0:P, (g % 2) * KS * GF:(g % 2 + 1) * KS * GF].rearrange("p (k c) -> p c k", k=KS),
                                        AX.X, ALU.add).then_inc(msgs_done, 1)
                    for g in range(G):
                        rq.next()
                        dve.wait_ge(msgs_done, rq.room)
                        for q in range(3):
                            at, bank = vq.next()
                            dve.wait_ge(v_ready, at + 1)
                            to = (g % 2) * KS * GF + q * 3 * GF
                            v.tensor_tensor(products[0:P, to:to + 3 * GF].rearrange("p (k o) -> p k o", o=F),
                                            V[bank][0:P, 0:3 * GF].rearrange("p (k o) -> p k o", o=F),
                                            basis[0:P, bass.ds((c * G + g) * 4 * KS + q * 12, 12)].unsqueeze(2).to_broadcast([P, 12, F]),
                                            ALU.mult).then_inc(v_done, 1)
                        pending.append((g, at))
                        if g > 0:
                            reduce_group()
                        if g < 2:
                            _, rows = bank_ready()
                            part = nodes[0:P, j, g * W:(g + 1) * W]
                            i = v.tensor_tensor(part, rows, part, ALU.add)
                            i.then_inc(c_done, 1)
                            if g == 1:
                                dve.wait_ge(c_done, cq.at + 1 + CREDIT)
                                dve.sem_inc(nodes_ready, 1)
                    reduce_group()
                scans_and_carry(msgs, b, F + 1)
                tq.end(NB, 6 * NJ + 2); cq.end(NB, 5 * NJ); vq.end(NB, 12 * NJ); nq.end(NB, 3 * NJ); rq.end(NB, 4 * NJ); steps.end(NB, STEPS)

            def node_unit(j):
                part = nodes[0:P, j, 0:W]
                tq.next(); tq.next(); tq.next()
                relu_rows(1, spread(1))
                rows_over_std(1, spread(1))
                finish_rows(part, part, nodes_ready)

            def finish_rows(x1_part, to, signal):
                v.tensor_tensor(slots(x1_part), slots(x1_part), be2_b[0:P, :].unsqueeze(1).to_broadcast([P, CE, F]), ALU.add)
                at_c = rows_over_std(1, spread(1))
                dve.wait_ge(c_done, at_c + 1 + CREDIT)
                step(v.tensor_tensor(slots(unit(hrow, 1)), slots(unit(hrow, 1)), g2_b[0:P, :].unsqueeze(1).to_broadcast([P, CE, F]), ALU.mult))
                v.tensor_tensor(to, x1_part, unit(hrow, 1), ALU.add).then_inc(signal, 1)

            step(v.tensor_scalar(degree[0:P, :], degree[0:P, :], 1.0, None, ALU.max))
            step(v.reciprocal(degree[0:P, :], degree[0:P, :]))
            cq.restart()
            with dve.Fori(0, NB) as b:
                tq.loop(b, 3 * NJ); cq.loop(b, 3 * NJ); nq.loop(b, 3 * NJ); steps.loop(b, 4 * NJ)
                for j in range(NJ):
                    c = b * NJ + j
                    dve.wait_ge(ring_dma[j], NB * DMAS + b * DMAS)
                    v.tensor_tensor(slots(ring[0:P, j, :]), slots(msgs[0:P, bass.ds(c * W, W)]),
                                    wide(degree[0:P, bass.ds(c * CE, CE)]), ALU.mult)
                    v.tensor_copy(index[0:P, j, :], scatter_to[0:P, bass.ds(c * CE, CE)]).then_inc(ring_filled, 1)
                    node_unit(j)
                tq.end(NB, 3 * NJ); cq.end(NB, 3 * NJ); nq.end(NB, 3 * NJ); steps.end(NB, 4 * NJ)

            heads_of = lambda a: a[0:P, :].rearrange("p (h t) -> p h t", h=H)
            with dve.Fori(0, NB) as b:
                tq.loop(b, 5 * NJ); cq.loop(b, 6 * NJ); nq.loop(b, 4 * NJ); steps.loop(b, 7 * NJ)
                for j in range(NJ):
                    c = b * NJ + j
                    now = bass.ds(c * CE, CE)
                    tq.next(); tq.next()
                    relu_rows(0, spread(0))
                    dve.wait_ge(c_done, cq.at + 1 + CREDIT)
                    v.tensor_copy(diff[0:P, bass.ds(c * W, W)], unit(hrow, 0))
                    _, rows = bank_ready()
                    dve.wait_ge(nodes_in[j], 2 * NB * 16 + (b + 1) * 16)
                    v.tensor_copy(nodes[0:P, j, W:2 * W], rows).then_inc(c_done, 1)
                    _, rows = bank_ready()
                    logits = rows[:, 0:2 * H * CE].rearrange("p (s h) -> p h s", h=2 * H)
                    step(v.tensor_copy(heads_of(beta)[:, :, now], logits[:, H:2 * H, :]))
                    v.tensor_tensor(heads_of(self_logit)[:, :, now], logits[:, 0:H, :], heads_of(beta)[:, :, now], ALU.add).then_inc(c_done, 1)
                    dve.wait_ge(c_done, cq.at + 1 + CREDIT)
                    step(v.scalar_tensor_tensor(out=heads_of(self_logit)[:, :, now], in0=heads_of(self_logit)[:, :, now], scalar=SLOPE,
                                                in1=heads_of(self_logit)[:, :, now], op0=ALU.mult, op1=ALU.max))
                    node_unit(j)
                tq.end(NB, 5 * NJ); cq.end(NB, 6 * NJ); nq.end(NB, 4 * NJ); steps.end(NB, 7 * NJ)
            with dve.Fori(0, NB) as b:
                tq.loop(b, 2 * NJ); cq.loop(b, 2 * NJ); nq.loop(b, NJ); steps.loop(b, 3 * NJ)
                for j in range(NJ):
                    c = b * NJ + j
                    now = bass.ds(c * CE, CE)
                    tq.next(); tq.next()
                    relu_rows(0, spread(0))
                    dve.wait_ge(c_done, cq.at + 1 + CREDIT)
                    v.tensor_tensor(diff[0:P, bass.ds(c * W, W)], unit(hrow, 0), diff[0:P, bass.ds(c * W, W)], ALU.subtract)
                    _, rows = bank_ready()
                    bt = heads_of(beta)[:, :, now]
                    v.tensor_tensor(bt, rows[:, 0:H * CE].rearrange("p (s h) -> p h s", h=H), bt, ALU.add).then_inc(c_done, 1)
                    dve.wait_ge(c_done, cq.at + 1 + CREDIT)
                    step(v.scalar_tensor_tensor(out=bt, in0=bt, scalar=SLOPE, in1=bt, op0=ALU.mult, op1=ALU.max))
                    step(v.tensor_tensor(bt, bt, heads_of(self_logit)[:, :, now], ALU.subtract))
                tq.end(NB, 2 * NJ); cq.end(NB, 2 * NJ); nq.end(NB, NJ); steps.end(NB, 3 * NJ)

            tq.restart()
            def join(a, forward, op):
                edge = SE - 1 if forward else 0
                v.tensor_copy(tails[0:P, 0:H * NB].rearrange("p (b h) -> p h b", h=H),
                              a[0:P, :].rearrange("p (h b s) -> p h b s", h=H, b=NB)[:, :, :, edge]).then_inc(tails_ready, 1)
                for _ in range(NB):
                    at, _ = tq.next()
                dve.wait_ge(t_done, at + 1 + CREDIT)
                if forward:
                    step(v.tensor_tensor(s_in, s_tails[:, 0:R], row_cont[0:H, :], ALU.mult))
                    v.tensor_tensor_scan(s_carry, row_pass[0:H, :], s_in, 0.0, ALU.mult, op).then_inc(carry_ready, 1)
                else:
                    v.memset(s_in[:, R - 1:R], 0.0)
                    step(v.tensor_tensor(s_in[:, 0:R - 1], s_tails[:, 2:R + 1], row_cont[0:H, 1:R], ALU.mult))
                    v.tensor_tensor_scan(s_carry[:, ::-1], row_pass_back[0:H, ::-1], s_in[:, ::-1], 0.0, ALU.mult, op).then_inc(carry_ready, 1)
                for _ in range(NB):
                    at, _ = tq.next()
                dve.wait_ge(t_done, at + 1 + CREDIT)
                by = lambda x: x.rearrange("p (h b s) -> p h b s", h=H, b=NB)
                mask = (head if forward else tail)[0:P, :].rearrange("p (b s) -> p b s", b=NB).unsqueeze(1).to_broadcast([P, H, NB, SE])
                step(v.tensor_tensor(by(masked[0:P, :]), mask,
                                     carry[0:P, 0:H * NB].rearrange("p (b h) -> p h b", h=H).unsqueeze(3).to_broadcast([P, H, NB, SE]), ALU.mult))
                step(v.tensor_tensor(a[0:P, :], a[0:P, :], masked[0:P, :], op))

            def each_head(to, frm, op, forward=True):
                for h in range(H):
                    way = slice(None) if forward else slice(None, None, -1)
                    mask = (cont if forward else cont_next)[0:P, way]
                    i = v.tensor_tensor_scan(heads_of(to)[:, h, way], mask, heads_of(frm)[:, h, way], 0.0, ALU.mult, op)
                step(i)

            v.memset(s_tails[:, 0:1], 0.0)
            each_head(self_logit, beta, ALU.max)
            join(self_logit, True, ALU.max)
            each_head(self_logit, self_logit, ALU.max, False)
            join(self_logit, False, ALU.max)
            step(v.tensor_tensor(beta[0:P, :], beta[0:P, :], self_logit[0:P, :], ALU.subtract))
            dve.sem_inc(exp_in, 1)
            dve.wait_ge(exp_ready, 2)
            each_head(denom, beta, ALU.add)
            join(denom, True, ALU.add)
            each_head(denom, denom, ALU.max, False)
            join(denom, False, ALU.max)
            step(v.scalar_tensor_tensor(out=denom[0:P, :], in0=self_logit[0:P, :], scalar=1e-16, in1=denom[0:P, :], op0=ALU.add, op1=ALU.add))
            step(v.reciprocal(denom[0:P, :], denom[0:P, :]))
            step(v.tensor_tensor(beta[0:P, :], beta[0:P, :], denom[0:P, :], ALU.mult))
            for a in (tails_row, carry_last):
                i = v.memset(a[:, :], 0.0)
            step(i)
            dve.sem_inc(softmax_done, 1)

            tq.restart(); cq.restart(); vq.restart(); vq.depth = 2; rq.restart()
            with dve.Fori(0, NB) as b:
                STEPS = 3 + 3 * NJ
                tq.loop(b, 2 * NJ + 2); cq.loop(b, NJ); vq.loop(b, 8 * NJ); nq.loop(b, 2 * NJ); rq.loop(b, 4 * NJ); steps.loop(b, STEPS)
                for j in range(NJ):
                    c = b * NJ + j
                    tq.next()
                    pending = []
                    def reduce_heads():
                        g, at = pending.pop(0)
                        dve.wait_ge(v_done, at + 1 + CREDIT)
                        v.tensor_reduce(diff[0:P, bass.ds(c * W + g * GF, GF)],
                                        weighted[0:P, (g % 2) * H * GF:(g % 2 + 1) * H * GF].rearrange("p (h c) -> p c h", h=H),
                                        AX.X, ALU.add).then_inc(msgs_done, 1)
                    for g in range(G):
                        rq.next()
                        dve.wait_ge(msgs_done, rq.room)
                        for q in range(2):
                            at, bank = vq.next()
                            dve.wait_ge(v_ready, at + 1)
                            to = (g % 2) * H * GF + q * 512
                            v.tensor_tensor(weighted[0:P, to:to + 512].rearrange("p (h t o) -> p h t o", h=4, t=4),
                                            V[bank][0:P, :].rearrange("p (h t o) -> p h t o", h=4, t=4),
                                            heads_of(beta)[:, 4 * q:4 * q + 4, bass.ds(c * CE + 4 * g, 4)].unsqueeze(3).to_broadcast([P, 4, 4, F]),
                                            ALU.mult).then_inc(v_done, 1)
                        pending.append((g, at))
                        if g > 0:
                            reduce_heads()
                    reduce_heads()
                scans_and_carry(diff, b, F)
                for j in range(NJ):
                    c = b * NJ + j
                    tq.next()
                    dve.wait_ge(nodes_in[j], 3 * NB * 16 + (b + 1) * 32)
                    v.tensor_tensor(unit(hrow, 1), diff[0:P, bass.ds(c * W, W)], nodes[0:P, j, W:2 * W], ALU.add).then_inc(sum_ready, 1)
                    scale_of(1, spread(1))
                    v.tensor_tensor(slots(unit(hrow, 1)), slots(unit(hrow, 1)), wide(unit(rstd, 1)), ALU.mult).then_inc(row_ready, 1)
                    dve.wait_ge(ring_dma[j], 4 * NB * DMAS + b * DMAS)
                    v.tensor_copy(index[0:P, j, :], scatter_to[0:P, bass.ds(c * CE, CE)])
                    finish_rows(nodes[0:P, j, 0:W], ring[0:P, j, :], ring_filled)
                    dve.wait_ge(ring_filled, NC + c + 1)
                    dve.sem_inc(nodes_ready, 1)
                tq.end(NB, 2 * NJ + 2); cq.end(NB, NJ); vq.end(NB, 8 * NJ); nq.end(NB, 2 * NJ); rq.end(NB, 4 * NJ); steps.end(NB, STEPS)


_INS = ["x", "src", "dst", "edge_attr_2", "L0_gnn_weight", "L0_gnn_root_w", "L0_gnn_root_b", "L1_gnn_W_gat",
        "L1_gnn_att_src", "L1_gnn_att_dst", "L1_gnn_bias_gat", "L1_gnn_w1", "L1_gnn_b1", "L1_gnn_w2", "L1_gnn_b2",
        "L1_gnn_g1", "L1_gnn_be1", "L1_gnn_g2", "L1_gnn_be2"]


def kernel(**inputs):
    import numpy as np
    import concourse.bacc as bacc
    from concourse.bass_utils import run_bass_kernel_spmd

    nc = bacc.Bacc("TRN2", target_bir_lowering=False, num_devices=1)
    arrays, args = {}, []
    for name in _INS:
        a = np.ascontiguousarray(inputs[name])
        arrays[f"in_{name}"] = a
        args.append(nc.dram_tensor(f"in_{name}", a.shape, mybir.dt.from_np(a.dtype), kind="ExternalInput").ap())
    out = nc.dram_tensor("out_rows", (N, F), F32, kind="ExternalOutput").ap()
    gnn_program(nc, *args, out)
    r = run_bass_kernel_spmd(nc, [arrays], core_ids=[0])
    return r.results[0]["out_rows"]
```

```python
import concourse.bass as bass
from concourse import mybir
from concourse.alu_op_type import AluOpType as ALU
from contextlib import ExitStack

F32 = mybir.dt.float32
I32 = mybir.dt.int32
ACT = mybir.ActivationFunctionType
AX = mybir.AxisListType

N, E, F, H, HID, KS = 100000, 50000, 32, 8, 128, 9
P = 125
TN = N // P
NB, NJ, CE = 5, 5, 16
SE = NJ * CE
TE = NB * SE
NC = NB * NJ
CN = TN // NC
W = CE * F
G = CE // 4
GF = 4 * F
WT = G * P
EPS = 1e-5
SLOPE = 0.2
DMAS = 16 * CE
N_BOOT = 2 + 6 * 4 + 2 + 2 + 2 + 3 + 2 + 2
UNITS = {"C": 4, "B": 3, "D": 3}
FIRST = {"C": 0, "B": 20, "D": 35}
OUT_DONE = [NB * 32 + 16 * NB * sum(j < n for n in UNITS.values()) for j in range(NJ)]
CREDIT = 4


class Uses:

    def __init__(self, depth=1):
        self.depth, self.base, self.n = depth, 0, 0

    def next(self):
        self.at = self.base + self.n
        self.room = self.at + CREDIT - min(self.n, self.depth - 1)
        bank = self.n % self.depth
        self.n += 1
        return self.at, bank

    def loop(self, b, per):
        self.first = self.base + self.n
        self.base, self.n = self.first + b * per, 0

    def end(self, times, per):
        assert self.n == per, (self.n, per)
        self.base, self.n = self.first + times * per, 0

    def restart(self):
        self.base, self.n = self.base + self.n, 0


NORMED = (2, 0)
HE = (0, 3, 4, 0, 3)


def waves(name, before):
    out = []
    for w in range(NJ if name else 2):
        wave = {}
        for part, lag in (("n3", 2), ("n2", 1), ("n1", 0), ("e2", 1), ("e1", 0)):
            back = w < lag
            phase, j = (before, w - lag + NJ) if back else (name, w - lag)
            if phase and (phase != "C" if part[0] == "e" else j < UNITS[phase]):
                wave[part] = (phase, j, back)
        out.append(wave)
    return out


PER = {name: dict(t=3 * n + (name != "C") * NJ * (3 if name == "B" else 2), c=3 * n + (name != "C") * NJ * 2, f=4 * n,
                  n=3 * n + (name != "C") * NJ, steps=4 * n + {"C": 2 * NJ, "B": 3 * NJ, "D": 3 * NJ}[name])
       for name, n in UNITS.items()}
LOADED = [NB * 16 * (1 + sum(j < n for n in UNITS.values())) for j in range(NJ)]


def gnn_program(nc, x, src, dst, edge_attr, w0, root_w, root_b, w_gat, att_src, att_dst, bias_gat,
                w1, b1, w2, b2, g1, be1, g2, be2, out):
    x1_table = nc.dram_tensor("x1_table", [N + E, F], F32, kind="Internal").ap()
    x1_plain = nc.dram_tensor("x1_plain", [P, TN * F], F32, kind="Internal").ap()
    x1_dst = nc.dram_tensor("x1_dst", [NC, P, W], F32, kind="Internal").ap()
    base_dst = nc.dram_tensor("base_dst", [NC, P, W], F32, kind="Internal").ap()
    x_rows = x.rearrange("(p t) f -> p (t f)", p=P)
    x1_rows = x1_table[0:N, :].rearrange("(p t) f -> p (t f)", p=P)
    spare_rows = x1_table[N:N + E, :].rearrange("(c p s) f -> c p (s f)", c=NC, p=P)
    out_rows = out.rearrange("(p t) f -> p (t f)", p=P)
    edge_slots = lambda a: a.rearrange("(b p s) -> p b s", b=NB, p=P)

    with ExitStack() as ctx:
        sb = lambda name, shape, dt=F32: ctx.enter_context(nc.sbuf_tensor(name, shape, dt))
        ps = lambda name: ctx.enter_context(nc.psum_tensor(name, [128, 512], F32))
        sem = lambda name: ctx.enter_context(nc.semaphore(name))

        region1 = sb("region1", [128, TE * F])
        region2 = sb("region2", [128, TE * F])
        msgs = region1
        beta = region1[:, 0:H * TE]
        self_logit = region1[:, H * TE:2 * H * TE]
        denom = region1[:, 2 * H * TE:3 * H * TE]
        masked = region1[:, 3 * H * TE:4 * H * TE]
        weighted = region1[:, 3 * H * TE:3 * H * TE + 2048]
        basis = region2[:, 0:TE * KS]
        products = region2[:, TE * KS:TE * KS + 2 * KS * GF]
        w0_bd = region2[:, 5904:5904 + KS * GF]
        attr = region1[:, 0:800]
        hats = region1[:, 800:3200]
        row_f = region1[0:33, 3200:3200 + 2 * NB * P]
        row_s = region1[0:1, 4500:4500 + 2 * NB * P]
        whole = region1[0:33, 5800:5800 + NB * P]
        row_i = region1[0:1, 6500:6500 + 2 * NB * P].bitcast(I32)
        dst_i = region1[:, 7800:7800 + TE].bitcast(I32)
        dst_f = region1[:, 8200:8200 + TE]
        att = region1[:, 8600:8600 + 2 * H * F].rearrange("p (k c) -> p k c", k=2)
        gat = region1[:, 9200:9200 + H * F]
        diff = region2

        ring = sb("ring", [128, NJ, W])
        index = sb("index", [128, NJ, CE], I32)
        index_out = sb("index_out", [128, NJ, CE], I32)
        nodes = sb("nodes", [128, NJ, 2 * W])
        xT = sb("xT", [128, 3, WT]); hT = sb("hT", [128, 5, WT])
        sq = sb("sq", [128, 4, W]); hrow = sb("hrow", [128, 4, W])
        var = sb("var", [128, 4, CE]); std = sb("std", [128, 4, CE]); rstd = sb("rstd", [128, 4, CE])
        hid = sb("hid", [128, 4, WT])
        stage = sb("stage", [128, W])

        ident = sb("ident", [128, 128]); ident_bias = sb("ident_bias", [128, 128]); center = sb("center", [128, GF])
        root_bd = sb("root_bd", [128, GF])
        gat_bd = sb("gat_bd", [128, H * GF])
        base_bd = sb("base_bd", [128, GF])
        att_vec = sb("att_vec", [128, 2 * H])
        att_bd = sb("att_bd", [128, 4, 2 * H]); src_bd = sb("src_bd", [128, 4, H])
        w1_q = sb("w1_q", [128, 4, HID]); w2_c = sb("w2_c", [128, F])
        cols = sb("cols", [128, 8])
        ones = sb("ones", [128, 128])
        bias_row = sb("bias_row", [128, 2, W])
        g2_b = sb("g2_b", [128, F]); be2_b = sb("be2_b", [128, F])
        cont = sb("cont", [128, TE]); cont_next = sb("cont_next", [128, TE])
        head = sb("head", [128, TE]); tail = sb("tail", [128, TE])
        degree = sb("degree", [128, TE])
        scatter_to = sb("scatter_to", [128, TE], I32)
        row_cont = sb("row_cont", [33, NB * P]); row_pass = sb("row_pass", [33, NB * P])
        row_pass_back = sb("row_pass_back", [33, NB * P])
        tails = sb("tails", [128, NB * (F + 1)]); tails_row = sb("tails_row", [33, 1 + P])
        carry_in = sb("carry_in", [33, P]); carry_row = sb("carry_row", [128, P]); carry_last = sb("carry_last", [33, 1])
        carry = sb("carry", [128, NB * (F + 1)])
        next_i = sb("next_i", [128, NB], I32)
        rows = hid[:, :, :].rearrange("p t w -> p (t w)")
        a_tails, a_in, a_carry = rows[0:F + 1, 0:1 + NB * P], rows[0:F + 1, 640:640 + NB * P], rows[0:F + 1, 1280:1280 + NB * P]
        flat = nodes[:, :, :].rearrange("p j w -> p (j w)")
        s_tails, s_in, s_carry = flat[0:H, 0:1 + NB * P], flat[0:H, 640:640 + NB * P], flat[0:H, 1280:1280 + NB * P]

        T = [ps(f"T{i}") for i in range(2)]
        C = [ps(f"C{i}") for i in range(2)]
        V = [ps(f"V{i}") for i in range(4)]

        boot_dma = sem("boot_dma"); boot_pool = sem("boot_pool"); boot_dve = sem("boot_dve")
        boot_pe = sem("boot_pe"); boot_act = sem("boot_act")
        ring_dma = [sem(f"ring_dma{j}") for j in range(NJ)]
        index_in = [sem(f"index_in{j}") for j in range(NJ)]
        ring_used = sem("ring_used")
        ring_saved = [sem(f"ring_saved{j}") for j in range(NJ)]
        ring_filled = sem("ring_filled")
        nodes_in = [sem(f"nodes_in{j}") for j in range(NJ)]
        nodes_ready = sem("nodes_ready")
        base_ready = sem("base_ready")
        rows_used = sem("rows_used")
        nodes_out = [sem(f"nodes_out{j}") for j in range(NJ)]
        spare_zero = sem("spare_zero")
        t_ready = sem("t_ready"); t_done = sem("t_done")
        c_ready = sem("c_ready"); c_done = sem("c_done")
        v_ready = sem("v_ready"); v_done = sem("v_done")
        f_ready = sem("f_ready"); f_done = sem("f_done")
        sq_ready = sem("sq_ready"); var_ready = sem("var_ready"); std_ready = sem("std_ready")
        dve_step = sem("dve_step")
        tails_ready = sem("tails_ready"); carry_ready = sem("carry_ready")
        exp_ready = sem("exp_ready")
        cleared = sem("cleared")
        exp_in = sem("exp_in")
        softmax_done = sem("softmax_done")
        sum_ready = sem("sum_ready")
        row_ready = sem("row_ready")
        stage_ready = sem("stage_ready"); msgs_done = sem("msgs_done")

        block = ctx.enter_context(nc.Block())
        unit = lambda t, k: t[0:P, k, :]

        BOOT = 0
        @block.sync
        def _(sp):
            n = [0]
            def load(to, frm, **kw):
                sp.dma_start(to, frm, **kw).then_inc(boot_dma, 16)
                n[0] += 1
            def index_load(of, b, j, done):
                if done is not None:
                    sp.wait_ge(ring_dma[j], done)
                rows = of.rearrange("(b p j s) -> b p j s", b=NB, p=P, j=NJ)
                sp.dma_start(index[0:P, j, :], rows[b, :, j, :] if isinstance(b, int) else rows[bass.ds(b, 1), :, j, :]).then_inc(index_in[j], 16)
            for j in range(NJ):
                index_load(src, 0, j, None)
            load(dst_i[0:P, :].rearrange("p (b s) -> p b s", b=NB), edge_slots(dst))
            load(attr[0:P, :].rearrange("p (b s) -> p b s", b=NB), edge_attr.rearrange("(b p s) a -> p b (s a)", b=NB, p=P))
            for j in range(NJ):
                sp.dma_start(nodes[0:P, j, :], x_rows[:, j * 2 * W:(j + 1) * 2 * W]).then_inc(nodes_in[j], 16)
            sp.wait_ge(boot_pool, 3)
            sp.wait_ge(boot_dve, 1)
            for t in range(4):
                q = slice(t * F, (t + 1) * F)
                load(w0_bd[q, :].rearrange("f (k t o) -> f k t o", k=KS, t=4)[:, :, t, :], w0.rearrange("k f o -> f k o"))
                load(root_bd[q, q], root_w)
                load(gat[q, :], w_gat)
                load(w1_q[q, t, :], w1)
                load(cols[q, 1:2], g1.rearrange("(f a) -> f a", a=1))
                load(cols[q, 2:3], be1.rearrange("(f a) -> f a", a=1))
            load(cols[:, 0:1], b1.rearrange("(f a) -> f a", a=1))
            load(w2_c[:, :], w2)
            for k, v in enumerate((att_src, att_dst)):
                load(att[:, k, :], v.rearrange("(a h) f -> a (h f)", a=1).to_broadcast([128, H * F]))
            for k, v in enumerate((g2, be2)):
                load((g2_b, be2_b)[k][0:P, :], v.rearrange("(a f) -> a f", a=1).to_broadcast([P, F]))
            for k, v in enumerate((bias_gat, b2)):
                load(bias_row[0:1, k, 0:F], v.rearrange("(a f) -> a f", a=1))
            load(nodes[P:P + 1, :, :].rearrange("a j (s f) -> a (j s) f", f=F),
                 root_b.rearrange("(a b f) -> a b f", a=1, b=1).to_broadcast([1, NJ * 2 * CE, F]))
            ends = dst.rearrange("(c s) -> s c", s=SE)
            load(row_i[0:1, 0:NB * P], ends[0:1, :], allow_slow_non_contiguous=True)
            load(row_i[0:1, NB * P:2 * NB * P], ends[SE - 1:SE, :], allow_slow_non_contiguous=True)
            first = ends[0, :].rearrange("(b p) -> p b", b=NB)
            load(next_i[0:P - 1, :], first[1:P, :], allow_slow_non_contiguous=True)
            load(next_i[P - 1:P, 0:NB - 1], first[0:1, 1:NB], allow_slow_non_contiguous=True)
            assert n[0] == N_BOOT, n[0]

            def a_chunk(b, j, more):
                c = b * NJ + j
                if more:
                    index_load(src, b + 1, j, (b + 1) * DMAS)
                sp.dma_start(spare_rows[bass.ds(c, 1), :, :].rearrange("a p w -> (a p) w"), stage[0:P, :]).then_inc(spare_zero, 16)
                sp.wait_ge(nodes_ready, c + 1)
                for to in (x1_rows, x1_plain):
                    sp.dma_start(to[:, bass.ds(c * 2 * W, 2 * W)], nodes[0:P, j, :]).then_inc(nodes_out[j], 16)
                if more:
                    sp.wait_ge(nodes_out[j], (b + 1) * 32)
                    sp.dma_start(nodes[0:P, j, :], x_rows[:, bass.ds((c + NJ) * 2 * W, 2 * W)]).then_inc(nodes_in[j], 16)
            with sp.Fori(0, NB - 1) as b:
                for j in range(NJ):
                    a_chunk(b, j, True)
            for j in range(NJ):
                a_chunk(NB - 1, j, False)
            for j in range(NJ):
                sp.wait_ge(nodes_out[j], NB * 32)

            def node_load(u, i):
                sp.dma_start(nodes[0:P, i, 0:W], x1_plain[:, bass.ds(u * W, W)]).then_inc(nodes_in[i], 16)

            def node_store(u, i, ready):
                sp.wait_ge(nodes_ready, ready)
                sp.dma_start(out_rows[:, bass.ds(u * W, W)], nodes[0:P, i, 0:W]).then_inc(nodes_out[i], 16)

            stored = [NB * 32] * NJ
            finished = NC

            stored, finished, before = {}, {}, None
            for name in "CBD":
                last = UNITS.get(before, 0)
                stored[name] = [(stored[before][i] if before else NB * 32) + (16 * NB if i < last else 0) for i in range(NJ)]
                finished[name] = (finished[before] if before else NC) + NB * last
                before = name

            def unit_turn(name, b, i):
                n = UNITS[name]
                following = {"C": "B", "B": "D"}.get(name) if isinstance(b, int) and b == NB - 1 else name
                node_store(FIRST[name] + b * n + i, i, finished[name] + b * n + i + 1)
                if following and i < UNITS[following]:
                    sp.wait_ge(nodes_out[i], stored[name][i] + (b + 1) * 16)
                    node_load(FIRST[name] + (b + 1) * n + i if following == name else FIRST[following] + i, i)

            def base_save(c, j):
                sp.wait_ge(base_ready, c + 1)
                sp.dma_start(base_dst[bass.ds(c, 1), :, :].rearrange("a p w -> (a p) w"), nodes[0:P, j, W:2 * W]).then_inc(ring_saved[j], 16)

            def wave_moves(name, b, w, wave):
                if name == "B":
                    more = not isinstance(b, int) or b < NB - 1
                    index_load(dst if more else src, b + 1 if more else 0, w, (2 * NB + b + 1) * DMAS)
                    sp.dma_start(x1_dst[bass.ds(b * NJ + w, 1), :, :].rearrange("a p w -> (a p) w"), ring[0:P, w, :]).then_inc(ring_saved[w], 16)
                if name == "D" and (not isinstance(b, int) or b < NB - 1):
                    index_load(src, b + 1, w, (3 * NB + 1 + b) * DMAS)
                for part in ("e2", "n3"):
                    if part in wave:
                        owner, j, back = wave[part]
                        at = NB - 1 if owner != name else b - 1 if back else b
                        if part == "n3":
                            unit_turn(owner, at, j)
                        elif owner == "B":
                            base_save(at * NJ + j, j)

            for j in range(NJ):
                index_load(dst, 0, j, NB * DMAS)
            for i in range(UNITS["C"]):
                node_load(i, i)
            before = None
            for name in "CBD":
                for w, wave in enumerate(waves(name, before)):
                    wave_moves(name, 0, w, wave)
                with sp.Fori(0, NB - 2) as b:
                    for w, wave in enumerate(waves(name, name)):
                        wave_moves(name, b + 1, w, wave)
                for w, wave in enumerate(waves(name, name)):
                    wave_moves(name, NB - 1, w, wave)
                before = name
            for w, wave in enumerate(waves(None, "D")):
                wave_moves(None, None, w, wave)

            def e_load(c, j):
                sp.dma_start(nodes[0:P, j, 0:W], x1_dst[bass.ds(c, 1), :, :].rearrange("a p w -> (a p) w")).then_inc(nodes_in[j], 16)
                sp.dma_start(nodes[0:P, j, W:2 * W], base_dst[bass.ds(c, 1), :, :].rearrange("a p w -> (a p) w")).then_inc(nodes_in[j], 16)
            for j in range(NJ):
                sp.wait_ge(nodes_out[j], OUT_DONE[j])
                sp.wait_ge(ring_saved[j], NB * 32)
            sp.wait_ge(softmax_done, 1)
            for j in range(NJ):
                e_load(j, j)
            with sp.Fori(0, NB - 1) as b:
                for j in range(NJ):
                    sp.wait_ge(rows_used, b * NJ + j + 1)
                    e_load((b + 1) * NJ + j, j)
            for j in range(NJ):
                sp.wait_ge(ring_dma[j], 5 * NB * DMAS)

        @block.gpsimd
        def _(pool):
            pool.memset(ident[:, :], 0.0).then_inc(boot_pe, 1)
            pool.memset(w0_bd[:, :], 0.0).then_inc(boot_pool, 1)
            pool.memset(root_bd[:, :], 0.0).then_inc(boot_pool, 1)
            pool.memset(w1_q[:, :, :], 0.0).then_inc(boot_pool, 1)
            pool.wait_ge(boot_pe, 1)
            pool.affine_select(out=ident[:, :], in_=ident[:, :], compare_op=ALU.not_equal, fill=1.0, base=0,
                               pattern=[[-1, 128]], channel_multiplier=1).then_inc(boot_pool, 1)
            pool.wait_ge(boot_pool, 4)
            pool.affine_select(out=ident_bias[:, :], in_=ident[:, :], compare_op=ALU.is_gt, fill=1.0, base=P,
                               pattern=[[0, 128]], channel_multiplier=-1).then_inc(boot_pool, 1)
            pool.iota(scatter_to[:, :], pattern=[[P * SE, NB], [1, SE]], base=N, channel_multiplier=SE).then_inc(boot_pool, 1)

            def gather(table, rows, j):
                pool.sem_inc(cleared, 1)
                for s in range(CE):
                    pool.indirect_dma_start(
                        out=ring[0:P, j, s * F:(s + 1) * F], out_offset=None, in_=table[:, :],
                        in_offset=bass.IndirectOffsetOnAxis(ap=index[0:P, j, s:s + 1], axis=0)).then_inc(ring_dma[j], 16)

            def gather_phase(table, rows, phase, used, saved=False):
                with pool.Fori(0, NB) as b:
                    for j in range(NJ):
                        pool.wait_ge(index_in[j], 16 * NB * phase + 16 * (b + 1))
                        pool.wait_ge(ring_used, NC * used + b * NJ + j + 1)
                        gather(table, rows, j)

            gather_phase(x, N, 0, 0)
            for j in range(NJ):
                pool.wait_ge(nodes_out[j], NB * 32)
            pool.wait_ge(spare_zero, NC * 16)
            with pool.Fori(0, NB) as b:
                for j in range(NJ):
                    pool.wait_ge(ring_filled, b * NJ + j + 1)
                    pool.sem_inc(cleared, 1)
                    for s in range(CE):
                        pool.indirect_dma_start(
                            out=x1_table[:, :], out_offset=bass.IndirectOffsetOnAxis(ap=index_out[0:P, j, s:s + 1], axis=0),
                            in_=ring[0:P, j, s * F:(s + 1) * F], in_offset=None, compute_op=ALU.add).then_inc(ring_dma[j], 16)
            for j in range(NJ):
                pool.wait_ge(ring_dma[j], 2 * NB * DMAS)
            def b_block(b):
                for j in range(NJ):
                    pool.wait_ge(index_in[j], 16 * NB + 16 * (b + 1))
                    pool.wait_ge(ring_used, NC + b * NJ + j + 1)
                    if not isinstance(b, int):
                        pool.wait_ge(ring_saved[j], 32 * b)
                    gather(x1_table, N + E, j)
            b_block(0)
            with pool.Fori(1, NB) as b:
                b_block(b)
            with pool.Fori(0, NB) as b:
                for j in range(NJ):
                    pool.wait_ge(index_in[j], 16 * NB * 2 + 16 * (b + 1))
                    pool.wait_ge(ring_used, 2 * NC + b * NJ + j + 1)
                    pool.wait_ge(ring_saved[j], 32 * NB)
                    gather(x1_table, N + E, j)
            for j in range(NJ):
                pool.wait_ge(nodes_out[j], OUT_DONE[j])
            last_row = pool.to_reg(N - 1)
            with pool.Fori(0, NB) as b:
                for j in range(NJ):
                    pool.wait_ge(ring_filled, NC + b * NJ + j + 1)
                    pool.sem_inc(cleared, 1)
                    for s in range(CE):
                        pool.indirect_dma_start(
                            out=out[:, :], out_offset=bass.IndirectOffsetOnAxis(ap=index_out[0:P, j, s:s + 1], axis=0),
                            in_=ring[0:P, j, s * F:(s + 1) * F], in_offset=None,
                            bounds_check=last_row, oob_is_err=False).then_inc(ring_dma[j], 16)

        @block.tensor
        def _(pe):
            tq, cq, vq, fq = Uses(2), Uses(2), Uses(4), Uses(4)
            mm = nc.tensor.matmul
            pe.sem_inc(ring_used, NJ)

            def transpose(rows, then=None):
                at, bank = tq.next()
                pe.wait_ge(t_done, tq.room)
                for g in range(G):
                    i = nc.tensor.transpose(T[bank][:, g * P:(g + 1) * P], rows[:, g * GF:(g + 1) * GF], ident[0:P, 0:P])
                    i.then_inc(t_ready, 1) if g == G - 1 else None
                return at

            def product(cols_T, right, n=GF, bias=None, t_at=None, frees=None):
                at, bank = cq.next()
                pe.wait_ge(c_done, cq.room)
                if t_at is not None:
                    pe.wait_ge(t_done, t_at + 1 + CREDIT)
                if bias is not None:
                    mm(C[bank][0:P, :], ones[:, 0:P], bias_row[:, bias, :], start=True, stop=True, skip_group_check=True)
                for g in range(G):
                    i = mm(C[bank][0:P, g * n:(g + 1) * n], cols_T[:, g * P:(g + 1) * P], right,
                           start=bias is None, stop=True, skip_group_check=True)
                    if g == 0 and frees is not None:
                        i.then_inc(frees, 1)
                i.then_inc(c_ready, 1)
                return at

            pe.wait_ge(boot_pool, 6)
            pe.wait_ge(boot_dma, 16 * N_BOOT)
            pe.wait_ge(boot_dve, 2)
            nc.tensor.transpose(T[0][:, 0:GF], root_bd[:, :], ident[:, :]).then_inc(boot_pe, 1)
            for m in range(2):
                for q, (lo, hi) in enumerate(((0, 4 * P), (4 * P, NB * P))):
                    mm(V[2 * m + q][0:33, 0:hi - lo], ones[0:1, 0:33], row_s[0:1, m * NB * P + lo:m * NB * P + hi],
                       start=True, stop=True).then_inc(boot_pe, 1)
            pe.wait_ge(boot_dve, 4)
            pe.wait_ge(t_done, CREDIT)

            def hidden(nT):
                for t in range(4):
                    at, bank = fq.next()
                    pe.wait_ge(f_done, fq.room)
                    mm(V[4 - fq.depth + bank][:, 0:WT], w1_q[:, t, :], nT, start=True, stop=True).then_inc(f_ready, 1)

            def back(nT):
                at, bank = cq.next()
                pe.wait_ge(c_done, cq.room)
                mm(C[bank][0:P, :], ones[:, 0:P], bias_row[:, 1, :], start=True, stop=True, skip_group_check=True)
                for g in range(G):
                    mm(C[bank][0:P, g * GF:(g + 1) * GF], nT[:, g * P:(g + 1) * P], center[:, :], start=False, stop=True, skip_group_check=True)
                for t in range(4):
                    pe.wait_ge(f_done, fq.at - 3 + t + 1 + CREDIT)
                    for g in range(G):
                        i = mm(C[bank][0:P, (4 * g + t) * F:(4 * g + t + 1) * F], hid[:, t, g * P:(g + 1) * P], w2_c[:, :],
                               start=False, stop=True, skip_group_check=True)
                i.then_inc(c_ready, 1)

            def carries(m):
                at, bank = tq.next()
                pe.wait_ge(t_done, tq.room)
                pe.wait_ge(tails_ready, m + 1)
                nc.tensor.transpose(T[bank][:, 0:P], tails[0:P, 0:128], ident[0:P, 0:P]).then_inc(t_ready, 1)
                at, bank = tq.next()
                pe.wait_ge(t_done, tq.room)
                pe.wait_ge(carry_ready, m + 1)
                nc.tensor.transpose(T[bank][0:P, 0:128], carry_row[:, :], ident[:, :]).then_inc(t_ready, 1)

            def to_T(cols_T, right, t_at, bias=None, plus=None):
                at, bank = tq.next()
                pe.wait_ge(t_done, tq.room)
                pe.wait_ge(t_done, t_at + 1 + CREDIT)
                if plus is not None:
                    mm(T[bank][0:P, :], ident_bias[0:P + 1, 0:P], plus, start=True, stop=True, skip_group_check=True)
                else:
                    mm(T[bank][0:P, :], ones[:, 0:P], bias_row[:, bias, :], start=True, stop=True, skip_group_check=True)
                for g in range(G):
                    i = mm(T[bank][0:P, g * GF:(g + 1) * GF], cols_T[:, g * P:(g + 1) * P], right, start=False, stop=True, skip_group_check=True)
                i.then_inc(t_ready, 1)

            def values(j, g):
                for q in range(3):
                    at, bank = vq.next()
                    pe.wait_ge(v_done, vq.room)
                    mm(V[bank][0:P, 0:3 * GF], hT[:, HE[j], g * P:(g + 1) * P], w0_bd[:, q * 3 * GF:(q + 1) * 3 * GF],
                       start=True, stop=True).then_inc(v_ready, 1)

            st_t, st = {}, {}
            def a_wave(jx, jh, jv, b):
                h, old = {}, st_t.get("h0")
                def rows_T(k):
                    if jh is not None:
                        pe.wait_ge(c_done, st[k] + 1 + CREDIT)
                        h[k] = transpose(unit(hrow, k))
                def center_rows(k):
                    if jx is not None:
                        if k == 0:
                            pe.wait_ge(ring_dma[jx], (b + 1) * DMAS)
                        if k == 1:
                            pe.wait_ge(nodes_in[jx], (b + 1) * 16)
                        t = transpose(unit(ring, jx) if k == 0 else nodes[0:P, jx, (k - 1) * W:k * W])
                        return t
                def centred(k, t):
                    if jx is not None:
                        st[k] = product(xT[:, k, :], center[:, :], t_at=t, frees=ring_used if k == 0 else None)
                def dense(k):
                    if jh is not None:
                        to_T(hT[:, k, :], root_bd[:, :], h[k], plus=nodes[0:P + 1, jh, (k - 1) * W:k * W])
                def weigh(g):
                    if jv is not None:
                        if g == 0:
                            pe.wait_ge(t_done, old + 1 + CREDIT)
                        values(jv, g)
                rows_T(0); rows_T(1)
                weigh(0)
                rows_T(2); t = center_rows(0)
                centred(0, t); dense(1)
                weigh(1)
                t = center_rows(1); centred(1, t)
                dense(2); t = center_rows(2)
                weigh(2)
                centred(2, t)
                weigh(3)
                if jh is not None:
                    st_t["h0"] = h[0]
            def a_block(b, first, last=False):
                for w in range(2 if last else NJ):
                    a_wave(None if last else w, None if first and w == 0 or last and w == 1 else (w - 1) % NJ,
                           None if first and w < 2 else (w - 2) % NJ, b)
            tq.restart(); cq.restart()
            a_block(0, True)
            tq.restart(); cq.restart(); vq.restart()
            lag_t, lags = tq.base - st_t["h0"], {k: cq.base - at for k, at in st.items()}
            with pe.Fori(0, NB - 1) as b:
                tq.loop(b, 8 * NJ); cq.loop(b, 3 * NJ); vq.loop(b, 12 * NJ)
                st_t["h0"] = tq.base - lag_t; st.update({k: cq.base - lag for k, lag in lags.items()})
                a_block(b + 1, False)
                tq.end(NB - 1, 8 * NJ); cq.end(NB - 1, 3 * NJ); vq.end(NB - 1, 12 * NJ)
            st_t["h0"] = tq.base - lag_t; st.update({k: cq.base - lag for k, lag in lags.items()})
            a_block(None, False, True)
            st.clear()

            def joins(m, n, tail_cols, carries_in):
                for half in (0, 1):
                    pe.wait_ge((tails_ready, carry_ready)[half], m + 1)
                    for bb in range(NB):
                        at, bank = tq.next()
                        pe.wait_ge(t_done, tq.room)
                        if half == 0:
                            nc.tensor.transpose(T[bank][0:n, 0:P], tail_cols[0:P, bb * n:(bb + 1) * n], ident[0:P, 0:P]).then_inc(t_ready, 1)
                        else:
                            nc.tensor.transpose(T[bank][0:P, 0:n], carries_in[:, bb * P:(bb + 1) * P], ident[0:n, 0:n]).then_inc(t_ready, 1)
            tq.restart()
            joins(0, F + 1, tails, a_carry)

            def wave_products(wave, loaded, gathered):
                t = {}
                if "n3" in wave:
                    pe.wait_ge(c_done, st["n2"] + 1 + CREDIT)
                    t["n3"] = transpose(unit(hrow, 2))
                if "n2" in wave:
                    pe.wait_ge(c_done, st["n1"] + 1 + CREDIT)
                    t["n2"] = transpose(unit(hrow, 1))
                if "n3" in wave:
                    pe.wait_ge(t_done, t["n3"] + 1 + CREDIT)
                    hidden(xT[:, 2, :])
                if "n2" in wave:
                    st["n2"] = product(hT[:, 1, :], base_bd[:, :], bias=0, t_at=t["n2"])
                if "n1" in wave:
                    pe.wait_ge(nodes_in[wave["n1"][1]], loaded(wave["n1"]))
                    t["n1"] = transpose(nodes[0:P, wave["n1"][1], 0:W])
                if "e2" in wave:
                    pe.wait_ge(c_done, st["e1"] + 1 + CREDIT)
                    t["e2"] = transpose(unit(hrow, 0))
                if "n1" in wave:
                    st["n1"] = product(xT[:, 1, :], center[:, :], t_at=t["n1"])
                if "n3" in wave:
                    back(xT[:, 2, :])
                if "e2" in wave and wave["e2"][0] == "B":
                    to_T(hT[:, 0, :], base_bd[:, :], bias=0, t_at=t["e2"])
                    product(hT[:, 0, :], att_bd[:, :, :].rearrange("f t h -> f (t h)"), n=8 * H)
                elif "e2" in wave:
                    product(hT[:, 0, :], src_bd[:, :, :].rearrange("f t h -> f (t h)"), n=4 * H, t_at=t["e2"])
                if "e1" in wave:
                    pe.wait_ge(ring_dma[wave["e1"][1]], gathered)
                    t["e1"] = transpose(unit(ring, wave["e1"][1]))
                    st["e1"] = product(xT[:, 0, :], center[:, :], t_at=t["e1"], frees=ring_used)

            pe.wait_ge(v_done, 12 * NC + CREDIT)
            loads = [NB * 16] * NJ
            def wave_block(name, before, b):
                for wave in waves(name, before):
                    wave_products(wave, lambda unit_of: loads[unit_of[1]] + (b + 1) * 16,
                                  ({"B": 2, "D": 3}.get(name, 0) * NB + b + 1) * DMAS)
            before = None
            for name in "CBD":
                per = PER[name]
                tq.restart(); cq.restart(); fq.restart()
                wave_block(name, before, 0)
                lags = {k: cq.base + cq.n - at for k, at in st.items()}
                with pe.Fori(0, NB - 1) as b:
                    tq.loop(b, per["t"]); cq.loop(b, per["c"]); fq.loop(b, per["f"])
                    for k, lag in lags.items():
                        st[k] = cq.base - lag
                    wave_block(name, name, b + 1)
                    tq.end(NB - 1, per["t"]); cq.end(NB - 1, per["c"]); fq.end(NB - 1, per["f"])
                for k, lag in lags.items():
                    st[k] = cq.base - lag
                for i in range(UNITS[name]):
                    loads[i] += NB * 16
                before = name
            for wave in waves(None, "D"):
                wave_products(wave, None, None)

            tq.restart()
            for m in range(4):
                joins(1 + m, H, tails, s_carry)

            tq.restart(); cq.restart(); vq.restart()
            vq.depth = 2; fq.depth = 2; fq.restart()
            pe.wait_ge(f_done, 4 * sum(UNITS.values()) * NB + CREDIT)
            def x1_stage(staged, js):
                pe.wait_ge(stage_ready, staged)
                t = transpose(stage[0:P, :])
                pe.wait_ge(t_done, t + 1 + CREDIT)
            def x_values(groups):
                for g in groups:
                    for q in range(2):
                        at, bank = vq.next()
                        pe.wait_ge(v_done, vq.room)
                        mm(V[bank][0:P, :], hT[:, 0, g * P:(g + 1) * P], gat_bd[:, q * 512:(q + 1) * 512],
                           start=True, stop=True).then_inc(v_ready, 1)
            def y_stage(j, ready):
                pe.wait_ge(row_ready, ready)
                t = transpose(unit(hrow, NORMED[j % 2]))
                pe.wait_ge(t_done, t + 1 + CREDIT)
                hidden(xT[:, 2, :])
                back(xT[:, 2, :])
            def e_block(x_block, y_block):
                for j in range(NJ + 1):
                    x = x_block is not None and j < NJ
                    y = y_block is not None and j > 0
                    if x:
                        x1_stage(x_block * NJ + j + 1, None)
                        x_values((0, 1))
                    if y:
                        y_stage(j - 1, y_block * NJ + j)
                    if x:
                        x_values((2, 3))
                if x_block is not None:
                    carries(1 + 4 + x_block)
            e_block(0, None)
            tq.restart(); cq.restart(); vq.restart(); fq.restart()
            with pe.Fori(0, NB - 1) as b:
                tq.loop(b, 2 * NJ + 2); cq.loop(b, NJ); vq.loop(b, 8 * NJ); fq.loop(b, 4 * NJ)
                e_block(b + 1, b)
                tq.end(NB - 1, 2 * NJ + 2); cq.end(NB - 1, NJ); vq.end(NB - 1, 8 * NJ); fq.end(NB - 1, 4 * NJ)
            e_block(None, NB - 1)

        @block.scalar
        def _(act):
            tq, cq, fq, nq = Uses(2), Uses(2), Uses(4), Uses()
            act.sem_inc(t_done, CREDIT)
            act.sem_inc(f_done, CREDIT)
            act.wait_ge(boot_dve, 4)

            def evac(to, rows=128, width=WT, func=ACT.Copy, **kw):
                at, bank = tq.next()
                act.wait_ge(t_ready, at + 1)
                nc.scalar.activation(to, T[bank][0:rows, 0:width], func, **kw).then_inc(t_done, 1)

            def square(k, rows=None):
                if rows is None:
                    at, bank = cq.next()
                    act.wait_ge(c_ready, at + 1)
                    rows = C[bank][0:P, :]
                nc.scalar.activation(unit(sq, k), rows, ACT.Square).then_inc(sq_ready, 1)

            def root(k):
                at, _ = nq.next()
                act.wait_ge(var_ready, at + 1)
                nc.scalar.activation(unit(std, k), unit(var, k), ACT.Sqrt, scale=1.0 / F, bias=cols[0:P, 3:4]).then_inc(std_ready, 1)

            def hidden():
                for t in range(4):
                    at, bank = fq.next()
                    act.wait_ge(f_ready, at + 1)
                    nc.scalar.activation(hid[:, t, :], V[4 - fq.depth + bank][:, 0:WT], ACT.Relu, bias=cols[:, 0:1]).then_inc(f_done, 1)

            def affine():
                evac(xT[:, 2, :], func=ACT.Identity, scale=cols[:, 1:2], bias=cols[:, 2:3])

            def carries(n):
                evac(tails_row[0:n, 1:1 + P], rows=n, width=P)
                evac(carry[0:P, 0:n], rows=P, width=n)

            def a_wave(jx, jh):
                x, h = jx is not None, jh is not None
                if h:
                    evac(hT[:, HE[jh], :]); evac(hT[:, 1, :]); evac(hT[:, 2, :])
                if x: evac(xT[:, 0, :]); square(0)
                if h: evac(nodes[0:P, jh, 0:W], rows=P, width=W)
                if x: evac(xT[:, 1, :]); root(0); square(1)
                if h:
                    evac(nodes[0:P, jh, W:2 * W], rows=P, width=W)
                    act.wait_ge(t_done, tq.at + 1 + CREDIT)
                    act.sem_inc(nodes_ready, 1)
                if x: root(1); evac(xT[:, 2, :]); square(2); root(2)
            def a_block(first, last=False):
                for w in range(2 if last else NJ):
                    a_wave(None if last else w, None if first and w == 0 or last and w == 1 else (w - 1) % NJ)
            a_block(True)
            tq.restart(); cq.restart()
            with act.Fori(0, NB - 1) as b:
                tq.loop(b, 8 * NJ); cq.loop(b, 3 * NJ); nq.loop(b, 3 * NJ)
                a_block(False)
                tq.end(NB - 1, 8 * NJ); cq.end(NB - 1, 3 * NJ); nq.end(NB - 1, 3 * NJ)
            a_block(False, True)
            def joins(n, to_rows):
                for bb in range(NB):
                    evac(to_rows[:, 1 + bb * P:1 + (bb + 1) * P], rows=n, width=P)
                for bb in range(NB):
                    evac(carry[0:P, bb * n:(bb + 1) * n], rows=P, width=n)
            tq.restart()
            joins(F + 1, a_tails)

            def wave_block(name, before):
                for wave in waves(name, before):
                    if "n3" in wave: affine()
                    if "n2" in wave: evac(hT[:, 1, :])
                    if "n3" in wave: hidden()
                    if "n2" in wave: square(2)
                    if "n1" in wave: evac(xT[:, 1, :])
                    if "e2" in wave: evac(hT[:, 0, :])
                    if "n2" in wave: root(2)
                    if "n1" in wave: square(1); root(1)
                    if "n3" in wave: square(3)
                    if "e2" in wave:
                        if wave["e2"][0] == "B":
                            evac(nodes[0:P, wave["e2"][1], W:2 * W], rows=P, width=W)
                            act.wait_ge(t_done, tq.at + 1 + CREDIT)
                            act.sem_inc(base_ready, 1)
                        cq.next()
                    if "n3" in wave: root(3)
                    if "e1" in wave: evac(xT[:, 0, :]); square(0); root(0)
            before = None
            for name in "CBD":
                per = PER[name]
                tq.restart(); cq.restart(); fq.restart()
                wave_block(name, before)
                with act.Fori(0, NB - 1) as b:
                    tq.loop(b, per["t"]); cq.loop(b, per["c"]); fq.loop(b, per["f"]); nq.loop(b, per["n"])
                    wave_block(name, name)
                    tq.end(NB - 1, per["t"]); cq.end(NB - 1, per["c"]); fq.end(NB - 1, per["f"]); nq.end(NB - 1, per["n"])
                before = name
            wave_block(None, "D")

            tq.restart()
            for m in range(4):
                if m == 2:
                    act.wait_ge(exp_in, 1)
                    nc.scalar.activation(beta[0:P, :], beta[0:P, :], ACT.Exp).then_inc(exp_ready, 1)
                    nc.scalar.activation(self_logit[0:P, :], self_logit[0:P, :], ACT.Exp, scale=-1.0).then_inc(exp_ready, 1)
                joins(H, s_tails)
            tq.restart(); cq.restart(); fq.depth = 2; fq.restart()
            def e_block(x_block, y_block):
                for j in range(NJ + 1):
                    x = x_block is not None and j < NJ
                    if x:
                        c = x_block * NJ + j
                        part = diff[0:P, bass.ds(c * W, W)]
                        nc.scalar.activation(stage[0:P, :], part, ACT.Copy).then_inc(stage_ready, 1)
                        evac(hT[:, 0, :])
                    y1 = y_block is not None and j < NJ
                    y2 = y_block is not None and j > 0
                    if y1:
                        act.wait_ge(sum_ready, y_block * NJ + j + 1)
                        square(2, unit(hrow, 1))
                    if y2:
                        affine()
                    if y1:
                        root(2)
                    if y2:
                        hidden(); square(3); root(3)
                if x_block is not None:
                    carries(F)
            e_block(0, None)
            tq.restart(); cq.restart(); fq.restart()
            with act.Fori(0, NB - 1) as b:
                tq.loop(b, 2 * NJ + 2); cq.loop(b, NJ); fq.loop(b, 4 * NJ); nq.loop(b, 2 * NJ)
                e_block(b + 1, b)
                tq.end(NB - 1, 2 * NJ + 2); cq.end(NB - 1, NJ); fq.end(NB - 1, 4 * NJ); nq.end(NB - 1, 2 * NJ)
            e_block(None, NB - 1)

        @block.vector
        def _(dve):
            v = nc.vector
            steps = Uses()
            R = NB * P
            tq, cq, vq, nq, rq = Uses(2), Uses(2), Uses(4), Uses(), Uses(2)
            slots = lambda a: a.rearrange("p (s f) -> p s f", f=F)
            wide = lambda a: a.unsqueeze(2).to_broadcast([P, CE, F])

            def step(i):
                at, _ = steps.next()
                i.then_inc(dve_step, 1)
                dve.wait_ge(dve_step, at + 1)

            dve.sem_inc(c_done, CREDIT)
            dve.sem_inc(v_done, CREDIT)
            dve.sem_inc(msgs_done, CREDIT)
            for a, value in ((ones, 1.0), (gat_bd, 0.0), (center, 0.0), (att_bd, 0.0), (src_bd, 0.0), (bias_row, 0.0),
                             (stage, 0.0), (cont, 0.0), (cont_next, 0.0), (row_cont, 0.0), (row_pass, 0.0),
                             (row_pass_back, 0.0), (tails_row, 0.0), (carry_last, 0.0), (tails, 0.0), (carry_row, 0.0)):
                v.memset(a[:, :] if len(a.shape) == 2 else a[:, :, :], value)
            v.memset(next_i[:, :], -1).then_inc(boot_dve, 1)
            dve.wait_ge(boot_dve, 1)
            for t in range(4):
                q = slice(t * F, (t + 1) * F)
                i = v.memset(center[q, q], 1.0 / F)
            step(i)
            dve.wait_ge(boot_pool, 6)
            dve.wait_ge(boot_dma, 16 * N_BOOT)
            v.memset(cols[:, 3:4], EPS)
            step(v.tensor_tensor(center[:, :], ident[:, :], center[:, :], ALU.subtract))
            v.tensor_copy(row_s, row_i[0:1, :]).then_inc(boot_dve, 1)
            tmp = hrow[:, 0, 0:H * F]
            heads = lambda a: a.rearrange("p (h f) -> p h f", f=F)
            for k in range(2):
                step(v.tensor_tensor(tmp, gat[:, :], att[:, k, :], ALU.mult))
                step(v.tensor_reduce(att_vec[:, k * H:(k + 1) * H], heads(tmp), AX.X, ALU.add))
            for t in range(4):
                q = slice(t * F, (t + 1) * F)
                v.tensor_copy(att_bd[q, t, :], att_vec[q, :])
                v.tensor_copy(src_bd[q, t, :], att_vec[q, 0:H])
            mean = hrow[:, 1, 0:H]
            step(v.tensor_reduce(mean, heads(gat[:, :]), AX.X, ALU.add))
            step(v.tensor_scalar(mean, mean, 1.0 / F, None, ALU.mult))
            step(v.tensor_tensor(heads(tmp), heads(gat[:, :]), mean.unsqueeze(2).to_broadcast([128, H, F]), ALU.subtract))
            for t in range(4):
                q = slice(t * F, (t + 1) * F)
                i = v.tensor_scalar(gat_bd[q, :].rearrange("p (h t o) -> p h t o", h=H, t=4)[:, :, t, :], heads(hrow[q, 0, 0:H * F]),
                                    1.0 / H, None, ALU.mult)
            step(i)
            step(v.tensor_reduce(base_bd[:, :], gat_bd[:, :].rearrange("p (h c) -> p c h", h=H), AX.X, ALU.add))
            v.tensor_tensor(base_bd[:, :], base_bd[:, :], center[:, :], ALU.add)
            m1 = hrow[:, 2, 0:1]
            step(v.tensor_reduce(m1, w2_c[:, :], AX.X, ALU.add))
            step(v.tensor_scalar(m1, m1, 1.0 / F, None, ALU.mult))
            v.tensor_tensor(w2_c[:, :], w2_c[:, :], m1.to_broadcast([128, F]), ALU.subtract)
            for k in range(2):
                m2 = hrow[0:1, 2, 1 + k:2 + k]
                step(v.tensor_reduce(m2, bias_row[0:1, k, 0:F], AX.X, ALU.add))
                step(v.tensor_scalar(m2, m2, 1.0 / F, None, ALU.mult))
                step(v.tensor_tensor(bias_row[0:1, k, 0:F], bias_row[0:1, k, 0:F], m2.to_broadcast([1, F]), ALU.subtract))
            for k in range(2):
                i = v.tensor_copy(bias_row[0:1, k, F:W].rearrange("p (s f) -> p s f", f=F),
                                  bias_row[0:1, k, 0:F].unsqueeze(1).to_broadcast([1, CE - 1, F]))
            step(v.tensor_copy(dst_f[0:P, :], dst_i[0:P, :]))
            blocks = lambda a: a[0:P, :].rearrange("p (b s) -> p b s", b=NB)
            d = blocks(dst_f)
            same = (d[:, :, 1:SE], d[:, :, 0:SE - 1])
            v.tensor_tensor(blocks(cont)[:, :, 1:SE], *same, ALU.is_equal)
            v.tensor_tensor(blocks(cont_next)[:, :, 0:SE - 1], *same, ALU.is_equal)
            v.tensor_tensor(blocks(head), d, d[:, :, 0:1].to_broadcast([P, NB, SE]), ALU.is_equal)
            v.tensor_tensor(blocks(tail), d, d[:, :, SE - 1:SE].to_broadcast([P, NB, SE]), ALU.is_equal)
            nxt, on, spare = hrow[0:P, 0, 0:NB], hrow[0:P, 1, 0:TE], hrow[0:P, 2, 0:TE]
            v.tensor_copy(nxt, next_i[0:P, :])
            step(v.tensor_copy(spare, scatter_to[0:P, :]))
            step(v.tensor_copy(on, cont_next[0:P, :]))
            step(v.tensor_tensor(on.rearrange("p (b s) -> p b s", b=NB)[:, :, SE - 1], d[:, :, SE - 1], nxt, ALU.is_equal))
            step(v.tensor_tensor(spare, spare, dst_f[0:P, :], ALU.subtract))
            step(v.tensor_tensor(spare, spare, on, ALU.mult))
            step(v.tensor_tensor(spare, spare, dst_f[0:P, :], ALU.add))
            v.tensor_copy(scatter_to[0:P, :], spare)
            dve.wait_ge(boot_pe, 6)
            v.tensor_copy(root_bd[:, :], T[0][:, 0:GF])
            for m in range(2):
                v.tensor_copy(row_f[:, m * NB * P:m * NB * P + 4 * P], V[2 * m][0:33, 0:4 * P])
                i = v.tensor_copy(row_f[:, m * NB * P + 4 * P:(m + 1) * NB * P], V[2 * m + 1][0:33, 0:P])
            step(i)
            v.tensor_tensor(row_cont[:, 1:R], row_f[:, 1:R], row_f[:, R:2 * R - 1], ALU.is_equal)
            step(v.tensor_tensor(whole, row_f[:, 0:R], row_f[:, R:2 * R], ALU.is_equal))
            v.tensor_tensor(row_pass[:, 1:R], row_cont[:, 1:R], whole[:, 0:R - 1], ALU.mult)
            v.tensor_tensor(row_pass_back[:, 0:R - 1], row_cont[:, 1:R], whole[:, 1:R], ALU.mult)
            step(v.tensor_scalar(attr[0:P, :], attr[0:P, :], 1.0, 0.0, ALU.min, ALU.max))
            hat = hats[0:P, :].rearrange("p (a k t) -> p a k t", a=2, k=3)
            for a in range(2):
                for k in range(3):
                    u = attr[0:P, :].rearrange("p (t a) -> p a t", a=2)[:, a, :]
                    i = v.tensor_scalar(hat[:, a, k, :], u, 0.5 * k, None, ALU.subtract)
            step(i)
            step(v.scalar_tensor_tensor(out=hats[0:P, :], in0=hats[0:P, :], scalar=-1.0, in1=hats[0:P, :], op0=ALU.mult, op1=ALU.max))
            step(v.tensor_scalar(hats[0:P, :], hats[0:P, :], -2.0, 1.0, ALU.mult, ALU.add))
            step(v.tensor_scalar(hats[0:P, :], hats[0:P, :], 0.0, None, ALU.max))
            for k in range(KS):
                i = v.tensor_tensor(basis[0:P, :].rearrange("p (g k t) -> p g k t", k=KS, t=4)[:, :, k, :],
                                    hat[:, 0, k // 3, :].rearrange("p (g t) -> p g t", t=4),
                                    hat[:, 1, k % 3, :].rearrange("p (g t) -> p g t", t=4), ALU.mult)
            step(i)
            v.memset(var[:, :, :], 0.0).then_inc(boot_dve, 2)

            def spread(k):
                at, _ = nq.next()
                dve.wait_ge(sq_ready, at + 1)
                v.tensor_reduce(unit(var, k), slots(unit(sq, k)), AX.X, ALU.add).then_inc(var_ready, 1)
                return at

            def scale_of(k, at):
                dve.wait_ge(std_ready, at + 1)
                step(v.reciprocal(unit(rstd, k), unit(std, k)))

            def bank_ready():
                at, bank = cq.next()
                dve.wait_ge(c_ready, at + 1)
                return at, C[bank][0:P, :]

            def relu_rows(k, at):
                _, rows = bank_ready()
                scale_of(k, at)
                v.scalar_tensor_tensor(out=slots(unit(hrow, k)), in0=slots(rows), scalar=0.0, in1=wide(unit(rstd, k)),
                                       op0=ALU.max, op1=ALU.mult).then_inc(c_done, 1)

            def rows_over_std(k, at):
                at_c, rows = bank_ready()
                scale_of(k, at)
                v.tensor_tensor(slots(unit(hrow, k)), slots(rows), wide(unit(rstd, k)), ALU.mult).then_inc(c_done, 1)
                return at_c

            def scan_block(rows, b):
                here = bass.ds(b * SE, SE)
                feature = rows[0:P, :].rearrange("p (t f) -> p t f", f=F)
                dve.wait_ge(msgs_done, rq.at + 1 + CREDIT)
                for f in range(F):
                    i = v.tensor_tensor_scan(feature[:, here, f], cont[0:P, here], feature[:, here, f], 0.0, ALU.mult, ALU.add)
                step(i)
                return feature

            def scans_and_carry(rows, b):
                here = bass.ds(b * SE, SE)
                feature = scan_block(rows, b)
                last = bass.ds(b * SE + SE - 1, 1)
                v.tensor_copy(tails[0:P, 0:F].rearrange("p (a f) -> p a f", a=1), feature[:, last, :]).then_inc(tails_ready, 1)
                at, _ = tq.next()
                dve.wait_ge(t_done, at + 1 + CREDIT)
                step(v.tensor_tensor(carry_in[0:F, :], tails_row[0:F, 0:P], row_cont[0:F, bass.ds(b * P, P)], ALU.mult))
                v.tensor_tensor_scan(carry_row[0:F, :], row_pass[0:F, bass.ds(b * P, P)], carry_in[0:F, :], carry_last[0:F, 0:1],
                                     ALU.mult, ALU.add).then_inc(carry_ready, 1)
                at, _ = tq.next()
                dve.wait_ge(t_done, at + 1 + CREDIT)
                v.tensor_copy(tails_row[0:F, 0:1], tails_row[0:F, P:P + 1])
                v.tensor_copy(carry_last[0:F, :], carry_row[0:F, P - 1:P])
                for f in range(F):
                    i = v.scalar_tensor_tensor(out=feature[:, here, f], in0=head[0:P, here], scalar=carry[0:P, f:f + 1],
                                               in1=feature[:, here, f], op0=ALU.mult, op1=ALU.add)
                step(i)

            def join_rows(tails_in, joined_in, out_rows_, n, op, forward=True):
                for _ in range(NB):
                    at, _ = tq.next()
                dve.wait_ge(t_done, at + 1 + CREDIT)
                if forward:
                    step(v.tensor_tensor(joined_in, tails_in[:, 0:R], row_cont[0:n, :], ALU.mult))
                    v.tensor_tensor_scan(out_rows_, row_pass[0:n, :], joined_in, 0.0, ALU.mult, op).then_inc(carry_ready, 1)
                else:
                    v.memset(joined_in[:, R - 1:R], 0.0)
                    step(v.tensor_tensor(joined_in[:, 0:R - 1], tails_in[:, 2:R + 1], row_cont[0:n, 1:R], ALU.mult))
                    v.tensor_tensor_scan(out_rows_[:, ::-1], row_pass_back[0:n, ::-1], joined_in[:, ::-1], 0.0, ALU.mult, op).then_inc(carry_ready, 1)
                for _ in range(NB):
                    at, _ = tq.next()
                dve.wait_ge(t_done, at + 1 + CREDIT)

            def a_wave(x, cv):
                pending = []
                def products_of(g):
                    rq.next()
                    dve.wait_ge(msgs_done, rq.room)
                    for q in range(3):
                        at, bank = vq.next()
                        dve.wait_ge(v_ready, at + 1)
                        to = (g % 2) * KS * GF + q * 3 * GF
                        v.tensor_tensor(products[0:P, to:to + 3 * GF].rearrange("p (k o) -> p k o", o=F),
                                        V[bank][0:P, 0:3 * GF].rearrange("p (k o) -> p k o", o=F),
                                        basis[0:P, bass.ds((cv * G + g) * 4 * KS + q * 12, 12)].unsqueeze(2).to_broadcast([P, 12, F]),
                                        ALU.mult).then_inc(v_done, 1)
                    pending.append((g, at))
                def sum_of():
                    g, at = pending.pop(0)
                    dve.wait_ge(v_done, at + 1 + CREDIT)
                    v.tensor_reduce(msgs[0:P, bass.ds(cv * W + g * GF, GF)],
                                    products[0:P, (g % 2) * KS * GF:(g % 2 + 1) * KS * GF].rearrange("p (k c) -> p c k", k=KS),
                                    AX.X, ALU.add).then_inc(msgs_done, 1)
                back = cv is not None
                if back: products_of(0)
                if x: at = spread(0)
                if back: products_of(1); sum_of()
                if x: relu_rows(0, at); at = spread(1)
                if back: products_of(2); sum_of()
                if x: relu_rows(1, at)
                if back: products_of(3); sum_of()
                if x: at = spread(2)
                if back: sum_of()
                if x: relu_rows(2, at)

            def a_block(b, first, last=False):
                for w in range(2 if last else NJ):
                    a_wave(not last, None if first and w < 2 else b * NJ + w - 2)
                    if w == 1 and not first:
                        scan_block(msgs, b - 1)
            a_block(0, True)
            cq.restart(); vq.restart(); rq.restart()
            with dve.Fori(0, NB - 1) as b:
                cq.loop(b, 3 * NJ); vq.loop(b, 12 * NJ); nq.loop(b, 3 * NJ); rq.loop(b, 4 * NJ); steps.loop(b, 3 * NJ + 1)
                a_block(b + 1, False)
                cq.end(NB - 1, 3 * NJ); vq.end(NB - 1, 12 * NJ); nq.end(NB - 1, 3 * NJ); rq.end(NB - 1, 4 * NJ)
                steps.end(NB - 1, 3 * NJ + 1)
            a_block(NB, False, True)
            by_block = lambda a: a[0:P, :].rearrange("p (b s) -> p b s", b=NB)
            block_carry = carry[0:P, :].rearrange("p (b f) -> p b f", f=F + 1)
            v.tensor_copy(tails[0:P, :].rearrange("p (b f) -> p b f", f=F + 1)[:, :, 0:F],
                          msgs[0:P, :].rearrange("p (b s f) -> p b s f", b=NB, f=F)[:, :, SE - 1, :])
            step(v.tensor_tensor_scan(degree[0:P, :], cont[0:P, :], ones[0:P, 0:1].to_broadcast([P, TE]), 0.0, ALU.mult, ALU.add))
            v.memset(a_tails[:, 0:1], 0.0)
            v.tensor_copy(tails[0:P, :].rearrange("p (b f) -> p b f", f=F + 1)[:, :, F], by_block(degree)[:, :, SE - 1]).then_inc(tails_ready, 1)
            tq.base += 8 * NC
            join_rows(a_tails, a_in, a_carry, F + 1, ALU.add)
            masked_degree = hrow[0:P, 0, 0:TE]
            step(v.tensor_tensor(masked_degree.rearrange("p (b s) -> p b s", b=NB), by_block(head),
                                 block_carry[:, :, F:F + 1].to_broadcast([P, NB, SE]), ALU.mult))
            step(v.tensor_tensor(degree[0:P, :], degree[0:P, :], masked_degree, ALU.add))
            step(v.tensor_scalar(degree[0:P, :], degree[0:P, :], 1.0, None, ALU.max))
            step(v.reciprocal(degree[0:P, :], degree[0:P, :]))

            def finish_rows(x1_part, to, at, signal):
                v.tensor_tensor(slots(x1_part), slots(x1_part), be2_b[0:P, :].unsqueeze(1).to_broadcast([P, CE, F]), ALU.add)
                at_c = rows_over_std(3, at)
                dve.wait_ge(c_done, at_c + 1 + CREDIT)
                step(v.tensor_tensor(slots(unit(hrow, 3)), slots(unit(hrow, 3)), g2_b[0:P, :].unsqueeze(1).to_broadcast([P, CE, F]), ALU.mult))
                v.tensor_tensor(to, x1_part, unit(hrow, 3), ALU.add).then_inc(signal, 1)

            heads_of = lambda a: a[0:P, :].rearrange("p (h t) -> p h t", h=H)
            def logits_dst(c):
                now = bass.ds(c * CE, CE)
                v.tensor_copy(diff[0:P, bass.ds(c * W, W)], unit(hrow, 0))
                _, rows = bank_ready()
                logits = rows[:, 0:2 * H * CE].rearrange("p (s h) -> p h s", h=2 * H)
                step(v.tensor_copy(heads_of(beta)[:, :, now], logits[:, H:2 * H, :]))
                own = heads_of(self_logit)[:, :, now]
                v.tensor_tensor(own, logits[:, 0:H, :], heads_of(beta)[:, :, now], ALU.add).then_inc(c_done, 1)
                dve.wait_ge(c_done, cq.at + 1 + CREDIT)
                step(v.scalar_tensor_tensor(out=own, in0=own, scalar=SLOPE, in1=own, op0=ALU.mult, op1=ALU.max))
            def logits_src(c):
                now = bass.ds(c * CE, CE)
                v.tensor_tensor(diff[0:P, bass.ds(c * W, W)], unit(hrow, 0), diff[0:P, bass.ds(c * W, W)], ALU.subtract)
                _, rows = bank_ready()
                bt = heads_of(beta)[:, :, now]
                v.tensor_tensor(bt, rows[:, 0:H * CE].rearrange("p (s h) -> p h s", h=H), bt, ALU.add).then_inc(c_done, 1)
                dve.wait_ge(c_done, cq.at + 1 + CREDIT)
                step(v.scalar_tensor_tensor(out=bt, in0=bt, scalar=SLOPE, in1=bt, op0=ALU.mult, op1=ALU.max))
                step(v.tensor_tensor(bt, bt, heads_of(self_logit)[:, :, now], ALU.subtract))
            st = {}
            def wave_rows(name, b, w, wave):
                if name == "C":
                    c = b * NJ + w
                    dve.wait_ge(ring_dma[w], NB * DMAS + b * DMAS)
                    to = ring[0:P, w, :]
                    step(v.tensor_tensor(slots(to), carry[0:P, bass.ds(b * (F + 1), F)].unsqueeze(1).to_broadcast([P, CE, F]),
                                         wide(head[0:P, bass.ds(c * CE, CE)]), ALU.mult))
                    step(v.tensor_tensor(to, to, msgs[0:P, bass.ds(c * W, W)], ALU.add))
                    v.tensor_tensor(slots(to), slots(to), wide(degree[0:P, bass.ds(c * CE, CE)]), ALU.mult)
                    v.tensor_copy(index_out[0:P, w, :], scatter_to[0:P, bass.ds(c * CE, CE)]).then_inc(ring_filled, 1)
                at = {}
                if "n2" in wave: at["n2"] = spread(2)
                if "n1" in wave: at["n1"] = spread(1)
                if "n2" in wave: rows_over_std(2, at["n2"])
                if "n1" in wave: relu_rows(1, at["n1"])
                if "n3" in wave:
                    i = wave["n3"][1]
                    finish_rows(nodes[0:P, i, 0:W], nodes[0:P, i, 0:W], spread(3), nodes_ready)
                if "e2" in wave:
                    phase, j, back = wave["e2"]
                    dve.wait_ge(c_done, st["h"] + 1 + CREDIT)
                    c = (NC if phase != name else b * NJ) + j - (NJ if back else 0)
                    (logits_dst if phase == "B" else logits_src)(c)
                if "e1" in wave:
                    relu_rows(0, spread(0))
                    st["h"] = cq.at
            before = None
            for name in "CBD":
                per = PER[name]
                tq.restart(); cq.restart()
                start = tq.base
                for w, wave in enumerate(waves(name, before)):
                    wave_rows(name, 0, w, wave)
                lag = cq.base + cq.n - st.get("h", 0)
                with dve.Fori(0, NB - 1) as b:
                    cq.loop(b, per["c"]); nq.loop(b, per["n"]); steps.loop(b, per["steps"])
                    st["h"] = cq.base - lag
                    for w, wave in enumerate(waves(name, name)):
                        wave_rows(name, b + 1, w, wave)
                    cq.end(NB - 1, per["c"]); nq.end(NB - 1, per["n"]); steps.end(NB - 1, per["steps"])
                st["h"] = cq.base - lag
                before = name
            for w, wave in enumerate(waves(None, "D")):
                wave_rows(None, None, w, wave)
            tq.base += NB * sum(per["t"] for per in PER.values())

            tq.restart()
            def join(a, forward, op):
                edge = SE - 1 if forward else 0
                v.tensor_copy(tails[0:P, 0:H * NB].rearrange("p (b h) -> p h b", h=H),
                              a[0:P, :].rearrange("p (h b s) -> p h b s", h=H, b=NB)[:, :, :, edge]).then_inc(tails_ready, 1)
                join_rows(s_tails, s_in, s_carry, H, op, forward)
                by = lambda x: x.rearrange("p (h b s) -> p h b s", h=H, b=NB)
                mask = (head if forward else tail)[0:P, :].rearrange("p (b s) -> p b s", b=NB).unsqueeze(1).to_broadcast([P, H, NB, SE])
                step(v.tensor_tensor(by(masked[0:P, :]), mask,
                                     carry[0:P, 0:H * NB].rearrange("p (b h) -> p h b", h=H).unsqueeze(3).to_broadcast([P, H, NB, SE]), ALU.mult))
                step(v.tensor_tensor(a[0:P, :], a[0:P, :], masked[0:P, :], op))

            def each_head(to, frm, op, forward=True):
                for h in range(H):
                    way = slice(None) if forward else slice(None, None, -1)
                    mask = (cont if forward else cont_next)[0:P, way]
                    i = v.tensor_tensor_scan(heads_of(to)[:, h, way], mask, heads_of(frm)[:, h, way], 0.0, ALU.mult, op)
                step(i)

            for j in range(2):
                dve.wait_ge(nodes_out[j], OUT_DONE[j])
                dve.wait_ge(ring_saved[j], NB * 32)
            v.memset(s_tails[:, 0:1], 0.0)
            each_head(self_logit, beta, ALU.max)
            join(self_logit, True, ALU.max)
            each_head(self_logit, self_logit, ALU.max, False)
            join(self_logit, False, ALU.max)
            step(v.tensor_tensor(beta[0:P, :], beta[0:P, :], self_logit[0:P, :], ALU.subtract))
            dve.sem_inc(exp_in, 1)
            dve.wait_ge(exp_ready, 2)
            each_head(denom, beta, ALU.add)
            join(denom, True, ALU.add)
            each_head(denom, denom, ALU.max, False)
            join(denom, False, ALU.max)
            step(v.scalar_tensor_tensor(out=denom[0:P, :], in0=self_logit[0:P, :], scalar=1e-16, in1=denom[0:P, :], op0=ALU.add, op1=ALU.add))
            step(v.reciprocal(denom[0:P, :], denom[0:P, :]))
            step(v.tensor_tensor(beta[0:P, :], beta[0:P, :], denom[0:P, :], ALU.mult))
            for a in (tails_row, carry_last):
                i = v.memset(a[:, :], 0.0)
            step(i)
            dve.sem_inc(softmax_done, 1)

            tq.restart(); cq.restart(); vq.restart(); vq.depth = 2; rq.restart()
            def x_products(c, g, pending):
                rq.next()
                dve.wait_ge(msgs_done, rq.room)
                for q in range(2):
                    at, bank = vq.next()
                    dve.wait_ge(v_ready, at + 1)
                    to = (g % 2) * H * GF + q * 512
                    v.tensor_tensor(weighted[0:P, to:to + 512].rearrange("p (h t o) -> p h t o", h=4, t=4),
                                    V[bank][0:P, :].rearrange("p (h t o) -> p h t o", h=4, t=4),
                                    heads_of(beta)[:, 4 * q:4 * q + 4, bass.ds(c * CE + 4 * g, 4)].unsqueeze(3).to_broadcast([P, 4, 4, F]),
                                    ALU.mult).then_inc(v_done, 1)
                pending.append((g, at))
            def x_sum(c, pending):
                g, at = pending.pop(0)
                dve.wait_ge(v_done, at + 1 + CREDIT)
                v.tensor_reduce(diff[0:P, bass.ds(c * W + g * GF, GF)],
                                weighted[0:P, (g % 2) * H * GF:(g % 2 + 1) * H * GF].rearrange("p (h c) -> p c h", h=H),
                                AX.X, ALU.add).then_inc(msgs_done, 1)
            def e_block(x_block, y_block):
                for j in range(NJ + 1):
                    x = x_block is not None and j < NJ
                    y1 = y_block is not None and j < NJ
                    y2 = y_block is not None and j > 0
                    pending = []
                    if x:
                        cx = x_block * NJ + j
                    if y1:
                        c = y_block * NJ + j
                        dve.wait_ge(nodes_in[j], LOADED[j] + (y_block + 1) * 32)
                        if j > 0:
                            dve.wait_ge(row_ready, y_block * NJ + j)
                        v.tensor_tensor(unit(hrow, 1), diff[0:P, bass.ds(c * W, W)], nodes[0:P, j, W:2 * W], ALU.add).then_inc(sum_ready, 1)
                    if x:
                        x_products(cx, 0, pending)
                    if y1:
                        n1 = spread(2)
                    if x:
                        x_products(cx, 1, pending); x_sum(cx, pending)
                    if y1:
                        scale_of(2, n1)
                        v.tensor_tensor(slots(unit(hrow, NORMED[j % 2])), slots(unit(hrow, 1)), wide(unit(rstd, 2)), ALU.mult).then_inc(row_ready, 1)
                    if x:
                        x_products(cx, 2, pending); x_sum(cx, pending)
                    if y2:
                        n2 = spread(3)
                    if x:
                        x_products(cx, 3, pending); x_sum(cx, pending)
                    if y2:
                        dve.wait_ge(ring_dma[j - 1], (4 * NB + y_block) * DMAS)
                        c = y_block * NJ + j - 1
                        v.tensor_copy(index_out[0:P, j - 1, :], scatter_to[0:P, bass.ds(c * CE, CE)])
                        finish_rows(nodes[0:P, j - 1, 0:W], ring[0:P, j - 1, :], n2, ring_filled)
                    if x:
                        x_sum(cx, pending)
                    if y2:
                        dve.wait_ge(ring_filled, NC + c + 1)
                        dve.sem_inc(rows_used, 1)
                    tq.next() if x else None
                    tq.next() if y2 else None
                if x_block is not None:
                    scans_and_carry(diff, x_block)
            e_block(0, None)
            tq.restart(); cq.restart(); vq.restart(); rq.restart()
            with dve.Fori(0, NB - 1) as b:
                STEPS = 3 + 3 * NJ
                tq.loop(b, 2 * NJ + 2); cq.loop(b, NJ); vq.loop(b, 8 * NJ); nq.loop(b, 2 * NJ); rq.loop(b, 4 * NJ); steps.loop(b, STEPS)
                e_block(b + 1, b)
                tq.end(NB - 1, 2 * NJ + 2); cq.end(NB - 1, NJ); vq.end(NB - 1, 8 * NJ); nq.end(NB - 1, 2 * NJ); rq.end(NB - 1, 4 * NJ)
                steps.end(NB - 1, STEPS)
            e_block(None, NB - 1)


_INS = ["x", "src", "dst", "edge_attr_2", "L0_gnn_weight", "L0_gnn_root_w", "L0_gnn_root_b", "L1_gnn_W_gat",
        "L1_gnn_att_src", "L1_gnn_att_dst", "L1_gnn_bias_gat", "L1_gnn_w1", "L1_gnn_b1", "L1_gnn_w2", "L1_gnn_b2",
        "L1_gnn_g1", "L1_gnn_be1", "L1_gnn_g2", "L1_gnn_be2"]


def kernel(**inputs):
    import numpy as np
    import concourse.bacc as bacc
    from concourse.bass_utils import run_bass_kernel_spmd

    nc = bacc.Bacc("TRN2", target_bir_lowering=False, num_devices=1)
    arrays, args = {}, []
    for name in _INS:
        a = np.ascontiguousarray(inputs[name])
        arrays[f"in_{name}"] = a
        args.append(nc.dram_tensor(f"in_{name}", a.shape, mybir.dt.from_np(a.dtype), kind="ExternalInput").ap())
    out = nc.dram_tensor("out_rows", (N, F), F32, kind="ExternalOutput").ap()
    gnn_program(nc, *args, out)
    r = run_bass_kernel_spmd(nc, [arrays], core_ids=[0])
    return r.results[0]["out_rows"]
```

```python
import concourse.bass as bass
from concourse import mybir
from concourse.alu_op_type import AluOpType as ALU
from contextlib import ExitStack

F32 = mybir.dt.float32
I32 = mybir.dt.int32
ACT = mybir.ActivationFunctionType
AX = mybir.AxisListType

N, E, F, H, HID, KS = 100000, 50000, 32, 8, 128, 9
P = 125
TN = N // P
NB, NJ, CE = 5, 5, 16
SE = NJ * CE
TE = NB * SE
NC = NB * NJ
W = CE * F
G = CE // 4
GF = 4 * F
WT = G * P
EPS = 1e-5
SLOPE = 0.2
DMAS = 16 * CE
N_BOOT = 6 * 4 + 2 + 2 + 2 + 3
UNITS = {"C": 4, "B": 3, "D": 3}
FIRST = {"C": 0, "B": 20, "D": 35}
OUT_DONE = [NB * 32 + 16 * NB * sum(j < n for n in UNITS.values()) for j in range(NJ)]
CREDIT = 4


class Uses:

    def __init__(self, depth=1):
        self.depth, self.base, self.n = depth, 0, 0

    def next(self):
        self.at = self.base + self.n
        self.room = self.at + CREDIT - min(self.n, self.depth - 1)
        bank = self.n % self.depth
        self.n += 1
        return self.at, bank

    def loop(self, b, per):
        self.first = self.base + self.n
        self.base, self.n = self.first + b * per, 0

    def end(self, times, per):
        assert self.n == per, (self.n, per)
        self.base, self.n = self.first + times * per, 0

    def restart(self):
        self.base, self.n = self.base + self.n, 0


DIFF_T = (0, 3, 0, 3, 0)
NORMED = (2, 0)
HE = (0, 3, 4, 0, 3)


def waves(name, before):
    out = []
    for w in range(NJ if name else 2):
        wave = {}
        for part, lag in (("n3", 2), ("n2", 1), ("n1", 0), ("e2", 1), ("e1", 0)):
            back = w < lag
            phase, j = (before, w - lag + NJ) if back else (name, w - lag)
            if phase and (phase != "C" if part[0] == "e" else j < UNITS[phase]):
                wave[part] = (phase, j, back)
        out.append(wave)
    return out


PER = {name: dict(t=3 * n + (name != "C") * NJ * (3 if name == "B" else 2), c=3 * n + (name != "C") * NJ * 2, f=4 * n,
                  n=3 * n + (name != "C") * NJ, steps=4 * n + {"C": 2 * NJ, "B": 3 * NJ, "D": 3 * NJ + 1}[name])
       for name, n in UNITS.items()}
LOADED = [NB * 16 * (1 + sum(j < n for n in UNITS.values())) for j in range(NJ)]


def gnn_program(nc, x, src, dst, edge_attr, w0, root_w, root_b, w_gat, att_src, att_dst, bias_gat,
                w1, b1, w2, b2, g1, be1, g2, be2, out):
    x1_table = nc.dram_tensor("x1_table", [N + E, F], F32, kind="Internal").ap()
    x1_plain = nc.dram_tensor("x1_plain", [P, TN * F], F32, kind="Internal").ap()
    x1_dst = nc.dram_tensor("x1_dst", [NC, P, W], F32, kind="Internal").ap()
    base_dst = nc.dram_tensor("base_dst", [NC, P, W], F32, kind="Internal").ap()
    x_rows = x.rearrange("(p t) f -> p (t f)", p=P)
    x1_rows = x1_table[0:N, :].rearrange("(p t) f -> p (t f)", p=P)
    spare_rows = x1_table[N:N + E, :].rearrange("(c p s) f -> c p (s f)", c=NC, p=P)
    out_rows = out.rearrange("(p t) f -> p (t f)", p=P)
    edge_slots = lambda a: a.rearrange("(b p s) -> p b s", b=NB, p=P)

    with ExitStack() as ctx:
        sb = lambda name, shape, dt=F32: ctx.enter_context(nc.sbuf_tensor(name, shape, dt))
        ps = lambda name: ctx.enter_context(nc.psum_tensor(name, [128, 512], F32))
        sem = lambda name: ctx.enter_context(nc.semaphore(name))

        region1 = sb("region1", [128, TE * F])
        region2 = sb("region2", [128, TE * F])
        msgs = region1
        beta = region1[:, 0:H * TE]
        self_logit = region1[:, H * TE:2 * H * TE]
        denom = region1[:, 2 * H * TE:3 * H * TE]
        masked = region1[:, 3 * H * TE:4 * H * TE]
        weighted = region1[:, 3 * H * TE:3 * H * TE + 2048]
        basis = region2[:, 0:TE * KS]
        products = region2[:, TE * KS:TE * KS + 2 * KS * GF]
        w0_bd = region2[:, TE * KS + 2 * KS * GF:TE * KS + 3 * KS * GF]
        attr = region1[:, 0:800]
        hats = region1[:, 800:3200]
        row_f = region1[0:33, 3200:3200 + 2 * NB * P]
        row_s = region1[0:1, 4500:4500 + 2 * NB * P]
        whole = region1[0:33, 5800:5800 + NB * P]
        row_i = region1[0:1, 6500:6500 + 2 * NB * P].bitcast(I32)
        dst_i = region1[:, 7800:7800 + TE].bitcast(I32)
        dst_f = region1[:, 8200:8200 + TE]
        att = region1[:, 8600:8600 + 2 * H * F].rearrange("p (k c) -> p k c", k=2)
        gat = region1[:, 9200:9200 + H * F]
        diff = region2

        ring = sb("ring", [128, NJ, W])
        index = sb("index", [128, NJ, CE], I32)
        index_out = sb("index_out", [128, NJ, CE], I32)
        nodes = sb("nodes", [128, NJ, 2 * W])
        xT = sb("xT", [128, 3, WT]); hT = sb("hT", [128, 5, WT])
        sq = sb("sq", [128, 4, W]); hrow = sb("hrow", [128, 4, W])
        var = sb("var", [128, 4, CE]); std = sb("std", [128, 4, CE]); rstd = sb("rstd", [128, 4, CE])
        hid = sb("hid", [128, 4, WT])
        stage = sb("stage", [128, W])

        ident = sb("ident", [128, 128]); ident_bias = sb("ident_bias", [128, 128]); center = sb("center", [128, GF])
        root_bd = sb("root_bd", [128, GF])
        gat_bd = sb("gat_bd", [128, H * GF])
        base_bd = sb("base_bd", [128, GF])
        att_vec = sb("att_vec", [128, 2 * H])
        att_bd = sb("att_bd", [128, 4, 2 * H]); src_bd = sb("src_bd", [128, 4, H])
        w1_q = sb("w1_q", [128, 4, HID]); w2_c = sb("w2_c", [128, F])
        cols = sb("cols", [128, 8])
        ones = sb("ones", [128, 128])
        bias_row = sb("bias_row", [128, 2, W])
        g2_b = sb("g2_b", [128, F]); be2_b = sb("be2_b", [128, F])
        cont = sb("cont", [128, TE]); cont_next = sb("cont_next", [128, TE])
        head = sb("head", [128, TE]); tail = sb("tail", [128, TE])
        degree = sb("degree", [128, TE])
        scatter_to = sb("scatter_to", [128, TE], I32)
        row_cont = sb("row_cont", [33, NB * P]); row_pass = sb("row_pass", [33, NB * P])
        row_pass_back = sb("row_pass_back", [33, NB * P])
        tails = sb("tails", [128, NB * (F + 1)]); tails_row = sb("tails_row", [33, 1 + P])
        carry_in = sb("carry_in", [33, P]); carry_row = sb("carry_row", [128, P]); carry_last = sb("carry_last", [33, 1])
        carry = sb("carry", [128, NB * (F + 1)])
        next_i = sb("next_i", [128, NB], I32)
        rows = hid[:, :, :].rearrange("p t w -> p (t w)")
        a_tails, a_in, a_carry = rows[0:F + 1, 0:1 + NB * P], rows[0:F + 1, 640:640 + NB * P], rows[0:F + 1, 1280:1280 + NB * P]
        flat = nodes[0:H, :, :].rearrange("p j w -> p (j w)")
        s_ends, s_in, s_carry = flat[:, 0:1 + 2 * NB * P], (flat[:, 1280:1280 + NB * P], flat[:, 1920:1920 + NB * P]), \
            (flat[:, 2560:2560 + NB * P], flat[:, 3200:3200 + NB * P])

        T = [ps(f"T{i}") for i in range(2)]
        C = [ps(f"C{i}") for i in range(2)]
        V = [ps(f"V{i}") for i in range(4)]

        VE = [V[0], V[1], C[1], T[1]]

        edges_in = sem("edges_in"); ends_in = sem("ends_in")
        boot_dma = sem("boot_dma"); boot_pool = sem("boot_pool"); boot_dve = sem("boot_dve")
        boot_pe = sem("boot_pe")
        ring_dma = [sem(f"ring_dma{j}") for j in range(NJ)]
        index_in = [sem(f"index_in{j}") for j in range(NJ)]
        ring_used = sem("ring_used")
        ring_saved = [sem(f"ring_saved{j}") for j in range(NJ)]
        ring_filled = sem("ring_filled")
        nodes_in = [sem(f"nodes_in{j}") for j in range(NJ)]
        nodes_ready = sem("nodes_ready")
        rows_kept = sem("rows_kept")
        base_ready = sem("base_ready")
        rows_used = sem("rows_used")
        nodes_out = [sem(f"nodes_out{j}") for j in range(NJ)]
        spare_zero = sem("spare_zero")
        t_ready = sem("t_ready"); t_done = sem("t_done")
        c_ready = sem("c_ready"); c_done = sem("c_done")
        v_ready = sem("v_ready"); v_done = sem("v_done")
        f_ready = sem("f_ready"); f_done = sem("f_done")
        sq_ready = sem("sq_ready"); std_ready = sem("std_ready")
        var_ready = sem("var_ready")
        dve_step = sem("dve_step")
        tails_ready = sem("tails_ready")
        carry_ready = sem("carry_ready")
        exp_ready = sem("exp_ready")
        cleared = sem("cleared")
        exp_in = sem("exp_in")
        softmax_done = sem("softmax_done")
        sum_ready = sem("sum_ready")
        row_ready = sem("row_ready")
        stage_ready = sem("stage_ready")
        msgs_done = sem("msgs_done")

        block = ctx.enter_context(nc.Block())
        unit = lambda t, k: t[0:P, k, :]

        @block.sync
        def _(sp):
            n = [0]
            def load(to, frm, done=None, **kw):
                sp.dma_start(to, frm, **kw).then_inc(done or boot_dma, 16)
                n[0] += done is None
            def index_load(of, b, j, done):
                if done is not None:
                    sp.wait_ge(ring_dma[j], done)
                rows = of.rearrange("(b p j s) -> b p j s", b=NB, p=P, j=NJ)
                sp.dma_start(index[0:P, j, :], rows[b, :, j, :] if isinstance(b, int) else rows[bass.ds(b, 1), :, j, :]).then_inc(index_in[j], 16)
            for j in range(NJ):
                index_load(src, 0, j, None)
            load(dst_i[0:P, :].rearrange("p (b s) -> p b s", b=NB), edge_slots(dst), edges_in)
            load(attr[0:P, :].rearrange("p (b s) -> p b s", b=NB), edge_attr.rearrange("(b p s) a -> p b (s a)", b=NB, p=P), edges_in)
            for j in range(NJ):
                sp.dma_start(nodes[0:P, j, :], x_rows[:, j * 2 * W:(j + 1) * 2 * W]).then_inc(nodes_in[j], 16)
            sp.wait_ge(boot_dve, 1)
            ends = dst.rearrange("(c s) -> s c", s=SE)
            load(row_i[0:1, 0:NB * P], ends[0:1, :], ends_in, allow_slow_non_contiguous=True)
            load(row_i[0:1, NB * P:2 * NB * P], ends[SE - 1:SE, :], ends_in, allow_slow_non_contiguous=True)
            first = ends[0, :].rearrange("(b p) -> p b", b=NB)
            load(next_i[0:P - 1, :], first[1:P, :], ends_in, allow_slow_non_contiguous=True)
            load(next_i[P - 1:P, 0:NB - 1], first[0:1, 1:NB], ends_in, allow_slow_non_contiguous=True)
            sp.wait_ge(boot_pool, 3)
            for t in range(4):
                q = slice(t * F, (t + 1) * F)
                load(w0_bd[q, :].rearrange("f (k t o) -> f k t o", k=KS, t=4)[:, :, t, :], w0.rearrange("k f o -> f k o"))
                load(root_bd[q, q], root_w)
                load(gat[q, :], w_gat)
                load(w1_q[q, t, :], w1)
                load(cols[q, 1:2], g1.rearrange("(f a) -> f a", a=1))
                load(cols[q, 2:3], be1.rearrange("(f a) -> f a", a=1))
            load(cols[:, 0:1], b1.rearrange("(f a) -> f a", a=1))
            load(w2_c[:, :], w2)
            for k, v in enumerate((att_src, att_dst)):
                load(att[:, k, :], v.rearrange("(a h) f -> a (h f)", a=1).to_broadcast([128, H * F]))
            for k, v in enumerate((g2, be2)):
                load((g2_b, be2_b)[k][0:P, :], v.rearrange("(a f) -> a f", a=1).to_broadcast([P, F]))
            for k, v in enumerate((bias_gat, b2)):
                load(bias_row[0:1, k, 0:F], v.rearrange("(a f) -> a f", a=1))
            load(nodes[P:P + 1, :, :].rearrange("a j (s f) -> a (j s) f", f=F),
                 root_b.rearrange("(a b f) -> a b f", a=1, b=1).to_broadcast([1, NJ * 2 * CE, F]))
            assert n[0] == N_BOOT, n[0]

            def a_chunk(b, j, more):
                c = b * NJ + j
                if more:
                    index_load(src, b + 1, j, (b + 1) * DMAS)
                sp.dma_start(spare_rows[bass.ds(c, 1), :, :].rearrange("a p w -> (a p) w"), stage[0:P, :]).then_inc(spare_zero, 16)
                sp.wait_ge(nodes_ready, c + 1)
                for to in (x1_rows, x1_plain):
                    sp.dma_start(to[:, bass.ds(c * 2 * W, 2 * W)], nodes[0:P, j, :]).then_inc(nodes_out[j], 16)
                if more:
                    sp.wait_ge(nodes_out[j], (b + 1) * 32)
                    sp.dma_start(nodes[0:P, j, :], x_rows[:, bass.ds((c + NJ) * 2 * W, 2 * W)]).then_inc(nodes_in[j], 16)
            sp.wait_ge(boot_dve, 2)
            with sp.Fori(0, NB - 1) as b:
                for j in range(NJ):
                    a_chunk(b, j, True)
            for j in range(NJ):
                a_chunk(NB - 1, j, False)
            for j in range(NJ):
                sp.wait_ge(nodes_out[j], NB * 32)

            def node_load(u, i):
                sp.dma_start(nodes[0:P, i, 0:W], x1_plain[:, bass.ds(u * W, W)]).then_inc(nodes_in[i], 16)

            def node_store(u, i, ready):
                sp.wait_ge(nodes_ready, ready)
                sp.dma_start(out_rows[:, bass.ds(u * W, W)], nodes[0:P, i, 0:W]).then_inc(nodes_out[i], 16)

            stored = [NB * 32] * NJ
            finished = NC

            stored, finished, before = {}, {}, None
            for name in "CBD":
                last = UNITS.get(before, 0)
                stored[name] = [(stored[before][i] if before else NB * 32) + (16 * NB if i < last else 0) for i in range(NJ)]
                finished[name] = (finished[before] if before else NC) + NB * last
                before = name

            def unit_turn(name, b, i):
                n = UNITS[name]
                following = {"C": "B", "B": "D"}.get(name) if isinstance(b, int) and b == NB - 1 else name
                node_store(FIRST[name] + b * n + i, i, finished[name] + b * n + i + 1)
                if following and i < UNITS[following]:
                    sp.wait_ge(nodes_out[i], stored[name][i] + (b + 1) * 16)
                    node_load(FIRST[name] + (b + 1) * n + i if following == name else FIRST[following] + i, i)

            def base_save(c, j):
                sp.wait_ge(base_ready, c + 1)
                sp.dma_start(base_dst[bass.ds(c, 1), :, :].rearrange("a p w -> (a p) w"), nodes[0:P, j, W:2 * W]).then_inc(ring_saved[j], 16)

            def wave_moves(name, b, w, wave):
                if name == "B":
                    more = not isinstance(b, int) or b < NB - 1
                    index_load(dst if more else src, b + 1 if more else 0, w, (2 * NB + b + 1) * DMAS)
                    sp.wait_ge(rows_kept, b * NJ + w + 1)
                    sp.dma_start(x1_dst[bass.ds(b * NJ + w, 1), :, :].rearrange("a p w -> (a p) w"), ring[0:P, w, :]).then_inc(ring_saved[w], 16)
                if name == "D" and (not isinstance(b, int) or b < NB - 1):
                    index_load(src, b + 1, w, (3 * NB + 1 + b) * DMAS)
                for part in ("e2", "n3"):
                    if part in wave:
                        owner, j, back = wave[part]
                        at = NB - 1 if owner != name else b - 1 if back else b
                        if part == "n3":
                            unit_turn(owner, at, j)
                        elif owner == "B":
                            base_save(at * NJ + j, j)

            for j in range(NJ):
                index_load(dst, 0, j, NB * DMAS)
            for i in range(UNITS["C"]):
                node_load(i, i)
            before = None
            for name in "CBD":
                for w, wave in enumerate(waves(name, before)):
                    wave_moves(name, 0, w, wave)
                with sp.Fori(0, NB - 2) as b:
                    for w, wave in enumerate(waves(name, name)):
                        wave_moves(name, b + 1, w, wave)
                for w, wave in enumerate(waves(name, name)):
                    wave_moves(name, NB - 1, w, wave)
                before = name
            for w, wave in enumerate(waves(None, "D")):
                wave_moves(None, None, w, wave)

            def e_load(c, j):
                sp.dma_start(nodes[0:P, j, 0:W], x1_dst[bass.ds(c, 1), :, :].rearrange("a p w -> (a p) w")).then_inc(nodes_in[j], 16)
                sp.dma_start(nodes[0:P, j, W:2 * W], base_dst[bass.ds(c, 1), :, :].rearrange("a p w -> (a p) w")).then_inc(nodes_in[j], 16)
            for j in range(NJ):
                sp.wait_ge(nodes_out[j], OUT_DONE[j])
                sp.wait_ge(ring_saved[j], NB * 32)
            sp.wait_ge(softmax_done, 1)
            for j in range(NJ):
                e_load(j, j)
            with sp.Fori(0, NB - 1) as b:
                for j in range(NJ):
                    sp.wait_ge(rows_used, b * NJ + j + 1)
                    e_load((b + 1) * NJ + j, j)
            for j in range(NJ):
                sp.wait_ge(ring_dma[j], 5 * NB * DMAS)

        @block.gpsimd
        def _(pool):
            pool.memset(ident[:, :], 0.0).then_inc(boot_pe, 1)
            pool.memset(w0_bd[:, :], 0.0).then_inc(boot_pool, 1)
            pool.memset(root_bd[:, :], 0.0).then_inc(boot_pool, 1)
            pool.memset(w1_q[:, :, :], 0.0).then_inc(boot_pool, 1)
            pool.wait_ge(boot_pe, 1)
            pool.affine_select(out=ident[:, :], in_=ident[:, :], compare_op=ALU.not_equal, fill=1.0, base=0,
                               pattern=[[-1, 128]], channel_multiplier=1).then_inc(boot_pool, 1)
            pool.wait_ge(boot_pool, 4)
            pool.affine_select(out=ident_bias[:, :], in_=ident[:, :], compare_op=ALU.is_gt, fill=1.0, base=P,
                               pattern=[[0, 128]], channel_multiplier=-1).then_inc(boot_pool, 1)
            pool.iota(scatter_to[:, :], pattern=[[P * SE, NB], [1, SE]], base=N, channel_multiplier=SE).then_inc(boot_pool, 1)

            def gather(table, j):
                pool.sem_inc(cleared, 1)
                for s in range(CE):
                    pool.indirect_dma_start(
                        out=ring[0:P, j, s * F:(s + 1) * F], out_offset=None, in_=table[:, :],
                        in_offset=bass.IndirectOffsetOnAxis(ap=index[0:P, j, s:s + 1], axis=0)).then_inc(ring_dma[j], 16)

            with pool.Fori(0, NB) as b:
                for j in range(NJ):
                    pool.wait_ge(index_in[j], 16 * (b + 1))
                    pool.wait_ge(ring_used, b * NJ + j + 1)
                    gather(x, j)
            for j in range(NJ):
                pool.wait_ge(nodes_out[j], NB * 32)
            pool.wait_ge(spare_zero, NC * 16)
            with pool.Fori(0, NB) as b:
                for j in range(NJ):
                    pool.wait_ge(ring_filled, b * NJ + j + 1)
                    pool.sem_inc(cleared, 1)
                    for s in range(CE):
                        pool.indirect_dma_start(
                            out=x1_table[:, :], out_offset=bass.IndirectOffsetOnAxis(ap=index_out[0:P, j, s:s + 1], axis=0),
                            in_=ring[0:P, j, s * F:(s + 1) * F], in_offset=None, compute_op=ALU.add).then_inc(ring_dma[j], 16)
            for j in range(NJ):
                pool.wait_ge(ring_dma[j], 2 * NB * DMAS)
            def b_block(b):
                for j in range(NJ):
                    pool.wait_ge(index_in[j], 16 * NB + 16 * (b + 1))
                    pool.wait_ge(ring_used, NC + b * NJ + j + 1)
                    if not isinstance(b, int):
                        pool.wait_ge(ring_saved[j], 32 * b)
                    gather(x1_table, j)
            b_block(0)
            with pool.Fori(1, NB) as b:
                b_block(b)
            with pool.Fori(0, NB) as b:
                for j in range(NJ):
                    pool.wait_ge(index_in[j], 16 * NB * 2 + 16 * (b + 1))
                    pool.wait_ge(ring_used, 2 * NC + b * NJ + j + 1)
                    pool.wait_ge(ring_saved[j], 32 * NB)
                    gather(x1_table, j)
            for j in range(NJ):
                pool.wait_ge(nodes_out[j], OUT_DONE[j])
            last_row = pool.to_reg(N - 1)
            with pool.Fori(0, NB) as b:
                for j in range(NJ):
                    pool.wait_ge(ring_filled, NC + b * NJ + j + 1)
                    pool.sem_inc(cleared, 1)
                    for s in range(CE):
                        pool.indirect_dma_start(
                            out=out[:, :], out_offset=bass.IndirectOffsetOnAxis(ap=index_out[0:P, j, s:s + 1], axis=0),
                            in_=ring[0:P, j, s * F:(s + 1) * F], in_offset=None,
                            bounds_check=last_row, oob_is_err=False).then_inc(ring_dma[j], 16)

        @block.tensor
        def _(pe):
            tq, cq, vq, fq = Uses(2), Uses(2), Uses(4), Uses(4)
            mm = nc.tensor.matmul
            pe.sem_inc(ring_used, NJ)

            def transpose(rows):
                at, bank = tq.next()
                pe.wait_ge(t_done, tq.room)
                for g in range(G):
                    i = nc.tensor.transpose(T[bank][:, g * P:(g + 1) * P], rows[:, g * GF:(g + 1) * GF], ident[0:P, 0:P])
                    i.then_inc(t_ready, 1) if g == G - 1 else None
                return at

            def product(cols_T, right, n=GF, bias=None, t_at=None, frees=None):
                at, bank = cq.next()
                pe.wait_ge(c_done, cq.room)
                if t_at is not None:
                    pe.wait_ge(t_done, t_at + 1 + CREDIT)
                if bias is not None:
                    mm(C[bank][0:P, :], ones[:, 0:P], bias_row[:, bias, :], start=True, stop=True, skip_group_check=True)
                for g in range(G):
                    i = mm(C[bank][0:P, g * n:(g + 1) * n], cols_T[:, g * P:(g + 1) * P], right,
                           start=bias is None, stop=True, skip_group_check=True)
                    if g == 0 and frees is not None:
                        i.then_inc(frees, 1)
                i.then_inc(c_ready, 1)
                return at

            pe.wait_ge(boot_pool, 6)
            pe.wait_ge(boot_dve, 2)
            for m in range(2):
                for q, (lo, hi) in enumerate(((0, 4 * P), (4 * P, NB * P))):
                    to = V[1][0:33, m * 128:m * 128 + P] if q else V[2 * m][0:33, 0:4 * P]
                    mm(to, ones[0:1, 0:33], row_s[0:1, m * NB * P + lo:m * NB * P + hi],
                       start=True, stop=True).then_inc(boot_pe, 1)
            pe.wait_ge(boot_dma, 16 * N_BOOT)
            nc.tensor.transpose(V[3][:, 256:256 + GF], root_bd[:, :], ident[:, :]).then_inc(boot_pe, 1)
            pe.wait_ge(t_done, CREDIT)

            def hidden(nT, quarters=range(4)):
                for t in quarters:
                    at, bank = fq.next()
                    pe.wait_ge(f_done, fq.room)
                    mm(V[4 - fq.depth + bank][:, 0:WT], w1_q[:, t, :], nT, start=True, stop=True).then_inc(f_ready, 1)

            def back(nT):
                at, bank = cq.next()
                pe.wait_ge(c_done, cq.room)
                mm(C[bank][0:P, :], ones[:, 0:P], bias_row[:, 1, :], start=True, stop=True, skip_group_check=True)
                for g in range(G):
                    mm(C[bank][0:P, g * GF:(g + 1) * GF], nT[:, g * P:(g + 1) * P], center[:, :], start=False, stop=True, skip_group_check=True)
                for t in range(4):
                    pe.wait_ge(f_done, fq.at - 3 + t + 1 + CREDIT)
                    for g in range(G):
                        i = mm(C[bank][0:P, (4 * g + t) * F:(4 * g + t + 1) * F], hid[:, t, g * P:(g + 1) * P], w2_c[:, :],
                               start=False, stop=True, skip_group_check=True)
                i.then_inc(c_ready, 1)

            def to_T(cols_T, right, t_at, bias=None, plus=None):
                at, bank = tq.next()
                pe.wait_ge(t_done, tq.room)
                pe.wait_ge(t_done, t_at + 1 + CREDIT)
                if plus is not None:
                    mm(T[bank][0:P, :], ident_bias[0:P + 1, 0:P], plus, start=True, stop=True, skip_group_check=True)
                else:
                    mm(T[bank][0:P, :], ones[:, 0:P], bias_row[:, bias, :], start=True, stop=True, skip_group_check=True)
                for g in range(G):
                    i = mm(T[bank][0:P, g * GF:(g + 1) * GF], cols_T[:, g * P:(g + 1) * P], right, start=False, stop=True, skip_group_check=True)
                i.then_inc(t_ready, 1)

            def values(j, g, pieces):
                for q in pieces:
                    at, bank = vq.next()
                    pe.wait_ge(v_done, vq.room)
                    mm(V[bank][0:P, 0:3 * GF], hT[:, HE[j], g * P:(g + 1) * P], w0_bd[:, q * 3 * GF:(q + 1) * 3 * GF],
                       start=True, stop=True).then_inc(v_ready, 1)

            st_t, st = {}, {}
            def a_wave(jx, jh, jv, b):
                h, old = {}, st_t.get("h0")
                def rows_T(k):
                    if jh is not None:
                        pe.wait_ge(c_done, st[k] + 1 + CREDIT)
                        h[k] = transpose(unit(hrow, k))
                def center_rows(k):
                    if jx is not None:
                        if k == 0:
                            pe.wait_ge(ring_dma[jx], (b + 1) * DMAS)
                        if k == 1:
                            pe.wait_ge(nodes_in[jx], (b + 1) * 16)
                        t = transpose(unit(ring, jx) if k == 0 else nodes[0:P, jx, (k - 1) * W:k * W])
                        return t
                def centred(k, t):
                    if jx is not None:
                        st[k] = product(xT[:, k, :], center[:, :], t_at=t, frees=ring_used if k == 0 else None)
                def dense(k):
                    if jh is not None:
                        to_T(hT[:, k, :], root_bd[:, :], h[k], plus=nodes[0:P + 1, jh, (k - 1) * W:k * W])
                def weigh(g, *pieces):
                    if jv is not None:
                        if g == 0 and pieces[0] == 0:
                            pe.wait_ge(t_done, old + 1 + CREDIT)
                        values(jv, g, pieces)
                rows_T(0); rows_T(1)
                weigh(0, 0)
                t = center_rows(0)
                weigh(0, 1, 2)
                centred(0, t); dense(1)
                weigh(1, 0)
                rows_T(2)
                weigh(1, 1, 2)
                t = center_rows(1)
                weigh(2, 0)
                centred(1, t); dense(2)
                weigh(2, 1)
                t = center_rows(2)
                weigh(2, 2); weigh(3, 0)
                centred(2, t)
                weigh(3, 1, 2)
                if jh is not None:
                    st_t["h0"] = h[0]
            def a_block(b, first, last=False):
                for w in range(2 if last else NJ):
                    if first and w == 1:
                        pe.wait_ge(boot_dve, 4)
                    a_wave(None if last else w, None if first and w == 0 or last and w == 1 else (w - 1) % NJ,
                           None if first and w < 2 else (w - 2) % NJ, b)
            tq.restart(); cq.restart()
            a_block(0, True)
            tq.restart(); cq.restart(); vq.restart()
            lag_t, lags = tq.base - st_t["h0"], {k: cq.base - at for k, at in st.items()}
            with pe.Fori(0, NB - 1) as b:
                tq.loop(b, 8 * NJ); cq.loop(b, 3 * NJ); vq.loop(b, 12 * NJ)
                st_t["h0"] = tq.base - lag_t; st.update({k: cq.base - lag for k, lag in lags.items()})
                a_block(b + 1, False)
                tq.end(NB - 1, 8 * NJ); cq.end(NB - 1, 3 * NJ); vq.end(NB - 1, 12 * NJ)
            st_t["h0"] = tq.base - lag_t; st.update({k: cq.base - lag for k, lag in lags.items()})
            a_block(None, False, True)
            st.clear()

            tq.restart()
            for half in (0, 1):
                pe.wait_ge((tails_ready, carry_ready)[half], 1)
                for bb in range(NB):
                    at, bank = tq.next()
                    pe.wait_ge(t_done, tq.room)
                    if half == 0:
                        nc.tensor.transpose(T[bank][0:F + 1, 0:P], tails[0:P, bb * (F + 1):(bb + 1) * (F + 1)], ident[0:P, 0:P]).then_inc(t_ready, 1)
                    else:
                        nc.tensor.transpose(T[bank][0:P, 0:F + 1], a_carry[:, bb * P:(bb + 1) * P], ident[0:F + 1, 0:F + 1]).then_inc(t_ready, 1)

            def wave_products(wave, loaded, gathered):
                t = {}
                if "n3" in wave:
                    pe.wait_ge(c_done, st["n2"] + 1 + CREDIT)
                    t["n3"] = transpose(unit(hrow, 2))
                if "n2" in wave:
                    pe.wait_ge(c_done, st["n1"] + 1 + CREDIT)
                    t["n2"] = transpose(unit(hrow, 1))
                if "n3" in wave:
                    pe.wait_ge(t_done, t["n3"] + 1 + CREDIT)
                    hidden(xT[:, 2, :])
                if "n2" in wave:
                    st["n2"] = product(hT[:, 1, :], base_bd[:, :], bias=0, t_at=t["n2"])
                if "n1" in wave:
                    pe.wait_ge(nodes_in[wave["n1"][1]], loaded(wave["n1"]))
                    t["n1"] = transpose(nodes[0:P, wave["n1"][1], 0:W])
                if "e2" in wave:
                    pe.wait_ge(c_done, st["e1"] + 1 + CREDIT)
                    t["e2"] = transpose(unit(hrow, 0))
                if "n1" in wave:
                    st["n1"] = product(xT[:, 1, :], center[:, :], t_at=t["n1"])
                if "e1" in wave:
                    pe.wait_ge(ring_dma[wave["e1"][1]], gathered)
                    t["e1"] = transpose(unit(ring, wave["e1"][1]))
                if "n3" in wave:
                    back(xT[:, 2, :])
                if "e2" in wave and wave["e2"][0] == "B":
                    to_T(hT[:, 0, :], base_bd[:, :], bias=0, t_at=t["e2"])
                    product(hT[:, 0, :], att_bd[:, :, :].rearrange("f t h -> f (t h)"), n=8 * H)
                elif "e2" in wave:
                    product(hT[:, 0, :], src_bd[:, :, :].rearrange("f t h -> f (t h)"), n=4 * H, t_at=t["e2"])
                if "e1" in wave:
                    st["e1"] = product(xT[:, 0, :], center[:, :], t_at=t["e1"], frees=ring_used)

            pe.wait_ge(v_done, 12 * NC + CREDIT)
            loads = [NB * 16] * NJ
            def wave_block(name, before, b):
                for wave in waves(name, before):
                    wave_products(wave, lambda unit_of: loads[unit_of[1]] + (b + 1) * 16,
                                  ({"B": 2, "D": 3}.get(name, 0) * NB + b + 1) * DMAS)
            before = None
            for name in "CBD":
                per = PER[name]
                tq.restart(); cq.restart(); fq.restart()
                wave_block(name, before, 0)
                lags = {k: cq.base + cq.n - at for k, at in st.items()}
                with pe.Fori(0, NB - 1) as b:
                    tq.loop(b, per["t"]); cq.loop(b, per["c"]); fq.loop(b, per["f"])
                    for k, lag in lags.items():
                        st[k] = cq.base - lag
                    wave_block(name, name, b + 1)
                    tq.end(NB - 1, per["t"]); cq.end(NB - 1, per["c"]); fq.end(NB - 1, per["f"])
                for k, lag in lags.items():
                    st[k] = cq.base - lag
                for i in range(UNITS[name]):
                    loads[i] += NB * 16
                before = name
            for wave in waves(None, "D"):
                wave_products(wave, None, None)

            tq.restart()
            for m in (1, 2):
                pe.wait_ge(tails_ready, m + 1)
                for k in range(0, 2 * NB, 4):
                    at, bank = tq.next()
                    pe.wait_ge(t_done, tq.room)
                    for i in range(k, min(k + 4, 2 * NB)):
                        tr = nc.tensor.transpose(T[bank][0:H, (i - k) * P:(i - k + 1) * P], tails[0:P, i * H:(i + 1) * H], ident[0:P, 0:P])
                    tr.then_inc(t_ready, 1)
                at, bank = tq.next()
                pe.wait_ge(t_done, tq.room)
                pe.wait_ge(carry_ready, m + 1)
                for i in range(2 * NB):
                    tr = nc.tensor.transpose(T[bank][0:P, i * H:(i + 1) * H], s_carry[i // NB][:, (i % NB) * P:(i % NB + 1) * P], ident[0:H, 0:H])
                tr.then_inc(t_ready, 1)

            tq.restart(); cq.restart(); vq.restart()
            tq.depth, cq.depth, fq.depth = 1, 1, 2
            fq.restart()
            pe.wait_ge(f_done, 4 * sum(UNITS.values()) * NB + CREDIT)
            def x_rows(j, c):
                pe.wait_ge(stage_ready, c + 1)
                st["x"] = transpose(stage[0:P, :])
            def x_values(j, g):
                if g == 0:
                    pe.wait_ge(t_done, st["x"] + 1 + CREDIT)
                for q in range(2):
                    at, bank = vq.next()
                    pe.wait_ge(v_done, vq.room)
                    mm(VE[bank][0:P, :], hT[:, DIFF_T[j], g * P:(g + 1) * P], gat_bd[:, q * 512:(q + 1) * 512],
                       start=True, stop=True).then_inc(v_ready, 1)
            def e_block(x_block, y_block):
                x, y = x_block is not None, y_block is not None
                if x:
                    x_rows(0, x_block * NJ)
                for j in range(NJ):
                    y2 = y and j > 0
                    if y2:
                        pe.wait_ge(row_ready, y_block * NJ + j)
                        t = transpose(unit(hrow, NORMED[(j - 1) % 2]))
                    if x: x_values(j, 0)
                    if y2:
                        pe.wait_ge(t_done, t + 1 + CREDIT)
                        hidden(xT[:, 2, :], (0, 1))
                    if x: x_values(j, 1)
                    if y2: hidden(xT[:, 2, :], (2, 3))
                    if x: x_values(j, 2)
                    if x and j + 1 < NJ: x_rows(j + 1, x_block * NJ + j + 1)
                    if x: x_values(j, 3)
                    if y2: back(xT[:, 2, :])
                if y:
                    pe.wait_ge(row_ready, y_block * NJ + NJ)
                    t = transpose(unit(hrow, NORMED[(NJ - 1) % 2]))
                    pe.wait_ge(t_done, t + 1 + CREDIT)
                    hidden(xT[:, 2, :])
                if x:
                    at, bank = tq.next()
                    pe.wait_ge(t_done, tq.room)
                    pe.wait_ge(tails_ready, 1 + 2 + x_block + 1)
                    nc.tensor.transpose(T[bank][:, 0:P], tails[0:P, 0:128], ident[0:P, 0:P]).then_inc(t_ready, 1)
                if y:
                    back(xT[:, 2, :])
                if x:
                    at, bank = tq.next()
                    pe.wait_ge(t_done, tq.room)
                    pe.wait_ge(carry_ready, 1 + 2 + x_block + 1)
                    nc.tensor.transpose(T[bank][0:P, 0:128], carry_row[:, :], ident[:, :]).then_inc(t_ready, 1)
            e_block(0, None)
            tq.restart(); cq.restart(); vq.restart(); fq.restart()
            with pe.Fori(0, NB - 1) as b:
                tq.loop(b, 2 * NJ + 2); cq.loop(b, NJ); vq.loop(b, 8 * NJ); fq.loop(b, 4 * NJ)
                e_block(b + 1, b)
                tq.end(NB - 1, 2 * NJ + 2); cq.end(NB - 1, NJ); vq.end(NB - 1, 8 * NJ); fq.end(NB - 1, 4 * NJ)
            e_block(None, NB - 1)

        @block.scalar
        def _(act):
            tq, cq, fq, nq = Uses(2), Uses(2), Uses(4), Uses()
            act.sem_inc(t_done, CREDIT)
            act.sem_inc(f_done, CREDIT)
            act.wait_ge(boot_dve, 2)

            def evac(to, rows=128, width=WT, func=ACT.Copy, **kw):
                at, bank = tq.next()
                act.wait_ge(t_ready, at + 1)
                nc.scalar.activation(to, T[bank][0:rows, 0:width], func, **kw).then_inc(t_done, 1)

            def square(k, rows=None):
                if rows is None:
                    at, bank = cq.next()
                    act.wait_ge(c_ready, at + 1)
                    rows = C[bank][0:P, :]
                nc.scalar.activation(unit(sq, k), rows, ACT.Square).then_inc(sq_ready, 1)

            def root(k):
                at, _ = nq.next()
                act.wait_ge(var_ready, at + 1)
                nc.scalar.activation(unit(std, k), unit(var, k), ACT.Sqrt, scale=1.0 / F, bias=cols[0:P, 3:4]).then_inc(std_ready, 1)

            def hidden(quarters=range(4)):
                for t in quarters:
                    at, bank = fq.next()
                    act.wait_ge(f_ready, at + 1)
                    nc.scalar.activation(hid[:, t, :], V[4 - fq.depth + bank][:, 0:WT], ACT.Relu, bias=cols[:, 0:1]).then_inc(f_done, 1)

            def affine():
                evac(xT[:, 2, :], func=ACT.Identity, scale=cols[:, 1:2], bias=cols[:, 2:3])

            def a_wave(jx, jh):
                x, h = jx is not None, jh is not None
                if h: evac(hT[:, HE[jh], :]); evac(hT[:, 1, :]); root(2)
                if x: evac(xT[:, 0, :]); square(0)
                if h: evac(nodes[0:P, jh, 0:W], rows=P, width=W); evac(hT[:, 2, :])
                if x: root(0); evac(xT[:, 1, :]); square(1)
                if h:
                    evac(nodes[0:P, jh, W:2 * W], rows=P, width=W)
                    act.wait_ge(t_done, tq.at + 1 + CREDIT)
                    act.sem_inc(nodes_ready, 1)
                if x: root(1); evac(xT[:, 2, :]); square(2)
            def a_block(first, last=False):
                for w in range(2 if last else NJ):
                    a_wave(None if last else w, None if first and w == 0 or last and w == 1 else (w - 1) % NJ)
            a_block(True)
            tq.restart(); cq.restart()
            with act.Fori(0, NB - 1) as b:
                tq.loop(b, 8 * NJ); cq.loop(b, 3 * NJ); nq.loop(b, 3 * NJ)
                a_block(False)
                tq.end(NB - 1, 8 * NJ); cq.end(NB - 1, 3 * NJ); nq.end(NB - 1, 3 * NJ)
            a_block(False, True)
            tq.restart()
            for bb in range(NB):
                evac(a_tails[:, 1 + bb * P:1 + (bb + 1) * P], rows=F + 1, width=P)
            for bb in range(NB):
                evac(carry[0:P, bb * (F + 1):(bb + 1) * (F + 1)], rows=P, width=F + 1)

            late = []
            def wave_block(name, before):
                for wave in waves(name, before):
                    if "n3" in wave: affine()
                    if "n2" in wave: evac(hT[:, 1, :])
                    if late: root(late.pop())
                    if "e2" in wave: root(0)
                    if "n3" in wave: hidden()
                    if "n2" in wave: square(2)
                    if "n1" in wave: evac(xT[:, 1, :])
                    if "e2" in wave: evac(hT[:, 0, :])
                    if "n2" in wave: root(2)
                    if "n1" in wave: square(1); root(1)
                    if "e1" in wave: evac(xT[:, 0, :])
                    if "n3" in wave: square(3)
                    if "e2" in wave:
                        if wave["e2"][0] == "B":
                            evac(nodes[0:P, wave["e2"][1], W:2 * W], rows=P, width=W)
                            act.wait_ge(t_done, tq.at + 1 + CREDIT)
                            act.sem_inc(base_ready, 1)
                        cq.next()
                    if "n3" in wave and "e1" in wave: root(3)
                    elif "n3" in wave: late.append(3)
                    if "e1" in wave: square(0)
            before = None
            for name in "CBD":
                per = PER[name]
                tq.restart(); cq.restart(); fq.restart()
                wave_block(name, before)
                with act.Fori(0, NB - 1) as b:
                    tq.loop(b, per["t"]); cq.loop(b, per["c"]); fq.loop(b, per["f"]); nq.loop(b, per["n"])
                    wave_block(name, name)
                    tq.end(NB - 1, per["t"]); cq.end(NB - 1, per["c"]); fq.end(NB - 1, per["f"]); nq.end(NB - 1, per["n"])
                before = name
            wave_block(None, "D")

            tq.restart()
            for m in range(2):
                if m == 1:
                    for k in range(2):
                        half = beta[0:P, k * H * TE // 2:(k + 1) * H * TE // 2]
                        act.wait_ge(exp_in, k + 1)
                        nc.scalar.activation(half, half, ACT.Exp).then_inc(exp_ready, 1)
                    nc.scalar.activation(self_logit[0:P, :], self_logit[0:P, :], ACT.Exp, scale=-1.0).then_inc(exp_ready, 1)
                for k in range(0, 2 * NB, 4):
                    n = min(4, 2 * NB - k) * P
                    evac(s_ends[:, 1 + k * P:1 + k * P + n], rows=H, width=n)
                evac(carry[0:P, 0:2 * NB * H], rows=P, width=2 * NB * H)
            tq.restart(); cq.restart(); tq.depth, cq.depth, fq.depth = 1, 1, 2; fq.restart()
            def x_stage(c):
                nc.scalar.activation(stage[0:P, :], diff[0:P, bass.ds(c * W, W)], ACT.Copy).then_inc(stage_ready, 1)
            def e_block(x_block, y_block):
                x, y = x_block is not None, y_block is not None
                if x:
                    x_stage(x_block * NJ)
                    evac(hT[:, DIFF_T[0], :])
                for j in range(NJ):
                    y2, more = y and j > 0, x and j + 1 < NJ
                    if y2: affine()
                    if more: x_stage(x_block * NJ + j + 1)
                    if y:
                        act.wait_ge(sum_ready, y_block * NJ + j + 1)
                        square(2, unit(hrow, 1))
                    if y2: hidden((0, 1))
                    if y2 and j > 1: root(3)
                    if y: root(2)
                    if y2: hidden((2, 3))
                    if more: evac(hT[:, DIFF_T[j + 1], :])
                    if y2: square(3)
                if y: affine(); hidden(); root(3)
                if x: evac(tails_row[0:F, 1:1 + P], rows=F, width=P)
                if y: square(3)
                if x: evac(carry[0:P, 0:F], rows=P, width=F)
                if y: root(3)
            e_block(0, None)
            tq.restart(); cq.restart(); fq.restart()
            with act.Fori(0, NB - 1) as b:
                tq.loop(b, 2 * NJ + 2); cq.loop(b, NJ); fq.loop(b, 4 * NJ); nq.loop(b, 2 * NJ)
                e_block(b + 1, b)
                tq.end(NB - 1, 2 * NJ + 2); cq.end(NB - 1, NJ); fq.end(NB - 1, 4 * NJ); nq.end(NB - 1, 2 * NJ)
            e_block(None, NB - 1)

        @block.vector
        def _(dve):
            v = nc.vector
            steps = Uses()
            R = NB * P
            tq, cq, vq, nq, rq = Uses(2), Uses(2), Uses(4), Uses(), Uses(2)
            slots = lambda a: a.rearrange("p (s f) -> p s f", f=F)
            wide = lambda a: a.unsqueeze(2).to_broadcast([P, CE, F])

            def step(i):
                at, _ = steps.next()
                i.then_inc(dve_step, 1)
                dve.wait_ge(dve_step, at + 1)

            dve.sem_inc(c_done, CREDIT)
            dve.sem_inc(v_done, CREDIT)
            dve.sem_inc(msgs_done, CREDIT)
            v.memset(cols[:, 3:4], EPS)
            v.memset(bias_row[:, :, :], 0.0)
            v.memset(next_i[:, :], -1).then_inc(boot_dve, 1)
            for a, value in ((ones, 1.0), (gat_bd, 0.0), (center, 0.0), (att_bd, 0.0), (src_bd, 0.0),
                             (stage, 0.0), (cont, 0.0), (cont_next, 0.0), (row_cont, 0.0), (row_pass, 0.0),
                             (row_pass_back, 0.0), (tails_row, 0.0), (carry_last, 0.0), (tails, 0.0), (carry_row, 0.0)):
                i = v.memset(a[:, :] if len(a.shape) == 2 else a[:, :, :], value)
            step(i)
            for t in range(4):
                q = slice(t * F, (t + 1) * F)
                i = v.memset(center[q, q], 1.0 / F)
            step(i)
            dve.wait_ge(boot_pool, 6)
            step(v.tensor_tensor(center[:, :], ident[:, :], center[:, :], ALU.subtract))
            dve.wait_ge(ends_in, 64)
            v.tensor_copy(row_s, row_i[0:1, :]).then_inc(boot_dve, 1)
            dve.wait_ge(edges_in, 32)
            u = attr[0:P, :]
            hat = hats[0:P, :].rearrange("p (k t a) -> p a k t", a=2, k=3)
            of = lambda k: hats[0:P, k * 2 * TE:(k + 1) * 2 * TE]
            step(v.tensor_scalar(u, u, 1.0, 0.0, ALU.min, ALU.max))
            v.tensor_scalar(of(0), u, -2.0, 1.0, ALU.mult, ALU.add)
            v.tensor_scalar(of(1), u, 0.5, None, ALU.subtract)
            step(v.tensor_scalar(of(2), u, 1.0, 2.0, ALU.subtract, ALU.mult))
            v.tensor_scalar(of(0), of(0), 0.0, None, ALU.max)
            v.tensor_scalar(of(2), of(2), 1.0, 0.0, ALU.add, ALU.max)
            step(v.scalar_tensor_tensor(out=of(1), in0=of(1), scalar=-1.0, in1=of(1), op0=ALU.mult, op1=ALU.max))
            step(v.tensor_scalar(of(1), of(1), -2.0, 1.0, ALU.mult, ALU.add))
            for k in range(KS):
                i = v.tensor_tensor(basis[0:P, :].rearrange("p (g k t) -> p g k t", k=KS, t=4)[:, :, k, :],
                                    hat[:, 0, k // 3, :].rearrange("p (g t) -> p g t", t=4),
                                    hat[:, 1, k % 3, :].rearrange("p (g t) -> p g t", t=4), ALU.mult)
            step(i)
            step(v.tensor_copy(dst_f[0:P, :], dst_i[0:P, :]))
            blocks = lambda a: a[0:P, :].rearrange("p (b s) -> p b s", b=NB)
            d = blocks(dst_f)
            same = (d[:, :, 1:SE], d[:, :, 0:SE - 1])
            v.tensor_tensor(blocks(cont)[:, :, 1:SE], *same, ALU.is_equal)
            v.tensor_tensor(blocks(cont_next)[:, :, 0:SE - 1], *same, ALU.is_equal)
            v.tensor_tensor(blocks(head), d, d[:, :, 0:1].to_broadcast([P, NB, SE]), ALU.is_equal)
            v.tensor_tensor(blocks(tail), d, d[:, :, SE - 1:SE].to_broadcast([P, NB, SE]), ALU.is_equal)
            nxt, on, spare = hrow[0:P, 0, 0:NB], hrow[0:P, 1, 0:TE], hrow[0:P, 2, 0:TE]
            v.tensor_copy(nxt, next_i[0:P, :])
            step(v.tensor_copy(spare, scatter_to[0:P, :]))
            step(v.tensor_copy(on, cont_next[0:P, :]))
            step(v.tensor_tensor(on.rearrange("p (b s) -> p b s", b=NB)[:, :, SE - 1], d[:, :, SE - 1], nxt, ALU.is_equal))
            step(v.tensor_tensor(spare, spare, dst_f[0:P, :], ALU.subtract))
            step(v.tensor_tensor(spare, spare, on, ALU.mult))
            step(v.tensor_tensor(spare, spare, dst_f[0:P, :], ALU.add))
            v.tensor_copy(scatter_to[0:P, :], spare)
            dve.wait_ge(boot_pe, 5)
            for m in range(2):
                v.tensor_copy(row_f[:, m * NB * P:m * NB * P + 4 * P], V[2 * m][0:33, 0:4 * P])
                i = v.tensor_copy(row_f[:, m * NB * P + 4 * P:(m + 1) * NB * P], V[1][0:33, m * 128:m * 128 + P])
            step(i)
            v.tensor_tensor(row_cont[:, 1:R], row_f[:, 1:R], row_f[:, R:2 * R - 1], ALU.is_equal)
            step(v.tensor_tensor(whole, row_f[:, 0:R], row_f[:, R:2 * R], ALU.is_equal))
            v.tensor_tensor(row_pass[:, 1:R], row_cont[:, 1:R], whole[:, 0:R - 1], ALU.mult)
            v.tensor_tensor(row_pass_back[:, 0:R - 1], row_cont[:, 1:R], whole[:, 1:R], ALU.mult)
            dve.wait_ge(boot_dma, 16 * N_BOOT)
            dve.wait_ge(boot_pe, 6)
            step(v.tensor_copy(root_bd[:, :], V[3][:, 256:256 + GF]))
            dve.sem_inc(boot_dve, 2)

            def spread(k):
                at, _ = nq.next()
                dve.wait_ge(sq_ready, at + 1)
                v.tensor_reduce(unit(var, k), slots(unit(sq, k)), AX.X, ALU.add).then_inc(var_ready, 1)
                return at

            def scale_of(k, at):
                dve.wait_ge(std_ready, at + 1)
                step(v.reciprocal(unit(rstd, k), unit(std, k)))

            def bank_ready():
                at, bank = cq.next()
                dve.wait_ge(c_ready, at + 1)
                return at, C[bank][0:P, :]

            def relu_rows(k, at):
                _, rows = bank_ready()
                scale_of(k, at)
                v.scalar_tensor_tensor(out=slots(unit(hrow, k)), in0=slots(rows), scalar=0.0, in1=wide(unit(rstd, k)),
                                       op0=ALU.max, op1=ALU.mult).then_inc(c_done, 1)

            def rows_over_std(k, at):
                at_c, rows = bank_ready()
                scale_of(k, at)
                v.tensor_tensor(slots(unit(hrow, k)), slots(rows), wide(unit(rstd, k)), ALU.mult).then_inc(c_done, 1)
                return at_c

            def scan_block(rows, b):
                here = bass.ds(b * SE, SE)
                feature = rows[0:P, :].rearrange("p (t f) -> p t f", f=F)
                dve.wait_ge(msgs_done, rq.at + 1 + CREDIT)
                for f in range(F):
                    i = v.tensor_tensor_scan(feature[:, here, f], cont[0:P, here], feature[:, here, f], 0.0, ALU.mult, ALU.add)
                step(i)
                return feature

            def make_weights():
                tmp = hrow[:, 3, 0:H * F]
                heads = lambda a: a.rearrange("p (h f) -> p h f", f=F)
                for k in range(2):
                    step(v.tensor_tensor(tmp, gat[:, :], att[:, k, :], ALU.mult))
                    step(v.tensor_reduce(att_vec[:, k * H:(k + 1) * H], heads(tmp), AX.X, ALU.add))
                for t in range(4):
                    q = slice(t * F, (t + 1) * F)
                    v.tensor_copy(att_bd[q, t, :], att_vec[q, :])
                    v.tensor_copy(src_bd[q, t, :], att_vec[q, 0:H])
                mean = hrow[:, 3, H * F:H * F + H]
                step(v.tensor_reduce(mean, heads(gat[:, :]), AX.X, ALU.add))
                step(v.tensor_scalar(mean, mean, 1.0 / F, None, ALU.mult))
                step(v.tensor_tensor(heads(tmp), heads(gat[:, :]), mean.unsqueeze(2).to_broadcast([128, H, F]), ALU.subtract))
                for t in range(4):
                    q = slice(t * F, (t + 1) * F)
                    i = v.tensor_scalar(gat_bd[q, :].rearrange("p (h t o) -> p h t o", h=H, t=4)[:, :, t, :], heads(hrow[q, 3, 0:H * F]),
                                        1.0 / H, None, ALU.mult)
                step(i)
                step(v.tensor_reduce(base_bd[:, :], gat_bd[:, :].rearrange("p (h c) -> p c h", h=H), AX.X, ALU.add))
                v.tensor_tensor(base_bd[:, :], base_bd[:, :], center[:, :], ALU.add)
                m1 = hrow[:, 3, 300:301]
                step(v.tensor_reduce(m1, w2_c[:, :], AX.X, ALU.add))
                step(v.tensor_scalar(m1, m1, 1.0 / F, None, ALU.mult))
                v.tensor_tensor(w2_c[:, :], w2_c[:, :], m1.to_broadcast([128, F]), ALU.subtract)
                for k in range(2):
                    m2 = hrow[0:1, 3, 301 + k:302 + k]
                    step(v.tensor_reduce(m2, bias_row[0:1, k, 0:F], AX.X, ALU.add))
                    step(v.tensor_scalar(m2, m2, 1.0 / F, None, ALU.mult))
                    step(v.tensor_tensor(bias_row[0:1, k, 0:F], bias_row[0:1, k, 0:F], m2.to_broadcast([1, F]), ALU.subtract))
                for k in range(2):
                    i = v.tensor_copy(bias_row[0:1, k, F:W].rearrange("p (s f) -> p s f", f=F),
                                      bias_row[0:1, k, 0:F].unsqueeze(1).to_broadcast([1, CE - 1, F]))

            def a_wave(x, cv):
                pending = []
                def products_of(g):
                    rq.next()
                    dve.wait_ge(msgs_done, rq.room)
                    for q in range(3):
                        at, bank = vq.next()
                        dve.wait_ge(v_ready, at + 1)
                        to = (g % 2) * KS * GF + q * 3 * GF
                        v.tensor_tensor(products[0:P, to:to + 3 * GF].rearrange("p (k o) -> p k o", o=F),
                                        V[bank][0:P, 0:3 * GF].rearrange("p (k o) -> p k o", o=F),
                                        basis[0:P, bass.ds((cv * G + g) * 4 * KS + q * 12, 12)].unsqueeze(2).to_broadcast([P, 12, F]),
                                        ALU.mult).then_inc(v_done, 1)
                    pending.append((g, at))
                def sum_of():
                    g, at = pending.pop(0)
                    dve.wait_ge(v_done, at + 1 + CREDIT)
                    v.tensor_reduce(msgs[0:P, bass.ds(cv * W + g * GF, GF)],
                                    products[0:P, (g % 2) * KS * GF:(g % 2 + 1) * KS * GF].rearrange("p (k c) -> p c k", k=KS),
                                    AX.X, ALU.add).then_inc(msgs_done, 1)
                back = cv is not None
                if back: products_of(0)
                if x: at = spread(0)
                if back: products_of(1); sum_of()
                if x: relu_rows(0, at); at = spread(1)
                if back: products_of(2); sum_of()
                if x: relu_rows(1, at)
                if back: products_of(3)
                if x: at = spread(2)
                if back: sum_of()
                if x: relu_rows(2, at)
                if back: sum_of()

            def a_block(b, first, last=False):
                for w in range(2 if last else NJ):
                    a_wave(not last, None if first and w < 2 else b * NJ + w - 2)
                    if first and w == 0:
                        make_weights()
                    if w == 1 and not first:
                        scan_block(msgs, b - 1)
            a_block(0, True)
            cq.restart(); vq.restart(); rq.restart()
            with dve.Fori(0, NB - 1) as b:
                cq.loop(b, 3 * NJ); vq.loop(b, 12 * NJ); nq.loop(b, 3 * NJ); rq.loop(b, 4 * NJ); steps.loop(b, 3 * NJ + 1)
                a_block(b + 1, False)
                cq.end(NB - 1, 3 * NJ); vq.end(NB - 1, 12 * NJ); nq.end(NB - 1, 3 * NJ); rq.end(NB - 1, 4 * NJ)
                steps.end(NB - 1, 3 * NJ + 1)
            a_block(NB, False, True)
            by_block = lambda a: a[0:P, :].rearrange("p (b s) -> p b s", b=NB)
            block_carry = carry[0:P, :].rearrange("p (b f) -> p b f", f=F + 1)
            v.tensor_copy(tails[0:P, :].rearrange("p (b f) -> p b f", f=F + 1)[:, :, 0:F],
                          msgs[0:P, :].rearrange("p (b s f) -> p b s f", b=NB, f=F)[:, :, SE - 1, :])
            step(v.tensor_tensor_scan(degree[0:P, :], cont[0:P, :], ones[0:P, 0:1].to_broadcast([P, TE]), 0.0, ALU.mult, ALU.add))
            v.memset(a_tails[:, 0:1], 0.0)
            v.tensor_copy(tails[0:P, :].rearrange("p (b f) -> p b f", f=F + 1)[:, :, F], by_block(degree)[:, :, SE - 1]).then_inc(tails_ready, 1)
            tq.base += 8 * NC
            for _ in range(NB):
                at, _ = tq.next()
            dve.wait_ge(t_done, at + 1 + CREDIT)
            step(v.tensor_tensor(a_in, a_tails[:, 0:R], row_cont[0:F + 1, :], ALU.mult))
            v.tensor_tensor_scan(a_carry, row_pass[0:F + 1, :], a_in, 0.0, ALU.mult, ALU.add).then_inc(carry_ready, 1)
            for _ in range(NB):
                at, _ = tq.next()
            dve.wait_ge(t_done, at + 1 + CREDIT)
            masked_degree = hrow[0:P, 0, 0:TE]
            step(v.tensor_tensor(masked_degree.rearrange("p (b s) -> p b s", b=NB), by_block(head),
                                 block_carry[:, :, F:F + 1].to_broadcast([P, NB, SE]), ALU.mult))
            step(v.tensor_tensor(degree[0:P, :], degree[0:P, :], masked_degree, ALU.add))
            step(v.tensor_scalar(degree[0:P, :], degree[0:P, :], 1.0, None, ALU.max))
            step(v.reciprocal(degree[0:P, :], degree[0:P, :]))

            def finish_rows(x1_part, to, at, signal, with_be2=False):
                at_c = rows_over_std(3, at)
                if not with_be2:
                    v.tensor_tensor(slots(x1_part), slots(x1_part), be2_b[0:P, :].unsqueeze(1).to_broadcast([P, CE, F]), ALU.add)
                dve.wait_ge(c_done, at_c + 1 + CREDIT)
                step(v.tensor_tensor(slots(unit(hrow, 3)), slots(unit(hrow, 3)), g2_b[0:P, :].unsqueeze(1).to_broadcast([P, CE, F]), ALU.mult))
                v.tensor_tensor(to, x1_part, unit(hrow, 3), ALU.add).then_inc(signal, 1)

            heads_of = lambda a: a[0:P, :].rearrange("p (h t) -> p h t", h=H)
            def logits_dst(c):
                now = bass.ds(c * CE, CE)
                v.tensor_copy(diff[0:P, bass.ds(c * W, W)], unit(hrow, 0))
                _, rows = bank_ready()
                logits = rows[:, 0:2 * H * CE].rearrange("p (s h) -> p h s", h=2 * H)
                step(v.tensor_copy(heads_of(beta)[:, :, now], logits[:, H:2 * H, :]))
                own = heads_of(self_logit)[:, :, now]
                v.tensor_tensor(own, logits[:, 0:H, :], heads_of(beta)[:, :, now], ALU.add).then_inc(c_done, 1)
                dve.wait_ge(c_done, cq.at + 1 + CREDIT)
                step(v.scalar_tensor_tensor(out=own, in0=own, scalar=SLOPE, in1=own, op0=ALU.mult, op1=ALU.max))
            def logits_src(c):
                now = bass.ds(c * CE, CE)
                v.tensor_tensor(diff[0:P, bass.ds(c * W, W)], unit(hrow, 0), diff[0:P, bass.ds(c * W, W)], ALU.subtract)
                _, rows = bank_ready()
                bt = heads_of(beta)[:, :, now]
                v.tensor_tensor(bt, rows[:, 0:H * CE].rearrange("p (s h) -> p h s", h=H), bt, ALU.add).then_inc(c_done, 1)
                dve.wait_ge(c_done, cq.at + 1 + CREDIT)
                step(v.scalar_tensor_tensor(out=bt, in0=bt, scalar=SLOPE, in1=bt, op0=ALU.mult, op1=ALU.max))
                step(v.tensor_tensor(bt, bt, heads_of(self_logit)[:, :, now], ALU.subtract))
            st = {}
            def wave_rows(name, b, w, wave):
                if name == "C":
                    c = b * NJ + w
                    dve.wait_ge(ring_dma[w], NB * DMAS + b * DMAS)
                    to = ring[0:P, w, :]
                    step(v.tensor_tensor(slots(to), carry[0:P, bass.ds(b * (F + 1), F)].unsqueeze(1).to_broadcast([P, CE, F]),
                                         wide(head[0:P, bass.ds(c * CE, CE)]), ALU.mult))
                    step(v.tensor_tensor(to, to, msgs[0:P, bass.ds(c * W, W)], ALU.add))
                    v.tensor_tensor(slots(to), slots(to), wide(degree[0:P, bass.ds(c * CE, CE)]), ALU.mult)
                    v.tensor_copy(index_out[0:P, w, :], scatter_to[0:P, bass.ds(c * CE, CE)]).then_inc(ring_filled, 1)
                at = {}
                if "n2" in wave: at["n2"] = spread(2)
                if "n1" in wave: at["n1"] = spread(1)
                if "n2" in wave: rows_over_std(2, at["n2"])
                if "n1" in wave: relu_rows(1, at["n1"])
                if "n3" in wave:
                    i = wave["n3"][1]
                    finish_rows(nodes[0:P, i, 0:W], nodes[0:P, i, 0:W], spread(3), nodes_ready)
                if "e2" in wave:
                    phase, j, back = wave["e2"]
                    dve.wait_ge(c_done, st["h"] + 1 + CREDIT)
                    c = (NC if phase != name else b * NJ) + j - (NJ if back else 0)
                    (logits_dst if phase == "B" else logits_src)(c)
                    if phase == "D" and j == NJ - 1:
                        here = bass.ds(b * SE - SE, SE) if name else slice(TE - SE, TE)
                        for h in range(H):
                            i = v.tensor_tensor_scan(heads_of(self_logit)[:, h, here], cont[0:P, here], heads_of(beta)[:, h, here], 0.0, ALU.mult, ALU.max)
                        step(i)
                if "e1" in wave:
                    relu_rows(0, spread(0))
                    st["h"] = cq.at
                    if name == "B":
                        kept = ring[0:P, wave["e1"][1], :]
                        v.tensor_tensor(slots(kept), slots(kept), be2_b[0:P, :].unsqueeze(1).to_broadcast([P, CE, F]), ALU.add).then_inc(rows_kept, 1)
            before = None
            for name in "CBD":
                per = PER[name]
                tq.restart(); cq.restart()
                for w, wave in enumerate(waves(name, before)):
                    wave_rows(name, 0, w, wave)
                lag = cq.base + cq.n - st.get("h", 0)
                with dve.Fori(0, NB - 1) as b:
                    cq.loop(b, per["c"]); nq.loop(b, per["n"]); steps.loop(b, per["steps"])
                    st["h"] = cq.base - lag
                    for w, wave in enumerate(waves(name, name)):
                        wave_rows(name, b + 1, w, wave)
                    cq.end(NB - 1, per["c"]); nq.end(NB - 1, per["n"]); steps.end(NB - 1, per["steps"])
                st["h"] = cq.base - lag
                before = name
            for w, wave in enumerate(waves(None, "D")):
                wave_rows(None, None, w, wave)
            tq.base += NB * sum(per["t"] for per in PER.values())

            tq.restart()
            def to_segments(a):
                for h in range(H):
                    own = heads_of(a)[:, h, ::-1]
                    i = v.tensor_tensor_scan(own, cont_next[0:P, ::-1], own, 0.0, ALU.mult, ALU.max)
                step(i)

            def join(a, op):
                ends = tails[0:P, 0:2 * NB * H].rearrange("p (d b h) -> p d h b", d=2, h=H)
                by = lambda x: x[0:P, :].rearrange("p (h b s) -> p h b s", h=H, b=NB)
                v.tensor_copy(ends[:, 0], by(a)[:, :, :, SE - 1])
                v.tensor_copy(ends[:, 1], by(a)[:, :, :, 0]).then_inc(tails_ready, 1)
                for _ in range(0, 2 * NB, 4):
                    at, _ = tq.next()
                dve.wait_ge(t_done, at + 1 + CREDIT)
                v.tensor_tensor(s_in[0], s_ends[:, 0:R], row_cont[0:H, :], ALU.mult)
                v.memset(s_in[1][:, R - 1:R], 0.0)
                step(v.tensor_tensor(s_in[1][:, 0:R - 1], s_ends[:, R + 2:2 * R + 1], row_cont[0:H, 1:R], ALU.mult))
                v.tensor_tensor_scan(s_carry[0], row_pass[0:H, :], s_in[0], 0.0, ALU.mult, op)
                v.tensor_tensor_scan(s_carry[1][:, ::-1], row_pass_back[0:H, ::-1], s_in[1][:, ::-1], 0.0, ALU.mult, op).then_inc(carry_ready, 1)
                at, _ = tq.next()
                dve.wait_ge(t_done, at + 1 + CREDIT)
                for d, mask in enumerate((head, tail)):
                    step(v.tensor_tensor(by(masked), mask[0:P, :].rearrange("p (b s) -> p b s", b=NB).unsqueeze(1).to_broadcast([P, H, NB, SE]),
                                         carry[0:P, 0:2 * NB * H].rearrange("p (d b h) -> p d h b", d=2, h=H)[:, d].unsqueeze(3).to_broadcast([P, H, NB, SE]),
                                         ALU.mult))
                    step(v.tensor_tensor(a[0:P, :], a[0:P, :], masked[0:P, :], op))

            for j in range(4):
                dve.wait_ge(nodes_out[j], OUT_DONE[j])
                dve.wait_ge(ring_saved[j], NB * 32)
            v.memset(s_ends[:, 0:1], 0.0)
            to_segments(self_logit)
            join(self_logit, ALU.max)
            for k in range(2):
                half = slice(k * H * TE // 2, (k + 1) * H * TE // 2)
                v.tensor_tensor(beta[0:P, half], beta[0:P, half], self_logit[0:P, half], ALU.subtract).then_inc(exp_in, 1)
            for h in range(H):
                dve.wait_ge(exp_ready, 1 + h // (H // 2))
                i = v.tensor_tensor_scan(heads_of(denom)[:, h, :], cont[0:P, :], heads_of(beta)[:, h, :], 0.0, ALU.mult, ALU.add)
            step(i)
            to_segments(denom)
            join(denom, ALU.add)
            dve.wait_ge(exp_ready, 3)
            step(v.scalar_tensor_tensor(out=denom[0:P, :], in0=self_logit[0:P, :], scalar=1e-16, in1=denom[0:P, :], op0=ALU.add, op1=ALU.add))
            step(v.reciprocal(denom[0:P, :], denom[0:P, :]))
            step(v.tensor_tensor(beta[0:P, :], beta[0:P, :], denom[0:P, :], ALU.mult))
            for a in (tails_row, carry_last):
                i = v.memset(a[:, :], 0.0)
            step(i)
            dve.sem_inc(softmax_done, 1)

            tq.restart(); cq.restart(); vq.restart(); tq.depth, cq.depth = 1, 1; rq.restart()
            def x_products(c, g, pending):
                rq.next()
                dve.wait_ge(msgs_done, rq.room)
                for q in range(2):
                    at, bank = vq.next()
                    dve.wait_ge(v_ready, at + 1)
                    to = (g % 2) * H * GF + q * 512
                    v.tensor_tensor(weighted[0:P, to:to + 512].rearrange("p (h t o) -> p h t o", h=4, t=4),
                                    VE[bank][0:P, :].rearrange("p (h t o) -> p h t o", h=4, t=4),
                                    heads_of(beta)[:, 4 * q:4 * q + 4, bass.ds(c * CE + 4 * g, 4)].unsqueeze(3).to_broadcast([P, 4, 4, F]),
                                    ALU.mult).then_inc(v_done, 1)
                pending.append((g, at))
            def x_sum(c, pending):
                g, at = pending.pop(0)
                dve.wait_ge(v_done, at + 1 + CREDIT)
                v.tensor_reduce(diff[0:P, bass.ds(c * W + g * GF, GF)],
                                weighted[0:P, (g % 2) * H * GF:(g % 2 + 1) * H * GF].rearrange("p (h c) -> p c h", h=H),
                                AX.X, ALU.add).then_inc(msgs_done, 1)
            def e_block(x_block, y_block):
                x, y = x_block is not None, y_block is not None
                pending, spreads = [], {}
                def y_sum(j):
                    c = y_block * NJ + j
                    if j > 0:
                        dve.wait_ge(row_ready, y_block * NJ + j)
                    step(v.tensor_tensor(slots(unit(hrow, 1)), carry[0:P, 0:F].unsqueeze(1).to_broadcast([P, CE, F]),
                                         wide(head[0:P, bass.ds(c * CE, CE)]), ALU.mult))
                    step(v.tensor_tensor(unit(hrow, 1), unit(hrow, 1), diff[0:P, bass.ds(c * W, W)], ALU.add))
                    dve.wait_ge(nodes_in[j], LOADED[j] + (y_block + 1) * 32)
                    v.tensor_tensor(unit(hrow, 1), unit(hrow, 1), nodes[0:P, j, W:2 * W], ALU.add).then_inc(sum_ready, 1)
                def y_norm(j):
                    scale_of(2, spreads["sum"])
                    v.tensor_tensor(slots(unit(hrow, NORMED[j % 2])), slots(unit(hrow, 1)), wide(unit(rstd, 2)), ALU.mult).then_inc(row_ready, 1)
                def y_finish(j):
                    dve.wait_ge(ring_dma[j], (4 * NB + y_block) * DMAS)
                    c = y_block * NJ + j
                    v.tensor_copy(index_out[0:P, j, :], scatter_to[0:P, bass.ds(c * CE, CE)])
                    finish_rows(nodes[0:P, j, 0:W], ring[0:P, j, :], spreads["ff"], ring_filled, True)
                    dve.wait_ge(ring_filled, NC + c + 1)
                    dve.sem_inc(rows_used, 1)
                for j in range(NJ):
                    cx = x_block * NJ + j if x else None
                    if y: y_sum(j)
                    if x: x_products(cx, 0, pending)
                    if y and j > 1: spreads["ff"] = spread(3)
                    if y: spreads["sum"] = spread(2)
                    if x: x_products(cx, 1, pending); x_sum(cx, pending)
                    if y: y_norm(j)
                    if x: x_products(cx, 2, pending); x_sum(cx, pending)
                    if y and j > 1: y_finish(j - 2)
                    if x: x_products(cx, 3, pending); x_sum(cx, pending); x_sum(cx, pending)
                if y:
                    spreads["ff"] = spread(3)
                if x:
                    feature = scan_block(diff, x_block)
                    v.tensor_copy(tails[0:P, 0:F].rearrange("p (a f) -> p a f", a=1),
                                  feature[:, bass.ds(x_block * SE + SE - 1, 1), :]).then_inc(tails_ready, 1)
                if y:
                    y_finish(NJ - 2)
                if x:
                    for _ in range(NJ + (NJ if y else 0) + 1):
                        at, _ = tq.next()
                    dve.wait_ge(t_done, at + 1 + CREDIT)
                    step(v.tensor_tensor(carry_in[0:F, :], tails_row[0:F, 0:P], row_cont[0:F, bass.ds(x_block * P, P)], ALU.mult))
                    v.tensor_tensor_scan(carry_row[0:F, :], row_pass[0:F, bass.ds(x_block * P, P)], carry_in[0:F, :], carry_last[0:F, 0:1],
                                         ALU.mult, ALU.add).then_inc(carry_ready, 1)
                    at, _ = tq.next()
                if y:
                    spreads["ff"] = spread(3)
                    y_finish(NJ - 1)
                if x:
                    dve.wait_ge(t_done, at + 1 + CREDIT)
                    v.tensor_copy(tails_row[0:F, 0:1], tails_row[0:F, P:P + 1])
                    step(v.tensor_copy(carry_last[0:F, :], carry_row[0:F, P - 1:P]))
            e_block(0, None)
            tq.restart(); cq.restart(); vq.restart(); rq.restart()
            with dve.Fori(0, NB - 1) as b:
                tq.loop(b, 2 * NJ + 2); cq.loop(b, NJ); vq.loop(b, 8 * NJ); nq.loop(b, 2 * NJ); rq.loop(b, 4 * NJ)
                steps.loop(b, 3 + 5 * NJ)
                e_block(b + 1, b)
                tq.end(NB - 1, 2 * NJ + 2); cq.end(NB - 1, NJ); vq.end(NB - 1, 8 * NJ); nq.end(NB - 1, 2 * NJ); rq.end(NB - 1, 4 * NJ)
                steps.end(NB - 1, 3 + 5 * NJ)
            e_block(None, NB - 1)


_INS = ["x", "src", "dst", "edge_attr_2", "L0_gnn_weight", "L0_gnn_root_w", "L0_gnn_root_b", "L1_gnn_W_gat",
        "L1_gnn_att_src", "L1_gnn_att_dst", "L1_gnn_bias_gat", "L1_gnn_w1", "L1_gnn_b1", "L1_gnn_w2", "L1_gnn_b2",
        "L1_gnn_g1", "L1_gnn_be1", "L1_gnn_g2", "L1_gnn_be2"]


def kernel(**inputs):
    import numpy as np
    import concourse.bacc as bacc
    from concourse.bass_utils import run_bass_kernel_spmd

    nc = bacc.Bacc("TRN2", target_bir_lowering=False, num_devices=1)
    arrays, args = {}, []
    for name in _INS:
        a = np.ascontiguousarray(inputs[name])
        arrays[f"in_{name}"] = a
        args.append(nc.dram_tensor(f"in_{name}", a.shape, mybir.dt.from_np(a.dtype), kind="ExternalInput").ap())
    out = nc.dram_tensor("out_rows", (N, F), F32, kind="ExternalOutput").ap()
    gnn_program(nc, *args, out)
    r = run_bass_kernel_spmd(nc, [arrays], core_ids=[0])
    return r.results[0]["out_rows"]
```
